# Optimizing a Trainium2 kernel written in Bass

```python
import numpy as np
import jax
import jax.numpy as jnp

def _softmax(x, axis=-1):
    return jax.nn.softmax(x, axis=axis)

def _gelu(x):
    return jax.nn.gelu(x, approximate=True)

def _silu(x):
    return jax.nn.silu(x)

def _sigmoid(x):
    return jax.nn.sigmoid(x)

def _layernorm(x, axis=-1, eps=1e-05):
    m = jnp.mean(x, axis=axis, keepdims=True)
    v = jnp.var(x, axis=axis, keepdims=True)
    return (x - m) / jnp.sqrt(v + eps)

def _scatter_add(tgt, idx, src, axis=0):
    return tgt.at[idx].add(src)

def _segment_sum(src, seg, n):
    return jax.ops.segment_sum(src, seg, n)
kernel_name = 'mk_prb_d2_jaxref_r4_9a1ab1'

def setup_inputs(seed: int=0):
    np.random.seed(seed)
    _w = jnp.asarray

    def _L0_attn_setup():
        import jax, jax.numpy as jnp
        import numpy as np
        D_MODEL = 256
        key = jax.random.key(seed)
        k1, k2, k3, k4 = jax.random.split(key, 4)
        B, T, D, E = (8, 512, 256, 256)
        x = jax.random.normal(k1, (B, T, D), dtype=jnp.float32)
        Wq = jax.random.normal(k2, (D, E), dtype=jnp.float32) * (1.0 / np.sqrt(D))
        Wk = jax.random.normal(k3, (D, E), dtype=jnp.float32) * (1.0 / np.sqrt(D))
        Wv = jax.random.normal(k4, (D, E), dtype=jnp.float32) * (1.0 / np.sqrt(D))
        return {'x': x, 'Wq': Wq, 'Wk': Wk, 'Wv': Wv}
    _L0_attn_in = _L0_attn_setup()

    def _L0_ffn_setup():
        import jax, jax.numpy as jnp
        import numpy as np
        B, S, D, H, E = (4, 512, 256, 1024, 8)
        TOP_K = 2
        key = jax.random.key(seed)
        k = jax.random.split(key, 7)
        scale_in = 1.0 / np.sqrt(D)
        scale_h = 1.0 / np.sqrt(H)
        return {'x': jax.random.normal(k[0], (B, S, D), jnp.float32), 'Wr': jax.random.normal(k[1], (D, E), jnp.float32) * scale_in, 'br': jnp.zeros((E,), jnp.float32), 'W1': jax.random.normal(k[2], (E, D, H), jnp.float32) * scale_in, 'b1': jnp.zeros((E, H), jnp.float32), 'W2': jax.random.normal(k[3], (E, H, D), jnp.float32) * scale_h, 'b2': jnp.zeros((E, D), jnp.float32)}
    _L0_ffn_in = _L0_ffn_setup()

    def _L1_attn_setup():
        import jax, jax.numpy as jnp
        import numpy as np
        DIM = 256
        HEADS = 16
        HEAD_DIM = DIM // HEADS
        ROPE_BASE = 500000.0
        SCALE = HEAD_DIM ** (-0.5)

        def _rope_cos_sin(T, dtype=jnp.float32):
            inv_freq = 1.0 / ROPE_BASE ** (jnp.arange(0, HEAD_DIM, 2, dtype=jnp.float32) / HEAD_DIM)
            t = jnp.arange(T, dtype=jnp.float32)
            freqs = t[:, None] * inv_freq[None, :]
            emb = jnp.concatenate([freqs, freqs], axis=-1)
            return (jnp.cos(emb).astype(dtype), jnp.sin(emb).astype(dtype))

        def _rotate_half(x):
            x1, x2 = jnp.split(x, 2, axis=-1)
            return jnp.concatenate([-x2, x1], axis=-1)

        def _apply_rope(x, cos, sin):
            return x * cos + _rotate_half(x) * sin
        key = jax.random.key(seed)
        k1, k2, k3 = jax.random.split(key, 3)
        B, T = (4, 1024)
        x = jax.random.normal(k1, (B, T, DIM), dtype=jnp.float32)
        W_qkv = jax.random.normal(k2, (DIM, 3 * DIM), dtype=jnp.float32) * DIM ** (-0.5)
        W_out = jax.random.normal(k3, (DIM, DIM), dtype=jnp.float32) * DIM ** (-0.5)
        return {'x': x, 'W_qkv': W_qkv, 'W_out': W_out}
    _L1_attn_in = _L1_attn_setup()

    def _L1_ffn_setup():
        import jax, jax.numpy as jnp
        import numpy as np
        DIM = 256

        def _reference_tuple_inner(x, W_r, W_k, W_v, mu_r, mu_k):
            B, T, C = x.shape
            x_prev = jnp.concatenate([jnp.zeros((B, 1, C), x.dtype), x[:, :-1, :]], axis=1)
            xr = mu_r * x + (1.0 - mu_r) * x_prev
            xk = mu_k * x + (1.0 - mu_k) * x_prev
            r = jax.nn.sigmoid(jnp.einsum('btc,dc->btd', xr, W_r))
            k = jnp.einsum('btc,dc->btd', xk, W_k)
            k_act = jnp.square(jax.nn.relu(k))
            out = r * jnp.einsum('btc,dc->btd', k_act, W_v)
            new_state = x[:, -1, :]
            return (out, new_state)
        key = jax.random.key(seed)
        ks = jax.random.split(key, 6)
        B, T, C = (8, 512, DIM)
        x = jax.random.normal(ks[0], (B, T, C), dtype=jnp.float32)
        s = 1.0 / np.sqrt(C)
        W_r = jax.random.uniform(ks[1], (C, C), jnp.float32, -s, s)
        W_k = jax.random.uniform(ks[2], (C, C), jnp.float32, -s, s)
        W_v = jax.random.uniform(ks[3], (C, C), jnp.float32, -s, s)
        mu_r = jax.random.uniform(ks[4], (C,), jnp.float32)
        mu_k = jax.random.uniform(ks[5], (C,), jnp.float32)
        return {'x': x, 'W_r': W_r, 'W_k': W_k, 'W_v': W_v, 'mu_r': mu_r, 'mu_k': mu_k}
    _L1_ffn_in = _L1_ffn_setup()
    _d = {'L0_attn_x': _L0_attn_in['x'], 'L0_attn_Wq': _L0_attn_in['Wq'], 'L0_attn_Wk': _L0_attn_in['Wk'], 'L0_attn_Wv': _L0_attn_in['Wv'], 'L0_ffn_Wr': _L0_ffn_in['Wr'], 'L0_ffn_br': _L0_ffn_in['br'], 'L0_ffn_W1': _L0_ffn_in['W1'], 'L0_ffn_b1': _L0_ffn_in['b1'], 'L0_ffn_W2': _L0_ffn_in['W2'], 'L0_ffn_b2': _L0_ffn_in['b2'], 'L1_attn_W_qkv': _L1_attn_in['W_qkv'], 'L1_attn_W_out': _L1_attn_in['W_out'], 'L1_ffn_W_r': _L1_ffn_in['W_r'], 'L1_ffn_W_k': _L1_ffn_in['W_k'], 'L1_ffn_W_v': _L1_ffn_in['W_v'], 'L1_ffn_mu_r': _L1_ffn_in['mu_r'], 'L1_ffn_mu_k': _L1_ffn_in['mu_k']}
    _x0 = _d['L0_attn_x']
    _d['L0_attn_x'] = jax.random.normal(jax.random.fold_in(jax.random.key(seed), 1), (4, 1024, 256), dtype=_x0.dtype)
    del _x0
    return _d

def reference(L0_attn_x, L0_attn_Wq, L0_attn_Wk, L0_attn_Wv, L0_ffn_Wr, L0_ffn_br, L0_ffn_W1, L0_ffn_b1, L0_ffn_W2, L0_ffn_b2, L1_attn_W_qkv, L1_attn_W_out, L1_ffn_W_r, L1_ffn_W_k, L1_ffn_W_v, L1_ffn_mu_r, L1_ffn_mu_k):

    def _L0_attn_ref(x, Wq, Wk, Wv):
        import jax, jax.numpy as jnp
        import numpy as np
        D_MODEL = 256
        T = x.shape[1]
        Q = x @ Wq
        K = x @ Wk
        V = x @ Wv
        scale = 1.0 / jnp.sqrt(jnp.asarray(D_MODEL, dtype=x.dtype))
        w = jnp.einsum('bte,bse->bts', Q, K) * scale
        causal = jnp.tril(jnp.ones((T, T), dtype=bool))
        w = jnp.where(causal, w, -jnp.inf)
        w = jax.nn.softmax(w, axis=-1)
        return w @ V

    def _L0_ffn_ref(x, Wr, br, W1, b1, W2, b2):
        import jax, jax.numpy as jnp
        import numpy as np
        B, S, D, H, E = (4, 512, 256, 1024, 8)
        TOP_K = 2
        routing = jax.nn.softmax(x @ Wr + br, axis=-1)
        topk_vals, topk_idx = jax.lax.top_k(routing, TOP_K)
        topk_norm = topk_vals / jnp.sum(topk_vals, axis=-1, keepdims=True)
        gate = jnp.sum(jax.nn.one_hot(topk_idx, E, dtype=x.dtype) * topk_norm[..., None], axis=2)
        h = jax.nn.relu(jnp.einsum('bsd,edh->ebsh', x, W1) + b1[:, None, None, :])
        y = jnp.einsum('ebsh,ehd->ebsd', h, W2) + b2[:, None, None, :]
        out = jnp.einsum('ebsd,bse->bsd', y, gate)
        return out

    def _L1_attn_ref(x, W_qkv, W_out):
        import jax, jax.numpy as jnp
        import numpy as np
        DIM = 256
        HEADS = 16
        HEAD_DIM = DIM // HEADS
        ROPE_BASE = 500000.0
        SCALE = HEAD_DIM ** (-0.5)

        def _rope_cos_sin(T, dtype=jnp.float32):
            inv_freq = 1.0 / ROPE_BASE ** (jnp.arange(0, HEAD_DIM, 2, dtype=jnp.float32) / HEAD_DIM)
            t = jnp.arange(T, dtype=jnp.float32)
            freqs = t[:, None] * inv_freq[None, :]
            emb = jnp.concatenate([freqs, freqs], axis=-1)
            return (jnp.cos(emb).astype(dtype), jnp.sin(emb).astype(dtype))

        def _rotate_half(x):
            x1, x2 = jnp.split(x, 2, axis=-1)
            return jnp.concatenate([-x2, x1], axis=-1)

        def _apply_rope(x, cos, sin):
            return x * cos + _rotate_half(x) * sin
        B, T, D = x.shape
        H, hd = (HEADS, HEAD_DIM)
        qkv = (x @ W_qkv).reshape(B, T, 3, H, hd).transpose(2, 0, 3, 1, 4)
        q, k, v = (qkv[0], qkv[1], qkv[2])
        cos, sin = _rope_cos_sin(T, q.dtype)
        q = _apply_rope(q, cos, sin)
        k = _apply_rope(k, cos, sin)
        q_feat = jax.nn.elu(q * SCALE) + 1.0
        k_feat = jax.nn.elu(k) + 1.0
        kv = jnp.einsum('bhtd,bhtv->bhdv', k_feat, v)
        k_sum = k_feat.sum(axis=2)
        denom = jnp.maximum(jnp.einsum('bhtd,bhd->bht', q_feat, k_sum), 1e-06)
        out = jnp.einsum('bhtd,bhdv->bhtv', q_feat, kv) / denom[..., None]
        out = out.transpose(0, 2, 1, 3).reshape(B, T, D)
        return out @ W_out

    def _L1_ffn_ref(x, W_r, W_k, W_v, mu_r, mu_k):
        import jax, jax.numpy as jnp
        import numpy as np
        DIM = 256

        def _reference_tuple_inner(x, W_r, W_k, W_v, mu_r, mu_k):
            B, T, C = x.shape
            x_prev = jnp.concatenate([jnp.zeros((B, 1, C), x.dtype), x[:, :-1, :]], axis=1)
            xr = mu_r * x + (1.0 - mu_r) * x_prev
            xk = mu_k * x + (1.0 - mu_k) * x_prev
            r = jax.nn.sigmoid(jnp.einsum('btc,dc->btd', xr, W_r))
            k = jnp.einsum('btc,dc->btd', xk, W_k)
            k_act = jnp.square(jax.nn.relu(k))
            out = r * jnp.einsum('btc,dc->btd', k_act, W_v)
            new_state = x[:, -1, :]
            return (out, new_state)
        return _reference_tuple_inner(x, W_r, W_k, W_v, mu_r, mu_k)[0]
    x = L0_attn_x
    xn = _layernorm(x, axis=-1)
    x = x + _L0_attn_ref(xn, L0_attn_Wq, L0_attn_Wk, L0_attn_Wv) + _L0_ffn_ref(xn, L0_ffn_Wr, L0_ffn_br, L0_ffn_W1, L0_ffn_b1, L0_ffn_W2, L0_ffn_b2)
    xn = _layernorm(x, axis=-1)
    x = x + _L1_attn_ref(xn, L1_attn_W_qkv, L1_attn_W_out) + _L1_ffn_ref(xn, L1_ffn_W_r, L1_ffn_W_k, L1_ffn_W_v, L1_ffn_mu_r, L1_ffn_mu_k)
    return x

_drawn_inputs = setup_inputs


def setup_inputs(seed=0):
    import zlib

    import numpy as np

    out = dict(_drawn_inputs(seed))
    spreads = {'L0_ffn_br': (0.0, 0.1), 'L0_ffn_b1': (0.0, 0.1), 'L0_ffn_b2': (0.0, 0.1)}
    factors = {'L1_ffn_W_r': 3.651, 'L1_ffn_mu_r': 7.438}
    for name, (base, spread) in spreads.items():
        noise = np.random.default_rng([zlib.crc32(name.encode()), seed]).standard_normal(out[name].shape)
        drawn = base * np.exp(spread * noise) if base else spread * noise
        out[name] = jnp.asarray(drawn.astype(out[name].dtype))
    for name, factor in factors.items():
        out[name] = (out[name] * factor).astype(out[name].dtype)
    return out
```

```python
from contextlib import ExitStack

import concourse.bass as bass
from concourse import mybir

F32 = mybir.dt.float32
F32R = mybir.dt.float32r
BF16 = mybir.dt.bfloat16
I32 = mybir.dt.int32
U32 = mybir.dt.uint32
ALU = mybir.AluOpType
ACT = mybir.ActivationFunctionType
X = mybir.AxisListType.X
ds = bass.ds

P = 128
EPS = 1e-5
MASKED = -1e30


def hold(eng, semaphore, value, passed):
    eng.wait_ge(semaphore, value)
    eng.sem_inc(passed, 1)


class Shapes:

    def __init__(self, x, W1):
        self.B, self.T, self.D = x.shape
        self.E, _, self.H = W1.shape
        self.N = self.B * self.T
        self.DC = self.D // P
        self.HC = self.H // P
        self.BT = self.T // P
        self.NT = self.N // P
        self.K = 2
        self.M = 256
        self.MT = (self.K * self.N + self.E * (self.M - 1)) // self.M
        assert self.DC == 2 and self.B == 4 and self.MT % 2 == 1


def constants(nc, s):
    ctx = s.ctx

    def sb(name, shape, dt=F32):
        return ctx.enter_context(nc.sbuf_tensor(name, shape, dt))

    s.x_acc = sb("x_acc", [P, s.NT * s.D])
    s.ident = sb("ident", [P, P])
    s.slots = sb("slots", [P, s.NT * s.K], U32)
    s.gates = sb("gates", [P, s.NT * s.K])
    s.tile_expert = sb("tile_expert", [P, s.MT + 1], I32)
    s.b1T = sb("b1T", [P, s.E * s.HC])
    s.eps = sb("eps", [P, 1])
    s.ps = ctx.enter_context(nc.psum_tensor("ps", [P, 8, 512], F32))


def norm_route_attend(nc, s, x, Wq, Wk, Wv, Wr, br, b1, xn_rows, dispatched):
    B, BT, NT, D, DC, E, K, T, M, MT = s.B, s.BT, s.NT, s.D, s.DC, s.E, s.K, s.T, s.M, s.MT
    ps = s.ps
    with ExitStack() as ctx:
        def sb(name, shape, dt=F32):
            return ctx.enter_context(nc.sbuf_tensor(name, shape, dt))

        def sem(name):
            return ctx.enter_context(nc.semaphore(name))

        xnT = sb("xnT", [P, DC, s.N])
        xn = sb("xn", [P, 2, BT, D])
        xh, xl = sb("xh", [P, DC, T], F32R), sb("xl", [P, DC, T], F32R)
        qkh, qkl = sb("qkh", [P, 2, DC, T], F32R), sb("qkl", [P, 2, DC, T], F32R)
        vh, vl = sb("vh", [P, BT, D], F32R), sb("vl", [P, BT, D], F32R)
        wh, wl = sb("wh", [P, 3, DC, D], F32R), sb("wl", [P, 3, DC, D], F32R)
        wraw = xh[:, :, :].rearrange("p c t -> p (c t)")[:, 0:3 * DC * D].bitcast(F32)
        prob = sb("prob", [P, 2, T])
        pTh, pTl = sb("pTh", [P, 2, BT, P], F32R), sb("pTl", [P, 2, BT, P], F32R)
        row_sum, row_inv, neg_max = sb("row_sum", [P, BT]), sb("row_inv", [P, BT]), sb("neg_max", [P, BT])
        ident_b, above = sb("ident_b", [P, P], BF16), sb("above", [P, P], BF16)
        w3 = sb("w3", [P, 3, DC, D])
        earlier, ones = sb("earlier", [P, P]), sb("ones", [P, P])
        zero = sb("zero", [P, D])
        wr, brc = sb("wr", [P, DC, E]), sb("brc", [E, 1])
        lgT = sb("lgT", [E, T])
        stats, mv = sb("stats", [P, BT, 6]), sb("mv", [P, BT, 2])
        std, rstd = sb("std", [P, BT]), sb("rstd", [P, BT])
        b1r = sb("b1r", [E * s.HC, P])
        logits = sb("logits", [P, NT * E])
        R = [prob[:, n // 4, (n % 4) * NT * E:(n % 4 + 1) * NT * E].rearrange("p (t e) -> p t e", e=E) for n in range(8)]
        col = sb("col", [P, 8, NT])
        expert_row = sb("expert_row", [P, 6, E])
        expert_int = sb("expert_int", [P, E], I32)
        rank8, tile_no = sb("rank8", [P, E]), sb("tile_no", [P, MT + 1])
        cmp = sb("cmp", [P, MT + 1, E - 1])
        cnt = sb("cnt", [P, MT + 1])
        xrow, slot_now = sb("xrow", [P, 4, D]), sb("slot_now", [P, 4, K], U32)

        x_loaded = [sem(f"x_loaded{b}") for b in range(B)]
        w_loaded, small_loaded = sem("w_loaded"), sem("small_loaded")
        const_ready, zero_ready, zero_filled = sem("const_ready"), sem("zero_ready"), sem("zero_filled")
        wh_ready, wl_ready = sem("wh_ready"), sem("wl_ready")
        b1_turned, b1_ready = sem("b1_turned"), sem("b1_ready")
        stats_done, mv_done, std_done, rstd_done, xn_ready = (sem(n) for n in (
            "stats_done", "mv_done", "std_done", "rstd_done", "xn_ready"))
        xn_stored = [sem(f"xn_stored{u}") for u in range(2)]
        turned, xnT_ready, lgT_mm, lgT_ready, lg_turned, lg_ready = (sem(n) for n in (
            "turned", "xnT_ready", "lgT_mm", "lgT_ready", "lg_turned", "lg_ready"))
        step, passed = sem("step"), sem("passed")
        centered, exp_done, picked, counted, routed = (sem(n) for n in (
            "centered", "exp_done", "picked", "counted", "routed"))
        row_loaded = [sem(f"row_loaded{u}") for u in range(4)]
        slot_staged = sem("slot_staged")
        scattered = [sem(f"scattered{u}") for u in range(4)]
        xh_ready, xl_ready, proj_mm, proj_hi, proj_lo = (sem(n) for n in (
            "xh_ready", "xl_ready", "proj_mm", "proj_hi", "proj_lo"))
        score_mm, max_done, prob_ready, prob_turned, pT_hi, pT_lo, pv_mm, inv_done, attended = (sem(n) for n in (
            "score_mm", "max_done", "prob_ready", "prob_turned", "pT_hi", "pT_lo", "pv_mm", "inv_done", "attended"))

        def x_tile(t):
            return s.x_acc[:, ds(t * D, D)]

        NPROJ = 2 * DC * (T // 512) + BT // 2
        block = ctx.enter_context(nc.Block())

        @block.sync
        def _(sp):
            xv = x.rearrange("b (i p) d -> b p i d", p=P)
            for b in range(B):
                sp.dma_start(s.x_acc[:, b * BT * D:(b + 1) * BT * D].rearrange("p (i d) -> p i d", d=D),
                             xv[b]).then_inc(x_loaded[b], 16)
                if b == 0:
                    sp.dma_start(wr[:, :, :], Wr.rearrange("(c p) e -> p c e", p=P)).then_inc(small_loaded, 16)
                    sp.dma_start(brc[:, :], br.rearrange("(e a) -> e a", a=1)).then_inc(small_loaded, 16)
                    sp.dma_start(b1r[:, :], b1.rearrange("e (c p) -> (e c) p", p=P)).then_inc(small_loaded, 16)
                    for n, w in enumerate((Wq, Wk, Wv)):
                        sp.dma_start(w3[:, n], w.rearrange("(c p) e -> p c e", p=P)).then_inc(w_loaded, 16)
            sp.wait_ge(zero_ready, 1)
            nz = MT * M // P
            sp.dma_start(dispatched.rearrange("(p n) d -> p n d", p=P),
                         zero[:, :].unsqueeze(1).to_broadcast([P, nz, D])).then_inc(zero_filled, 16)
            for u in range(2):
                sp.sem_inc(xn_stored[u], 16)
            for b in range(B):
                sp.wait_ge(xn_ready, b + 1)
                sp.dma_start(xn_rows.rearrange("(b i p) d -> b p i d", b=B, p=P)[b], xn[:, b % 2]
                             ).then_inc(xn_stored[b % 2], 16)
            for u in range(2):
                sp.wait_ge(xn_stored[u], 16 + 16 * (B // 2))

            def load_rows(t, u):
                sp.dma_start(xrow[:, u], xn_rows[ds(t * P, P), :]).then_inc(row_loaded[u], 16)

            for u in range(4):
                load_rows(u, u)
            with sp.Fori(1, NT // 4) as g:
                for u in range(4):
                    sp.wait_ge(scattered[u], 16 * K * g)
                    load_rows(4 * g + u, u)

        @block.gpsimd
        def _(pool):
            pool.memset(zero[:, :], 0.0).then_inc(zero_ready, 1)
            pool.memset(s.ident[:, :], 0.0).then_inc(const_ready, 1)
            pool.memset(ident_b[:, :], 0.0).then_inc(const_ready, 1)
            pool.memset(above[:, :], 0.0).then_inc(const_ready, 1)
            pool.memset(earlier[:, :], 1.0).then_inc(const_ready, 1)
            pool.memset(ones[:, :], 1.0).then_inc(const_ready, 1)
            pool.memset(s.eps[:, :], EPS).then_inc(const_ready, 1)
            pool.iota(tile_no[:, :], [[1, MT + 1]], base=0, channel_multiplier=0,
                      allow_small_or_imprecise_dtypes=True).then_inc(const_ready, 1)
            pool.iota(rank8[:, :], [[-1, E]], base=E, channel_multiplier=0,
                      allow_small_or_imprecise_dtypes=True).then_inc(const_ready, 1)
            pool.wait_ge(const_ready, 8)
            for m in (s.ident, ident_b):
                pool.affine_select(out=m[:, :], in_=m[:, :], compare_op=ALU.not_equal, fill=1.0, base=0,
                                   pattern=[[-1, P]], channel_multiplier=1).then_inc(const_ready, 1)
            pool.affine_select(out=above[:, :], in_=above[:, :], compare_op=ALU.is_ge, fill=MASKED, base=0,
                               pattern=[[-1, P]], channel_multiplier=1).then_inc(const_ready, 1)
            pool.affine_select(out=earlier[:, :], in_=earlier[:, :], compare_op=ALU.is_gt, fill=0.0, base=0,
                               pattern=[[1, P]], channel_multiplier=-1).then_inc(const_ready, 1)

            pool.wait_ge(routed, 1)
            pool.wait_ge(zero_filled, 16)

            def scatter(t, u, turn):
                if turn is not None:
                    hold(pool, scattered[u], 16 * K * turn, passed)
                pool.tensor_copy(slot_now[:, u, :], s.slots[:, ds(K * t, K)]).then_inc(slot_staged, 1)
                hold(pool, slot_staged, t + 1, passed)
                hold(pool, row_loaded[u], 16 if turn is None else 16 * turn + 16, passed)
                for k in range(K):
                    pool.indirect_dma_start(out=dispatched, out_offset=bass.IndirectOffsetOnAxis(
                        ap=slot_now[:, u, k:k + 1], axis=0), in_=xrow[:, u], in_offset=None).then_inc(scattered[u], 16)

            for u in range(4):
                scatter(u, u, None)
            with pool.Fori(1, NT // 4) as g:
                for u in range(4):
                    scatter(4 * g + u, u, g)
            for u in range(4):
                pool.wait_ge(scattered[u], 16 * K * (NT // 4))

        @block.tensor
        def _(pe):
            pe.wait_ge(const_ready, 12)
            pe.wait_ge(small_loaded, 48)
            pe.transpose(ps[:, 7, 0:E * s.HC], b1r[:, :], s.ident[0:E * s.HC, 0:E * s.HC]).then_inc(b1_turned, 1)

            with pe.Fori(0, B // 2) as g:
                for u in range(2):
                    b = 2 * g + u
                    pe.wait_ge(xn_ready, b + 1)
                    for q in range(4):
                        c, half = q // 2, q % 2
                        for i in range(4):
                            mm = pe.transpose(ps[:, q, i * P:(i + 1) * P],
                                              xn[:, u, half * 4 + i, c * P:(c + 1) * P], s.ident[:, :])
                        mm.then_inc(turned, 1)
                    pe.wait_ge(xnT_ready, 4 * b + 4)
                    for half in range(2):
                        for c in range(DC):
                            mm = pe.matmul(ps[0:E, 4 + half, :], wr[:, c, :], xnT[:, c, ds(b * T + half * 512, 512)],
                                           start=(c == 0), stop=(c == DC - 1))
                    mm.then_inc(lgT_mm, 1)
                    hold(pe, lgT_ready, b + 1, passed)
                    for i in range(BT):
                        mm = pe.transpose(ps[:, 6, i * E:(i + 1) * E], lgT[:, i * P:(i + 1) * P], s.ident[0:E, 0:E])
                    mm.then_inc(lg_turned, 1)

            pe.wait_ge(picked, 1)
            pe.wait_ge(b1_ready, 1)
            pe.matmul(ps[:, 7, 0:NT * E], earlier[:, :], R[6], start=True, stop=True)
            pe.matmul(ps[:, 6, 0:NT * E], ones[:, :], R[6], start=True, stop=True).then_inc(counted, 1)

            def three(out, ah, al, bh, bl, start, stop):
                pe.matmul(out, ah, bh, start=start, stop=False, skip_group_check=True)
                pe.matmul(out, ah, bl, start=False, stop=False, skip_group_check=True)
                return pe.matmul(out, al, bh, start=False, stop=stop, skip_group_check=True)

            pe.wait_ge(wl_ready, 1)
            pe.wait_ge(routed, 1)
            with pe.Fori(0, B) as b:
                pe.wait_ge(xl_ready, b + 1)
                for n in range(NPROJ):
                    if n >= 4:
                        pe.wait_ge(proj_lo, NPROJ * b + n - 3)
                    bank = ps[:, n % 4, :]
                    if n < 2 * DC * 2:
                        w, m, half = n // 4, n // 2 % 2, n % 2
                        for c in range(DC):
                            mm = three(bank, wh[:, w, c, m * P:(m + 1) * P], wl[:, w, c, m * P:(m + 1) * P],
                                       xh[:, c, half * 512:(half + 1) * 512], xl[:, c, half * 512:(half + 1) * 512],
                                       c == 0, c == DC - 1)
                    else:
                        for j in range(2):
                            i = 2 * (n - 8) + j
                            for c in range(DC):
                                mm = three(bank[:, j * D:(j + 1) * D], xh[:, c, i * P:(i + 1) * P],
                                           xl[:, c, i * P:(i + 1) * P], wh[:, 2, c, :], wl[:, 2, c, :],
                                           c == 0, c == DC - 1)
                    mm.then_inc(proj_mm, 1)

                def scores(i):
                    if i == 0:
                        pe.wait_ge(proj_lo, NPROJ * b + NPROJ)
                    L = (i + 1) * P
                    for h in range((L + 511) // 512):
                        w = min(512, L - 512 * h)
                        bank = ps[:, 2 * (i % 2) + h, 0:w]
                        for c in range(DC):
                            qs, ks = slice(i * P, i * P + P), slice(512 * h, 512 * h + w)
                            mm = three(bank, qkh[:, 0, c, qs], qkl[:, 0, c, qs], qkh[:, 1, c, ks], qkl[:, 1, c, ks],
                                       c == 0, False)
                    mm = pe.matmul(bank[:, w - P:w], ident_b[:, :], above[:, :], start=False, stop=True,
                                   skip_group_check=True)
                    mm.then_inc(score_mm, 1)

                def turn(i):
                    pe.wait_ge(prob_ready, BT * b + i + 1)
                    if i > 0:
                        pe.wait_ge(pT_lo, BT * b + i)
                    for j in range(i + 1):
                        mm = pe.transpose(ps[:, 4 + j // 4, (j % 4) * P:(j % 4 + 1) * P],
                                          prob[:, i % 2, j * P:(j + 1) * P], s.ident[:, :])
                    mm.then_inc(prob_turned, 1)

                def values(i):
                    pe.wait_ge(pT_lo, BT * b + i + 1)
                    pe.wait_ge(attended, BT * b + i + 1)
                    for j in range(i + 1):
                        mm = three(ps[:, 6 + i % 2, 0:D], pTh[:, i % 2, j], pTl[:, i % 2, j], vh[:, j, :], vl[:, j, :],
                                   j == 0, j == i)
                    mm.then_inc(pv_mm, 1)

                scores(0)
                for i in range(BT):
                    if i + 1 < BT:
                        scores(i + 1)
                    turn(i)
                    if i > 0:
                        values(i - 1)
                values(BT - 1)

        @block.scalar
        def _(act):
            act.wait_ge(b1_turned, 1)
            act.activation(s.b1T[:, :], ps[:, 7, 0:E * s.HC], ACT.Copy).then_inc(b1_ready, 1)
            act.wait_ge(w_loaded, 48)
            act.activation(wh[:, :, :, :], w3[:, :, :, :], ACT.Copy).then_inc(wh_ready, 1)
            act.wait_ge(const_ready, 12)
            act.wait_ge(small_loaded, 48)
            with act.Fori(0, B) as b:
                act.wait_ge(mv_done, b + 1)
                act.activation(std[:, :], mv[:, :, 1], ACT.Sqrt, bias=s.eps[:, 0:1]).then_inc(std_done, 1)
                for q in range(4):
                    act.wait_ge(turned, 4 * b + q + 1)
                    act.activation(xnT[:, q // 2, ds(b * T + q % 2 * 512, 512)], ps[:, q, :], ACT.Copy
                                   ).then_inc(xnT_ready, 1)
                act.wait_ge(lgT_mm, b + 1)
                act.activation(lgT[:, :], ps[0:E, 4:6, :], ACT.Identity, bias=brc[:, 0:1]).then_inc(lgT_ready, 1)
                act.wait_ge(lg_turned, b + 1)
                act.activation(logits[:, ds(b * BT * E, BT * E)], ps[:, 6, 0:BT * E], ACT.Copy).then_inc(lg_ready, 1)

            act.wait_ge(centered, 1)
            act.activation(R[1], R[0], ACT.Exp).then_inc(exp_done, 1)

            act.wait_ge(routed, 1)
            with act.Fori(0, B) as b:
                act.activation(xh[:, :, :], xnT[:, :, ds(b * T, T)], ACT.Copy).then_inc(xh_ready, 1)
                act.wait_ge(xl_ready, b + 1)
                for n in range(NPROJ):
                    act.wait_ge(proj_mm, NPROJ * b + n + 1)
                    if n < 8:
                        act.activation(qkh[:, n // 4, n // 2 % 2, n % 2 * 512:(n % 2 + 1) * 512], ps[:, n % 4, :],
                                       ACT.Copy, scale=D ** -0.5 if n < 4 else 1.0).then_inc(proj_hi, 1)
                    else:
                        act.activation(vh[:, 2 * (n - 8):2 * (n - 8) + 2, :],
                                       ps[:, n % 4, :].rearrange("p (j d) -> p j d", j=2), ACT.Copy
                                       ).then_inc(proj_hi, 1)

                def softmax(i):
                    act.wait_ge(max_done, BT * b + i + 1)
                    L = (i + 1) * P
                    act.activation(prob[:, i % 2, 0:L], ps[:, 2 * (i % 2):2 * (i % 2) + 2, :].rearrange(
                        "p h k -> p (h k)")[:, 0:L], ACT.Exp, bias=neg_max[:, i:i + 1],
                        accum_out=row_sum[:, i:i + 1]).then_inc(prob_ready, 1)

                def turned_hi(i):
                    act.wait_ge(prob_turned, BT * b + i + 1)
                    act.wait_ge(attended, BT * b + i + 1)
                    L = (i + 1) * P
                    act.activation(pTh[:, i % 2, 0:i + 1, :].rearrange("p j q -> p (j q)"),
                                   ps[:, 4:6, :].rearrange("p h k -> p (h k)")[:, 0:L], ACT.Copy).then_inc(pT_hi, 1)

                softmax(0)
                for i in range(BT):
                    if i + 1 < BT:
                        softmax(i + 1)
                    turned_hi(i)

        @block.vector
        def _(dve):
            V = nc.vector
            dve.sem_inc(attended, 2)
            dve.wait_ge(const_ready, 12)
            for h in range(2):
                dve.wait_ge(x_loaded[h], 16)
            dve.wait_ge(wh_ready, 1)
            V.tensor_tensor(wl[:, :, :, :], w3[:, :, :, :], wh[:, :, :, :].bitcast(F32), ALU.subtract
                            ).then_inc(wl_ready, 1)
            for h in range(2, B):
                dve.wait_ge(x_loaded[h], 16)
            with dve.Fori(0, B // 2) as g:
                for u in range(2):
                    b = 2 * g + u
                    for i in range(BT):
                        op = V.bn_stats(stats[:, i, :], x_tile(b * BT + i))
                    op.then_inc(stats_done, 1)
                    hold(dve, stats_done, b + 1, passed)
                    for i in range(BT):
                        op = V.bn_aggr(mv[:, i, :], stats[:, i, :])
                    op.then_inc(mv_done, 1)
                    dve.wait_ge(std_done, b + 1)
                    V.reciprocal(rstd[:, :], std[:, :]).then_inc(rstd_done, 1)
                    dve.wait_ge(rstd_done, b + 1)
                    dve.wait_ge(xn_stored[u], 16 * g + 16)
                    for i in range(BT):
                        op = V.tensor_scalar(xn[:, u, i, :], x_tile(b * BT + i), mv[:, i, 0:1], rstd[:, i:i + 1],
                                             ALU.subtract, ALU.mult)
                    op.then_inc(xn_ready, 1)

            steps = [0]

            def then(op):
                steps[0] += 1
                op.then_inc(step, 1)
                dve.wait_ge(step, steps[0])

            def per_tile(a):
                return a.unsqueeze(2).to_broadcast([P, NT, E])

            def per_expert(a):
                return a.unsqueeze(1).to_broadcast([P, NT, E])

            lg = logits[:, :].rearrange("p (t e) -> p t e", e=E)
            dve.wait_ge(lg_ready, B)
            then(V.tensor_reduce(col[:, 0, :], lg, X, ALU.max))
            V.tensor_tensor(R[0], lg, per_tile(col[:, 0, :]), ALU.subtract).then_inc(centered, 1)
            dve.wait_ge(exp_done, 1)
            then(V.tensor_reduce(col[:, 1, :], R[1], X, ALU.add))
            then(V.reciprocal(col[:, 2, :], col[:, 1, :]))
            then(V.tensor_tensor(R[2], R[1], per_tile(col[:, 2, :]), ALU.mult))

            def pick(p, best, one_hot, scratch, key):
                then(V.tensor_reduce(best, p, X, ALU.max))
                then(V.tensor_tensor(scratch, p, per_tile(best), ALU.is_equal))
                then(V.tensor_tensor(scratch, scratch, per_expert(rank8[:, :]), ALU.mult))
                then(V.tensor_reduce(key, scratch, X, ALU.max))
                then(V.tensor_tensor(one_hot, scratch, per_tile(key), ALU.is_equal))

            pick(R[2], col[:, 3, :], R[3], R[0], col[:, 4, :])
            then(V.scalar_tensor_tensor(R[1], R[3], -4.0, R[2], ALU.mult, ALU.add))
            pick(R[1], col[:, 5, :], R[4], R[0], col[:, 4, :])
            V.tensor_tensor(R[6], R[3], R[4], ALU.add).then_inc(picked, 1)
            then(V.tensor_tensor(col[:, 6, :], col[:, 3, :], col[:, 5, :], ALU.add))
            then(V.reciprocal(col[:, 7, :], col[:, 6, :]))
            gv = s.gates[:, :].rearrange("p (t k) -> p t k", k=K)
            then(V.tensor_tensor(gv[:, :, 0], col[:, 3, :], col[:, 7, :], ALU.mult))
            then(V.tensor_tensor(gv[:, :, 1], col[:, 5, :], col[:, 7, :], ALU.mult))
            then(V.memset(col[:, 0, :], 1.0))
            dve.wait_ge(counted, 1)
            total = ps[:, 6, 0:NT * E].rearrange("p (t e) -> p t e", e=E)
            for e in range(E):
                op = V.tensor_tensor_scan(R[5][:, :, e], col[:, 0, :], total[:, :, e], 0.0, ALU.mult, ALU.add)
            then(op)
            then(V.tensor_tensor(R[7], R[5], total, ALU.subtract))
            then(V.tensor_scalar(expert_int[:, :], R[5][:, NT - 1, :], float(M - 1), None, ALU.add))
            then(V.tensor_scalar(expert_int[:, :], expert_int[:, :], M.bit_length() - 1, None, ALU.arith_shift_right))
            then(V.tensor_copy(expert_row[:, 0, :], expert_int[:, :]))
            then(V.memset(expert_row[:, 1, :], 1.0))
            then(V.tensor_tensor_scan(expert_row[:, 2, :], expert_row[:, 1, :], expert_row[:, 0, :], 0.0,
                                      ALU.mult, ALU.add))
            then(V.tensor_tensor(expert_row[:, 3, :], expert_row[:, 2, :], expert_row[:, 0, :], ALU.subtract))
            then(V.tensor_scalar(expert_row[:, 4, :], expert_row[:, 3, :], float(M), None, ALU.mult))
            then(V.tensor_tensor(R[7], R[7], per_expert(expert_row[:, 4, :]), ALU.add))
            before = ps[:, 7, 0:NT * E].rearrange("p (t e) -> p t e", e=E)
            then(V.tensor_tensor(R[7], R[7], before, ALU.add))
            sv = s.slots[:, :].rearrange("p (t k) -> p t k", k=K)
            for k in range(K):
                then(V.tensor_tensor(R[0], R[7], R[3 + k], ALU.mult))
                then(V.tensor_reduce(col[:, 1, :], R[0], X, ALU.add))
                then(V.tensor_copy(sv[:, :, k], col[:, 1, :]))
            then(V.tensor_tensor(cmp[:, :, :], tile_no[:, :].unsqueeze(2).to_broadcast([P, MT + 1, E - 1]),
                                 expert_row[:, 2, 0:E - 1].unsqueeze(1).to_broadcast([P, MT + 1, E - 1]), ALU.is_ge))
            then(V.tensor_reduce(cnt[:, :], cmp[:, :, :], X, ALU.add))
            V.tensor_copy(s.tile_expert[:, :], cnt[:, :]).then_inc(routed, 1)

            with dve.Fori(0, B) as b:
                dve.wait_ge(xh_ready, b + 1)
                V.tensor_tensor(xl[:, :, :], xnT[:, :, ds(b * T, T)], xh[:, :, :].bitcast(F32), ALU.subtract
                                ).then_inc(xl_ready, 1)
                for n in range(NPROJ):
                    dve.wait_ge(proj_hi, NPROJ * b + n + 1)
                    if n < 8:
                        at = (slice(None), n // 4, n // 2 % 2, slice(n % 2 * 512, (n % 2 + 1) * 512))
                        V.scalar_tensor_tensor(qkl[at], ps[:, n % 4, :], D ** -0.5 if n < 4 else 1.0,
                                               qkh[at].bitcast(F32), ALU.mult, ALU.subtract).then_inc(proj_lo, 1)
                    else:
                        at = (slice(None), slice(2 * (n - 8), 2 * (n - 8) + 2), slice(None))
                        V.tensor_tensor(vl[at], ps[:, n % 4, :].rearrange("p (j d) -> p j d", j=2),
                                        vh[at].bitcast(F32), ALU.subtract).then_inc(proj_lo, 1)

                def row_max(i):
                    dve.wait_ge(score_mm, BT * b + i + 1)
                    L = (i + 1) * P
                    V.tensor_reduce(neg_max[:, i:i + 1], ps[:, 2 * (i % 2):2 * (i % 2) + 2, :].rearrange(
                        "p h k -> p (h k)")[:, 0:L], X, ALU.max, negate=True).then_inc(max_done, 1)

                def turned_lo(i):
                    dve.wait_ge(pT_hi, BT * b + i + 1)
                    L = (i + 1) * P
                    V.tensor_tensor(pTl[:, i % 2, 0:i + 1, :].rearrange("p j q -> p (j q)"),
                                    ps[:, 4:6, :].rearrange("p h k -> p (h k)")[:, 0:L],
                                    pTh[:, i % 2, 0:i + 1, :].rearrange("p j q -> p (j q)").bitcast(F32),
                                    ALU.subtract).then_inc(pT_lo, 1)

                def add_attention(i):
                    V.reciprocal(row_inv[:, i:i + 1], row_sum[:, i:i + 1]).then_inc(inv_done, 1)
                    dve.wait_ge(inv_done, BT * b + i + 1)
                    dve.wait_ge(pv_mm, BT * b + i + 1)
                    V.scalar_tensor_tensor(x_tile(b * BT + i), ps[:, 6 + i % 2, 0:D], row_inv[:, i:i + 1],
                                           x_tile(b * BT + i), ALU.mult, ALU.add).then_inc(attended, 1)

                row_max(0)
                for i in range(BT):
                    if i + 1 < BT:
                        row_max(i + 1)
                    turned_lo(i)
                    if i > 0:
                        add_attention(i - 1)
                add_attention(BT - 1)


def experts(nc, s, W1, W2, b2, dispatched, expert_out):
    D, DC, E, H, HC, M, MT = s.D, s.DC, s.E, s.H, s.HC, s.M, s.MT
    MS = M // P
    NQ = HC // 2
    ps = s.ps
    with ExitStack() as ctx:
        def sb(name, shape, dt=F32):
            return ctx.enter_context(nc.sbuf_tensor(name, shape, dt))

        def sem(name):
            return ctx.enter_context(nc.semaphore(name))

        w1raw, w2raw = sb("w1raw", [P, 2, DC, H]), sb("w2raw", [P, 2, HC, D])
        w1h, w1l = sb("w1h", [P, 2, DC, H], F32R), sb("w1l", [P, 2, DC, H], F32R)
        w2h, w2l = sb("w2h", [P, 2, HC, D], F32R), sb("w2l", [P, 2, HC, D], F32R)
        rows = sb("rows", [P, 2, MS, D])
        xTh, xTl = sb("xTh", [P, DC, M], F32R), sb("xTl", [P, DC, M], F32R)
        h32 = sb("h32", [P, HC, M])
        hh, hl = sb("hh", [P, HC, M], F32R), sb("hl", [P, HC, M], F32R)
        y = sb("y", [P, 2, MS, D])
        b2all = sb("b2all", [P, E * D])

        b2_loaded, passed = sem("b2_loaded"), sem("passed")
        rows_loaded = [sem(f"rows_loaded{u}") for u in range(2)]
        w1_loaded = [sem(f"w1_loaded{u}") for u in range(2)]
        w2_loaded = [sem(f"w2_loaded{u}") for u in range(2)]
        y_stored = [sem(f"y_stored{u}") for u in range(2)]
        w1_hi, w1_lo, w2_hi, w2_lo = sem("w1_hi"), sem("w1_lo"), sem("w2_hi"), sem("w2_lo")
        rows_turned, xT_hi, xT_lo = sem("rows_turned"), sem("xT_hi"), sem("xT_lo")
        up_mm, relu_done, h_hi, h_lo, down_mm, y_done = (sem(n) for n in (
            "up_mm", "relu_done", "h_hi", "h_lo", "down_mm", "y_done"))

        def tiles(eng, body):
            body(0, 0)
            body(0, 1)
            with eng.Fori(1, MT // 2) as g:
                body(g, 0)
                body(g, 1)
            body(MT // 2, 0)

        def is_last(g, u):
            return isinstance(g, int) and 2 * g + u == MT - 1

        def following(g, u):
            return (g, 1) if u == 0 else (g + 1, 0)

        def first(g):
            return isinstance(g, int) and g == 0

        def expert_of(eng, g, u):
            return eng.value_load(s.tile_expert[0:1, ds(2 * g + u, 1)], min_val=0, max_val=E - 1)

        block = ctx.enter_context(nc.Block())

        @block.sync
        def _(sp):
            sp.dma_start(b2all[:, :], b2.rearrange("e d -> (e d)").partition_broadcast(P)).then_inc(b2_loaded, 16)
            w1v = W1.rearrange("e (c p) h -> e p c h", p=P)
            w2v = W2.rearrange("e (k p) d -> e p k d", p=P)

            def load(g, u):
                j = 2 * g + u
                e = expert_of(sp, g, u)
                if not first(g):
                    sp.wait_ge(rows_turned, j - 1)
                sp.dma_start(rows[:, u], dispatched[ds(j * M, M), :].rearrange("(s p) d -> p s d", p=P)
                             ).then_inc(rows_loaded[u], 16)
                if not first(g):
                    sp.wait_ge(w1_lo, NQ * (j - 1))
                sp.dma_start(w1raw[:, u], w1v[e]).then_inc(w1_loaded[u], 16)
                if not first(g):
                    sp.wait_ge(w2_lo, NQ * (j - 1))
                sp.dma_start(w2raw[:, u], w2v[e]).then_inc(w2_loaded[u], 16)

            tiles(sp, load)

        @block.gpsimd
        def _(pool):
            def split(g, u, q):
                pool.tensor_copy(w2h[:, u, 2 * q:2 * q + 2, :], w2raw[:, u, 2 * q:2 * q + 2, :]).then_inc(w2_hi, 1)

            def store(g, u):
                j = 2 * g + u
                hold(pool, y_done, j + 1, passed)
                pool.dma_start(expert_out[ds(j * M, M), :].rearrange("(s p) d -> p s d", p=P), y[:, u]
                               ).then_inc(y_stored[u], 16)

            pool.wait_ge(w2_loaded[0], 16)
            for q in range(NQ):
                split(0, 0, q)

            def body(g, u):
                if not is_last(g, u):
                    ng, nu = following(g, u)
                    hold(pool, w2_loaded[nu], 16 * ng + 16, passed)
                    if not (isinstance(g, int) and 2 * g + u == 0):
                        hold(pool, down_mm, 2 * g + u, passed)
                    for q in range(NQ):
                        split(ng, nu, q)
                store(g, u)

            tiles(pool, body)
            pool.wait_ge(y_stored[0], 16 * (MT // 2 + 1))
            pool.wait_ge(y_stored[1], 16 * (MT // 2))

        @block.tensor
        def _(pe):
            def three(out, ah, al, bh, bl, start, stop):
                pe.matmul(out, ah, bh, start=start, stop=False, skip_group_check=True)
                pe.matmul(out, ah, bl, start=False, stop=False, skip_group_check=True)
                return pe.matmul(out, al, bh, start=False, stop=stop, skip_group_check=True)

            def turn_rows(g, u):
                pe.wait_ge(rows_loaded[u], 16 * g + 16)
                for c in range(DC):
                    for part in range(MS):
                        mm = pe.transpose(ps[:, 6, c * M + part * P:c * M + (part + 1) * P],
                                          rows[:, u, part, c * P:(c + 1) * P], s.ident[:, :])
                mm.then_inc(rows_turned, 1)

            turn_rows(0, 0)

            def body(g, u):
                j = 2 * g + u
                pe.wait_ge(xT_lo, j + 1)
                pe.wait_ge(w1_lo, NQ * (j + 1))
                for q in range(NQ):
                    for k in (2 * q, 2 * q + 1):
                        for c in range(DC):
                            ws = slice(k * P, (k + 1) * P)
                            mm = three(ps[:, q, (k % 2) * M:(k % 2 + 1) * M], w1h[:, u, c, ws], w1l[:, u, c, ws],
                                       xTh[:, c, :], xTl[:, c, :], c == 0, c == DC - 1)
                    mm.then_inc(up_mm, 1)
                if not is_last(g, u):
                    turn_rows(*following(g, u))
                pe.wait_ge(w2_lo, NQ * (j + 1))
                if not (isinstance(g, int) and j == 0):
                    pe.wait_ge(y_done, j)
                for k in range(HC):
                    if k % 2 == 0:
                        pe.wait_ge(h_lo, NQ * j + k // 2 + 1)
                    for part in range(MS):
                        bank = 5 if part else 4
                        rs = slice(part * P, (part + 1) * P)
                        mm = three(ps[:, bank, 0:D], hh[:, k, rs], hl[:, k, rs], w2h[:, u, k, :], w2l[:, u, k, :],
                                   k == 0, k == HC - 1)
                mm.then_inc(down_mm, 1)

            tiles(pe, body)

        @block.scalar
        def _(act):
            def split(g, u, q):
                c, half = q // 2, q % 2
                at = (slice(None), u, c, slice(half * H // 2, (half + 1) * H // 2))
                act.activation(w1h[at], w1raw[at], ACT.Copy).then_inc(w1_hi, 1)

            def turned_hi(g, u):
                act.wait_ge(rows_turned, 2 * g + u + 1)
                act.activation(xTh[:, :, :], ps[:, 6, :].rearrange("p (c m) -> p c m", c=DC), ACT.Copy
                               ).then_inc(xT_hi, 1)

            turned_hi(0, 0)
            act.wait_ge(w1_loaded[0], 16)
            for q in range(NQ):
                split(0, 0, q)

            def body(g, u):
                j = 2 * g + u
                e = expert_of(act, g, u)
                ng, nu = following(g, u)
                for q in range(NQ):
                    act.wait_ge(up_mm, NQ * j + q + 1)
                    for k in (2 * q, 2 * q + 1):
                        op = act.activation(h32[:, k, :], ps[:, q, (k % 2) * M:(k % 2 + 1) * M], ACT.Relu,
                                            bias=s.b1T[:, ds(e * HC + k, 1)])
                    op.then_inc(relu_done, 1)
                    act.wait_ge(relu_done, NQ * j + q + 1)
                    act.activation(hh[:, 2 * q:2 * q + 2, :], h32[:, 2 * q:2 * q + 2, :], ACT.Copy).then_inc(h_hi, 1)
                    if not is_last(g, u):
                        if q == 0:
                            act.wait_ge(w1_loaded[nu], 16 * ng + 16)
                        split(ng, nu, q)
                if not is_last(g, u):
                    turned_hi(ng, nu)

            tiles(act, body)

        @block.vector
        def _(dve):
            V = nc.vector

            def split1(g, u, q):
                dve.wait_ge(w1_hi, NQ * (2 * g + u) + q + 1)
                c, half = q // 2, q % 2
                at = (slice(None), u, c, slice(half * H // 2, (half + 1) * H // 2))
                V.tensor_tensor(w1l[at], w1raw[at], w1h[at].bitcast(F32), ALU.subtract).then_inc(w1_lo, 1)

            def split2(g, u, q):
                dve.wait_ge(w2_hi, NQ * (2 * g + u) + q + 1)
                at = (slice(None), u, slice(2 * q, 2 * q + 2), slice(None))
                V.tensor_tensor(w2l[at], w2raw[at], w2h[at].bitcast(F32), ALU.subtract).then_inc(w2_lo, 1)

            def turned_lo(g, u):
                dve.wait_ge(xT_hi, 2 * g + u + 1)
                V.tensor_tensor(xTl[:, :, :], ps[:, 6, :].rearrange("p (c m) -> p c m", c=DC),
                                xTh[:, :, :].bitcast(F32), ALU.subtract).then_inc(xT_lo, 1)

            turned_lo(0, 0)
            for q in range(NQ):
                split1(0, 0, q)
            for q in range(NQ):
                split2(0, 0, q)
            dve.wait_ge(b2_loaded, 16)

            def body(g, u):
                j = 2 * g + u
                e = expert_of(dve, g, u)
                ng, nu = following(g, u)
                for q in range(NQ):
                    dve.wait_ge(h_hi, NQ * j + q + 1)
                    at = (slice(None), slice(2 * q, 2 * q + 2), slice(None))
                    V.tensor_tensor(hl[at], h32[at], hh[at].bitcast(F32), ALU.subtract).then_inc(h_lo, 1)
                    if not is_last(g, u):
                        split1(ng, nu, q)
                        split2(ng, nu, q)
                if not is_last(g, u):
                    turned_lo(ng, nu)
                dve.wait_ge(down_mm, j + 1)
                if not first(g):
                    dve.wait_ge(y_stored[u], 16 * g)
                for part in range(MS):
                    op = V.tensor_tensor(y[:, u, part, :], ps[:, 4 + part, 0:D], b2all[:, ds(e * D, D)], ALU.add)
                op.then_inc(y_done, 1)

            tiles(dve, body)


def combine_and_layer1(nc, s, expert_out, W_qkv, W_out, W_r, W_k, W_v, mu_r, mu_k, rope_cos, rope_sin, out):
    B, BT, D, DC, T, K = s.B, s.BT, s.D, s.DC, s.T, s.K
    HD = rope_cos.shape[1]
    HP = P // HD
    NG = BT // 2
    LOADS = 2 + 3 + 2 * DC + 2
    HB = T // 2
    ps = s.ps
    with ExitStack() as ctx:
        def sb(name, shape, dt=F32):
            return ctx.enter_context(nc.sbuf_tensor(name, shape, dt))

        def sem(name):
            return ctx.enter_context(nc.semaphore(name))

        picked_rows, slot_now = sb("picked_rows", [P, 4, K, D]), sb("slot_again", [P, 4, K], U32)
        stats, mv = sb("stats1", [P, BT, 6]), sb("mv1", [P, BT, 2])
        std, rstd, shift = sb("std1", [P, BT]), sb("rstd1", [P, BT]), sb("shift1", [P, BT])
        xn = sb("xn1", [P, BT, D])
        xnT = sb("xnT1", [P, DC, T + 1])
        step_T = sb("step_T", [P, DC, T])
        xrT, xkT = sb("xrT", [P, DC, T]), sb("xkT", [P, DC, T])
        qk, rot, straight = sb("qk", [P, 2, 2, 2 * D]), sb("rot", [P, 2, 2, 2 * D]), sb("straight", [P, 2, 2, 2 * D])
        feat = sb("feat", [P, BT, 2 * D])
        v1 = sb("v1", [P, BT, DC, P + 1])
        qT, oT, act_k = sb("qT", [P, DC, T]), sb("oT", [P, DC, T]), sb("act_k", [P, DC, T])
        gate = sb("gate", [P, BT, D])
        kv, ksum = sb("kv", [P, DC, P]), sb("ksum", [P, DC, P])
        same_head = sb("same_head", [P, P])
        wqkv, wout = sb("wqkv", [P, DC, 3 * D]), sb("wout", [P, DC, D])
        wraw, wT = sb("wraw", [P, 3, DC, D]), sb("wT", [P, 3, DC, D])
        mu = sb("mu", [P, 2, DC])
        cos, sin = sb("cos", [P, BT, HD]), sb("sin", [P, BT, HD])
        den = sb("den", [P, 2, HB])

        loaded, const_ready, weights_turned, weights_ready, passed = (sem(n) for n in (
            "loaded", "const_ready1", "weights_turned", "weights_ready", "passed1"))
        slot_staged, first_added, combined = sem("slot_staged1"), sem("first_added"), sem("combined")
        gathered = [sem(f"gathered{u}") for u in range(4)]
        stats_done, mv_done, std_done, rstd_done, shift_done, xn_ready = (sem(n) for n in (
            "stats_done1", "mv_done1", "std_done1", "rstd_done1", "shift_done1", "xn_ready1"))
        turned, xnT_ready, step_ready, mixed = sem("turned1"), sem("xnT_ready1"), sem("step_ready"), sem("mixed")
        qkv_mm, qkv_out, rotated, straight_done, summed, clipped, exp_done, feat_done = (sem(n) for n in (
            "qkv_mm", "qkv_out", "rotated", "straight_done", "summed", "clipped", "exp_done1", "feat_done"))
        k_mm, k_out, squared, r_mm, gate_ready = (sem(n) for n in ("k_mm", "k_out", "squared", "r_mm", "gate_ready"))
        qT_mm, qT_ready, kv_mm, kv_ready, v_mm, gated = (sem(n) for n in (
            "qT_mm", "qT_ready", "kv_mm", "kv_ready", "v_mm", "gated"))
        nd_mm, den_clipped, den_inv, oT_ready = (sem(n) for n in ("nd_mm", "den_clipped", "den_inv", "oT_ready"))
        out_mm, out_added, final, stored = (sem(n) for n in ("out_mm", "out_added", "final", "stored"))

        def x_tile(t, n=1):
            return s.x_acc[:, ds(t * D, n * D)]

        def pair_of_tiles(bank):
            return bank.rearrange("p (j d) -> p j d", j=2)

        def sequences(eng, body):
            with eng.Fori(0, B - 1) as b:
                body(b, False)
            body(B - 1, True)

        block = ctx.enter_context(nc.Block())

        @block.sync
        def _(sp):
            def feature_rows(w):
                return w.rearrange("(c p) e -> p c e", p=P)

            sp.dma_start(wqkv[:, :, :], feature_rows(W_qkv)).then_inc(loaded, 16)
            sp.dma_start(wout[:, :, :], feature_rows(W_out)).then_inc(loaded, 16)
            for n, w in enumerate((W_r, W_k, W_v)):
                sp.dma_start(wraw[:, n], feature_rows(w)).then_inc(loaded, 16)
            for n, m in enumerate((mu_r, mu_k)):
                for c in range(DC):
                    sp.dma_start(mu[:, n, c:c + 1], m[c * P:(c + 1) * P].rearrange("(p a) -> p a", a=1)
                                 ).then_inc(loaded, 16)
            sp.dma_start(cos[:, :, :], rope_cos.rearrange("(i p) f -> p i f", p=P)).then_inc(loaded, 16)
            sp.dma_start(sin[:, :, :], rope_sin.rearrange("(i p) f -> p i f", p=P)).then_inc(loaded, 16)
            with sp.Fori(0, B) as b:
                sp.wait_ge(final, NG * b + NG)
                sp.dma_start(out.rearrange("b (i p) d -> b p i d", p=P)[b],
                             x_tile(b * BT, BT).rearrange("p (i d) -> p i d", d=D)).then_inc(stored, 16)
            sp.wait_ge(stored, 16 * B)

        @block.gpsimd
        def _(pool):
            pool.memset(same_head[:, :], 1.0).then_inc(const_ready, 1)
            pool.memset(xnT[:, :, 0:1], 0.0).then_inc(const_ready, 1)
            pool.memset(v1[:, :, :, P:P + 1], 1.0).then_inc(const_ready, 1)
            heads = same_head[:, :].rearrange("p (h f) -> p h f", f=HD)
            pool.wait_ge(const_ready, 3)
            pool.affine_select(out=heads, in_=heads, compare_op=ALU.is_ge, fill=0.0, base=0,
                               pattern=[[-HD, HP], [0, HD]], channel_multiplier=1).then_inc(const_ready, 1)
            pool.wait_ge(const_ready, 4)
            pool.affine_select(out=heads, in_=heads, compare_op=ALU.is_gt, fill=0.0, base=HD,
                               pattern=[[HD, HP], [0, HD]], channel_multiplier=-1).then_inc(const_ready, 1)

            def gather(b):
                for i in range(BT):
                    t, u = b * BT + i, i % 4
                    if not (isinstance(b, int) and b == 0 and i < 4):
                        hold(pool, combined, 2 * b + i // 4, passed)
                    pool.tensor_copy(slot_now[:, u, :], s.slots[:, ds(K * t, K)]).then_inc(slot_staged, 1)
                    hold(pool, slot_staged, t + 1, passed)
                    for k in range(K):
                        pool.indirect_dma_start(out=picked_rows[:, u, k, :], out_offset=None, in_=expert_out,
                                                in_offset=bass.IndirectOffsetOnAxis(ap=slot_now[:, u, k:k + 1], axis=0)
                                                ).then_inc(gathered[u], 16)

            gather(0)

            def body(b, last):
                hold(pool, xnT_ready, 4 * b + 4, passed)
                pool.tensor_tensor(step_T[:, :, :], xnT[:, :, 1:T + 1], xnT[:, :, 0:T], ALU.subtract
                                   ).then_inc(step_ready, 1)
                for n in range(NG):
                    hold(pool, qkv_out, NG * b + n + 1, passed)
                    src = qk[:, n % 2].rearrange("p j (h f) -> p j h f", f=HD)
                    dst = rot[:, n % 2].rearrange("p j (h f) -> p j h f", f=HD)
                    for half in range(2):
                        to = slice(half * HD // 2, (half + 1) * HD // 2)
                        fro = slice((1 - half) * HD // 2, (2 - half) * HD // 2)
                        table = sin[:, 2 * n:2 * n + 2, to].unsqueeze(2).to_broadcast([P, 2, 2 * D // HD, HD // 2])
                        op = pool.tensor_tensor(dst[:, :, :, to], src[:, :, :, fro], table, ALU.mult)
                    op.then_inc(rotated, 1)
                if not last:
                    gather(b + 1)
                for n in range(NG):
                    hold(pool, out_added, NG * b + n + 1 + NG, passed)
                    pool.tensor_tensor(x_tile(b * BT + 2 * n, 2), x_tile(b * BT + 2 * n, 2),
                                       gate[:, 2 * n:2 * n + 2, :].rearrange("p j d -> p (j d)"), ALU.add
                                       ).then_inc(final, 1)

            pool.wait_ge(loaded, 16 * LOADS)
            sequences(pool, body)

        @block.tensor
        def _(pe):
            pe.wait_ge(loaded, 16 * LOADS)
            for n in range(3):
                for c in range(DC):
                    for d in range(DC):
                        mm = pe.transpose(ps[:, 4 + n, c * D + d * P:c * D + (d + 1) * P],
                                          wraw[:, n, d, c * P:(c + 1) * P], s.ident[:, :])
            mm.then_inc(weights_turned, 1)
            pe.wait_ge(weights_ready, 1)

            def turn(b):
                hold(pe, xn_ready, b + 1, passed)
                for q in range(4):
                    c, half = q // 2, q % 2
                    for i in range(4):
                        mm = pe.transpose(ps[:, q, i * P:(i + 1) * P], xn[:, half * 4 + i, c * P:(c + 1) * P],
                                          s.ident[:, :])
                    mm.then_inc(turned, 1)

            def product(dst, lhsT, rhs):
                pe.matmul(dst, lhsT(0), rhs(0), start=True, stop=False)
                return pe.matmul(dst, lhsT(1), rhs(1), start=False, stop=True)

            def tile_of(i):
                return slice(i * P, (i + 1) * P)

            def half_of(h):
                return slice(h * HB, (h + 1) * HB)

            def body(b, last):
                pe.wait_ge(out_added, NG * b + NG)
                pe.wait_ge(xnT_ready, 4 * b + 4)
                for n in range(NG):
                    if n >= 2:
                        pe.wait_ge(qkv_out, NG * b + n - 1)
                    for j in range(2):
                        i = 2 * n + j

                        def lhsT(c, i=i):
                            return xnT[:, c, 1 + i * P:1 + (i + 1) * P]

                        product(ps[:, (4 + 3 * n + j) % 8, :], lhsT, lambda c: wqkv[:, c, 0:2 * D])
                        mm = product(ps[:, (6 + 3 * n) % 8, j * D:(j + 1) * D], lhsT,
                                     lambda c: wqkv[:, c, 2 * D:3 * D])
                    mm.then_inc(qkv_mm, 1)
                pe.wait_ge(mixed, b + 1)
                pe.wait_ge(qkv_out, NG * b + 3)
                for n in range(4):
                    m, h = n // 2, n % 2
                    product(ps[:, n, :], lambda c: wT[:, 1, c, tile_of(m)], lambda c: xkT[:, c, half_of(h)]
                            ).then_inc(k_mm, 1)
                pe.wait_ge(qkv_out, NG * b + 4)
                for n in range(NG):
                    for j in range(2):
                        mm = product(ps[:, 4 + n, j * D:(j + 1) * D], lambda c: xrT[:, c, tile_of(2 * n + j)],
                                     lambda c: wT[:, 0, c, :])
                    mm.then_inc(r_mm, 1)
                pe.wait_ge(feat_done, NG * b + NG + 2)
                pe.wait_ge(k_out, 4 * b + 4)
                for n in range(4):
                    c, h = n // 2, n % 2
                    for i in range(4):
                        mm = pe.transpose(ps[:, n, tile_of(i)], feat[:, 4 * h + i, tile_of(c)], s.ident[:, :])
                    mm.then_inc(qT_mm, 1)
                pe.wait_ge(gate_ready, NG * b + 2)
                for c in range(DC):
                    for i in range(BT):
                        mm = pe.matmul(ps[:, 4 + c, 0:P + 1], feat[:, i, D + c * P:D + (c + 1) * P], v1[:, i, c, :],
                                       start=(i == 0), stop=(i == BT - 1))
                mm.then_inc(kv_mm, 1)
                pe.wait_ge(squared, 4 * b + 4)
                pe.wait_ge(gate_ready, NG * b + NG)
                for n in range(NG):
                    if n == 2:
                        pe.wait_ge(qT_ready, 4 * b + 2)
                    for j in range(2):
                        mm = product(ps[:, (6 + n) % 8, j * D:(j + 1) * D], lambda c: act_k[:, c, tile_of(2 * n + j)],
                                     lambda c: wT[:, 2, c, :])
                    mm.then_inc(v_mm, 1)
                pe.wait_ge(qT_ready, 4 * b + 4)
                pe.wait_ge(kv_ready, b + 1)
                for n in range(4):
                    h, c = n // 2, n % 2
                    if n >= 2:
                        pe.wait_ge(gated, NG * b + 2 * (n - 1))
                    pe.matmul(ps[:, (2 + 2 * n) % 8, :], kv[:, c, :], qT[:, c, half_of(h)], start=True, stop=True)
                    pe.matmul(ps[:, (3 + 2 * n) % 8, :], ksum[:, c, :], qT[:, c, half_of(h)], start=True, stop=True
                              ).then_inc(nd_mm, 1)
                for n in range(NG):
                    pe.wait_ge(oT_ready, 4 * b + (2 if n < 2 else 4))
                    for j in range(2):
                        mm = product(ps[:, 4 + n, j * D:(j + 1) * D], lambda c: oT[:, c, tile_of(2 * n + j)],
                                     lambda c: wout[:, c, :])
                    mm.then_inc(out_mm, 1)
                if not last:
                    turn(b + 1)

            turn(0)
            sequences(pe, body)

        @block.scalar
        def _(act):
            act.wait_ge(weights_turned, 1)
            act.activation(wT[:, :, :, :].rearrange("p n c d -> p n (c d)"), ps[:, 4:7, :], ACT.Copy
                           ).then_inc(weights_ready, 1)
            act.wait_ge(const_ready, 5)

            def normed(b):
                act.wait_ge(mv_done, b + 1)
                act.activation(std[:, :], mv[:, :, 1], ACT.Sqrt, bias=s.eps[:, 0:1]).then_inc(std_done, 1)
                act.wait_ge(shift_done, b + 1)
                for i in range(BT):
                    op = act.activation(xn[:, i, :], x_tile(b * BT + i), ACT.Identity, bias=shift[:, i:i + 1],
                                        scale=rstd[:, i:i + 1])
                op.then_inc(xn_ready, 1)

            def turned_out(b):
                for q in range(4):
                    act.wait_ge(turned, 4 * b + q + 1)
                    c, h = q // 2, q % 2
                    act.activation(xnT[:, c, 1 + h * HB:1 + (h + 1) * HB], ps[:, q, :], ACT.Copy
                                   ).then_inc(xnT_ready, 1)

            normed(0)
            turned_out(0)

            def body(b, last):
                def features(n):
                    act.wait_ge(clipped, NG * b + n + 1)
                    act.activation(qk[:, n % 2], qk[:, n % 2], ACT.Exp).then_inc(exp_done, 1)

                for n in range(NG):
                    act.wait_ge(qkv_mm, NG * b + n + 1)
                    act.wait_ge(feat_done, NG * b + n + 1)
                    for j in range(2):
                        bank = ps[:, (4 + 3 * n + j) % 8, :]
                        act.activation(qk[:, n % 2, j, 0:D], bank[:, 0:D], ACT.Copy, scale=HD ** -0.5)
                        act.activation(qk[:, n % 2, j, D:2 * D], bank[:, D:2 * D], ACT.Copy)
                    act.activation(v1[:, 2 * n:2 * n + 2, :, 0:P],
                                   ps[:, (6 + 3 * n) % 8, :].rearrange("p (j c f) -> p j c f", j=2, c=DC), ACT.Copy
                                   ).then_inc(qkv_out, 1)
                    if n > 0:
                        features(n - 1)
                features(NG - 1)
                for n in range(4):
                    act.wait_ge(k_mm, 4 * b + n + 1)
                    m, h = n // 2, n % 2
                    act.activation(act_k[:, m, h * HB:(h + 1) * HB], ps[:, n, :], ACT.Relu).then_inc(k_out, 1)
                act.wait_ge(rotated, NG * b + NG)
                for n in range(NG):
                    act.wait_ge(r_mm, NG * b + n + 1)
                    act.activation(gate[:, 2 * n:2 * n + 2, :], pair_of_tiles(ps[:, 4 + n, :]), ACT.Sigmoid
                                   ).then_inc(gate_ready, 1)
                for n in range(4):
                    act.wait_ge(qT_mm, 4 * b + n + 1)
                    c, h = n // 2, n % 2
                    act.activation(qT[:, c, h * HB:(h + 1) * HB], ps[:, n, :], ACT.Copy).then_inc(qT_ready, 1)
                if not last:
                    normed(b + 1)
                    act.wait_ge(mixed, b + 1)
                    turned_out(b + 1)

            sequences(act, body)

        @block.vector
        def _(dve):
            V = nc.vector
            dve.sem_inc(feat_done, 2)
            dve.sem_inc(out_added, NG)
            dve.wait_ge(loaded, 16 * LOADS)
            dve.wait_ge(const_ready, 5)

            def combine(b):
                for h in range(2):
                    for k in range(K):
                        for u in range(4):
                            t = b * BT + 4 * h + u
                            if k == 0:
                                dve.wait_ge(gathered[u], 32 * (2 * b + h + 1))
                            op = V.scalar_tensor_tensor(x_tile(t), picked_rows[:, u, k, :],
                                                        s.gates[:, ds(K * t + k, 1)], x_tile(t), ALU.mult, ALU.add)
                        if k == 0:
                            op.then_inc(first_added, 1)
                            dve.wait_ge(first_added, 2 * b + h + 1)
                    op.then_inc(combined, 1)
                hold(dve, combined, 2 * b + 2, passed)
                for i in range(BT):
                    op = V.bn_stats(stats[:, i, :], x_tile(b * BT + i))
                op.then_inc(stats_done, 1)
                hold(dve, stats_done, b + 1, passed)
                for i in range(BT):
                    op = V.bn_aggr(mv[:, i, :], stats[:, i, :])
                op.then_inc(mv_done, 1)
                dve.wait_ge(std_done, b + 1)
                V.reciprocal(rstd[:, :], std[:, :]).then_inc(rstd_done, 1)
                dve.wait_ge(rstd_done, b + 1)
                V.scalar_tensor_tensor(shift[:, :], mv[:, :, 0], -1.0, rstd[:, :], ALU.mult, ALU.mult
                                       ).then_inc(shift_done, 1)

            combine(0)

            def body(b, last):
                dve.wait_ge(step_ready, b + 1)
                for n, dst in enumerate((xrT, xkT)):
                    for c in range(DC):
                        op = V.scalar_tensor_tensor(dst[:, c, :], step_T[:, c, :], mu[:, n, c:c + 1], xnT[:, c, 0:T],
                                                    ALU.mult, ALU.add)
                op.then_inc(mixed, 1)
                for n in range(NG):
                    dve.wait_ge(qkv_out, NG * b + n + 1)
                    a = straight[:, n % 2]
                    V.tensor_tensor(a.rearrange("p j (h f) -> p j h f", f=HD),
                                    qk[:, n % 2].rearrange("p j (h f) -> p j h f", f=HD),
                                    cos[:, 2 * n:2 * n + 2, :].unsqueeze(2).to_broadcast([P, 2, 2 * D // HD, HD]),
                                    ALU.mult).then_inc(straight_done, 1)
                    dve.wait_ge(straight_done, NG * b + n + 1)
                    dve.wait_ge(rotated, NG * b + n + 1)
                    V.tensor_tensor(a, a, rot[:, n % 2], ALU.add).then_inc(summed, 1)
                    dve.wait_ge(summed, NG * b + n + 1)
                    V.tensor_scalar(qk[:, n % 2], a, 0.0, None, ALU.min).then_inc(clipped, 1)
                    dve.wait_ge(exp_done, NG * b + n + 1)
                    V.scalar_tensor_tensor(feat[:, 2 * n:2 * n + 2, :], a, 0.0, qk[:, n % 2], ALU.max, ALU.add
                                           ).then_inc(feat_done, 1)
                for n in range(4):
                    dve.wait_ge(k_out, 4 * b + n + 1)
                    m, h = n // 2, n % 2
                    at = act_k[:, m, h * HB:(h + 1) * HB]
                    V.tensor_tensor(at, at, at, ALU.mult).then_inc(squared, 1)
                dve.wait_ge(kv_mm, b + 1)
                for c in range(DC):
                    V.tensor_tensor(kv[:, c, :], ps[:, 4 + c, 0:P], same_head[:, :], ALU.mult)
                    op = V.tensor_scalar(ksum[:, c, :], same_head[:, :], ps[:, 4 + c, P:P + 1], None, ALU.mult)
                op.then_inc(kv_ready, 1)
                for n in range(NG):
                    dve.wait_ge(v_mm, NG * b + n + 1)
                    at = gate[:, 2 * n:2 * n + 2, :]
                    V.tensor_tensor(at, pair_of_tiles(ps[:, (6 + n) % 8, :]), at, ALU.mult).then_inc(gated, 1)
                for n in range(4):
                    h, c = n // 2, n % 2
                    dve.wait_ge(nd_mm, 4 * b + n + 1)
                    V.tensor_scalar(den[:, n % 2], ps[:, (3 + 2 * n) % 8, :], 1e-6, None, ALU.max
                                    ).then_inc(den_clipped, 1)
                    dve.wait_ge(den_clipped, 4 * b + n + 1)
                    V.reciprocal(den[:, n % 2], den[:, n % 2]).then_inc(den_inv, 1)
                    dve.wait_ge(den_inv, 4 * b + n + 1)
                    V.tensor_tensor(oT[:, c, h * HB:(h + 1) * HB], ps[:, (2 + 2 * n) % 8, :], den[:, n % 2], ALU.mult
                                    ).then_inc(oT_ready, 1)
                if not last:
                    combine(b + 1)
                for n in range(NG):
                    dve.wait_ge(out_mm, NG * b + n + 1)
                    V.tensor_tensor(x_tile(b * BT + 2 * n, 2), x_tile(b * BT + 2 * n, 2), ps[:, 4 + n, :], ALU.add
                                    ).then_inc(out_added, 1)

            sequences(dve, body)


def build(nc, t, out):
    s = Shapes(t["L0_attn_x"], t["L0_ffn_W1"])
    xn_rows = nc.dram_tensor("xn_rows", [s.N, s.D], F32, kind="Internal").ap()
    dispatched = nc.dram_tensor("dispatched", [s.MT * s.M, s.D], F32, kind="Internal").ap()
    expert_out = nc.dram_tensor("expert_out", [s.MT * s.M, s.D], F32, kind="Internal").ap()
    with ExitStack() as ctx:
        s.ctx = ctx
        constants(nc, s)
        norm_route_attend(nc, s, t["L0_attn_x"], t["L0_attn_Wq"], t["L0_attn_Wk"], t["L0_attn_Wv"],
                          t["L0_ffn_Wr"], t["L0_ffn_br"], t["L0_ffn_b1"], xn_rows, dispatched)
        experts(nc, s, t["L0_ffn_W1"], t["L0_ffn_W2"], t["L0_ffn_b2"], dispatched, expert_out)
        combine_and_layer1(nc, s, expert_out, t["L1_attn_W_qkv"], t["L1_attn_W_out"], t["L1_ffn_W_r"],
                           t["L1_ffn_W_k"], t["L1_ffn_W_v"], t["L1_ffn_mu_r"], t["L1_ffn_mu_k"],
                           t["rope_cos"], t["rope_sin"], out)


_INS = ["L0_attn_x", "L0_attn_Wq", "L0_attn_Wk", "L0_attn_Wv", "L0_ffn_Wr", "L0_ffn_br", "L0_ffn_W1", "L0_ffn_b1",
        "L0_ffn_W2", "L0_ffn_b2", "L1_attn_W_qkv", "L1_attn_W_out", "L1_ffn_W_r", "L1_ffn_W_k", "L1_ffn_W_v",
        "L1_ffn_mu_r", "L1_ffn_mu_k"]
_HEADS, _ROPE_BASE = 16, 500000.0


def _rope_tables(T, D):
    import numpy as _np

    hd = D // _HEADS
    inv = (_np.float32(1.0) / _np.float32(_ROPE_BASE) ** (_np.arange(0, hd, 2, dtype=_np.float32) / _np.float32(hd)))
    freqs = (_np.arange(T, dtype=_np.float32)[:, None] * inv.astype(_np.float32)[None, :]).astype(_np.float32)
    cos, sin = _np.cos(freqs), _np.sin(freqs)
    return (_np.concatenate([cos, cos], axis=1).astype(_np.float32),
            _np.concatenate([-sin, sin], axis=1).astype(_np.float32))


def kernel(**inputs):
    import numpy as _np
    import concourse.bacc as _bacc
    from concourse.bass_utils import run_bass_kernel_spmd as _run

    nc = _bacc.Bacc("TRN2", target_bir_lowering=False, num_devices=1)
    _, T, D = inputs["L0_attn_x"].shape
    cos, sin = _rope_tables(T, D)
    arrays, args = {}, {}
    for name, a in [(n, inputs[n]) for n in _INS] + [("rope_cos", cos), ("rope_sin", sin)]:
        a = _np.ascontiguousarray(a)
        arrays[f"in_{name}"] = a
        args[name] = nc.dram_tensor(f"in_{name}", a.shape, mybir.dt.from_np(a.dtype), kind="ExternalInput").ap()
    out = nc.dram_tensor("out", inputs["L0_attn_x"].shape, F32, kind="ExternalOutput").ap()
    build(nc, args, out)
    r = _run(nc, [arrays], core_ids=[0])
    return r.results[0]["out"]
```

```python
from contextlib import ExitStack

import concourse.bass as bass
from concourse import mybir

F32 = mybir.dt.float32
F32R = mybir.dt.float32r
BF16 = mybir.dt.bfloat16
I32 = mybir.dt.int32
U32 = mybir.dt.uint32
ALU = mybir.AluOpType
ACT = mybir.ActivationFunctionType
X = mybir.AxisListType.X
ds = bass.ds

P = 128
EPS = 1e-5
MASKED = -1e30


def hold(eng, semaphore, value, passed):
    eng.wait_ge(semaphore, value)
    eng.sem_inc(passed, 1)


class Shapes:

    def __init__(self, x, W1):
        self.B, self.T, self.D = x.shape
        self.E, _, self.H = W1.shape
        self.N = self.B * self.T
        self.DC = self.D // P
        self.HC = self.H // P
        self.BT = self.T // P
        self.NT = self.N // P
        self.K = 2
        self.M = 256
        self.MT = (self.K * self.N + self.E * (self.M - 1)) // self.M
        assert self.DC == 2 and self.B == 4 and self.MT % 2 == 1


def constants(nc, s):
    ctx = s.ctx

    def sb(name, shape, dt=F32):
        return ctx.enter_context(nc.sbuf_tensor(name, shape, dt))

    s.x_acc = sb("x_acc", [P, s.NT * s.D])
    s.ident = sb("ident", [P, P])
    s.slots = sb("slots", [P, s.NT * s.K], U32)
    s.gates = sb("gates", [P, s.NT * s.K])
    s.tile_expert = sb("tile_expert", [P, s.MT + 1], I32)
    s.b1T = sb("b1T", [P, s.E * s.HC])
    s.eps = sb("eps", [P, 1])
    s.raw = sb("raw", [P, (s.DC * s.H + s.HC * s.D)])
    s.raw_loaded = [ctx.enter_context(nc.semaphore(f"raw_loaded{n}")) for n in range(2)]
    s.ps = ctx.enter_context(nc.psum_tensor("ps", [P, 8, 512], F32))


def load_weights(sp, s, W1, W2, e, raw, loaded):
    n = s.DC * s.H
    sp.dma_start(raw[:, 0:n].rearrange("p (c h) -> p c h", c=s.DC),
                 W1.rearrange("e (c p) h -> e p c h", p=P)[e]).then_inc(loaded[0], 16)
    sp.dma_start(raw[:, n:].rearrange("p (k d) -> p k d", k=s.HC),
                 W2.rearrange("e (k p) d -> e p k d", p=P)[e]).then_inc(loaded[1], 16)


def norm_route_attend(nc, s, x, Wq, Wk, Wv, Wr, br, b1, W1, W2, xn_rows, dispatched):
    B, BT, NT, D, DC, E, K, T, M, MT = s.B, s.BT, s.NT, s.D, s.DC, s.E, s.K, s.T, s.M, s.MT
    ps = s.ps
    with ExitStack() as ctx:
        def sb(name, shape, dt=F32):
            return ctx.enter_context(nc.sbuf_tensor(name, shape, dt))

        def sem(name):
            return ctx.enter_context(nc.semaphore(name))

        xnT = sb("xnT", [P, DC, s.N])
        xn = s.raw[:, :].rearrange("p (u i d) -> p u i d", u=2, i=BT)
        xh, xl = sb("xh", [P, DC, T], F32R), sb("xl", [P, DC, T], F32R)
        qkh, qkl = sb("qkh", [P, 2, DC, T], F32R), sb("qkl", [P, 2, DC, T], F32R)
        vh, vl = sb("vh", [P, BT, D], F32R), sb("vl", [P, BT, D], F32R)
        wh, wl = sb("wh", [P, 3, DC, D], F32R), sb("wl", [P, 3, DC, D], F32R)
        prob = sb("prob", [P, 2, T])
        pTh, pTl = sb("pTh", [P, 2, BT, P], F32R), sb("pTl", [P, 2, BT, P], F32R)
        row_sum, row_inv, neg_max = sb("row_sum", [P, BT]), sb("row_inv", [P, BT]), sb("neg_max", [P, BT])
        ident_b, above = sb("ident_b", [P, P], BF16), sb("above", [P, P], BF16)
        w3 = sb("w3", [P, 3, DC, D])
        earlier, ones = sb("earlier", [P, P]), sb("ones", [P, P])
        zero = sb("zero", [P, D])
        wr, brc = sb("wr", [P, DC, E]), sb("brc", [E, 1])
        lgT = sb("lgT", [E, 2, T])
        stats, mv = sb("stats", [P, NT, 6]), sb("mv", [P, NT, 2])
        std, rstd = sb("std", [P, NT]), sb("rstd", [P, NT])
        b1r = sb("b1r", [E * s.HC, P])
        logits = sb("logits", [P, NT * E])
        R = [s.raw[:, n * NT * E:(n + 1) * NT * E].rearrange("p (t e) -> p t e", e=E) for n in range(10)]
        col = sb("col", [P, 8, NT])
        expert_row = sb("expert_row", [P, 6, E])
        expert_int = sb("expert_int", [P, E], I32)
        rank8, tile_no = sb("rank8", [P, E]), sb("tile_no", [P, MT + 1])
        cmp = sb("cmp", [P, MT + 1, E - 1])
        cnt = sb("cnt", [P, MT + 1])
        xrow, slot_now = sb("xrow", [P, 4, D]), sb("slot_now", [P, 4, K], U32)

        x_loaded = [sem(f"x_loaded{b}") for b in range(B)]
        w_loaded, small_loaded = sem("w_loaded"), sem("small_loaded")
        const_ready, zero_ready, zero_filled = sem("const_ready"), sem("zero_ready"), sem("zero_filled")
        wh_ready, wl_ready = sem("wh_ready"), sem("wl_ready")
        b1_turned, b1_ready = sem("b1_turned"), sem("b1_ready")
        stats_done, mv_done, std_done, rstd_done, xn_ready = (sem(n) for n in (
            "stats_done", "mv_done", "std_done", "rstd_done", "xn_ready"))
        xn_stored = [sem(f"xn_stored{u}") for u in range(2)]
        turned, xnT_ready, lgT_mm, lgT_ready, lg_turned, lg_ready = (sem(n) for n in (
            "turned", "xnT_ready", "lgT_mm", "lgT_ready", "lg_turned", "lg_ready"))
        step, passed = sem("step"), sem("passed")
        centered, exp_done, picked, counted, routed = (sem(n) for n in (
            "centered", "exp_done", "picked", "counted", "routed"))
        row_loaded = [sem(f"row_loaded{u}") for u in range(4)]
        slot_staged = sem("slot_staged")
        scattered = [sem(f"scattered{u}") for u in range(4)]
        xh_ready, xl_ready, proj_mm, proj_hi, proj_lo = (sem(n) for n in (
            "xh_ready", "xl_ready", "proj_mm", "proj_hi", "proj_lo"))
        score_mm, max_done, prob_ready, prob_turned, pT_hi, pT_lo, pv_mm, inv_done, attended = (sem(n) for n in (
            "score_mm", "max_done", "prob_ready", "prob_turned", "pT_hi", "pT_lo", "pv_mm", "inv_done", "attended"))

        def x_tile(t):
            return s.x_acc[:, ds(t * D, D)]

        def sequences(eng, body):
            body(0, True, False)
            with eng.Fori(1, B - 1) as b:
                body(b, False, False)
            body(B - 1, False, True)

        ORDER = (7, 6, 5, 4, 3, 2, 1, 0)
        NPROJ = 2 * DC * (T // 512) + BT // 2
        block = ctx.enter_context(nc.Block())

        @block.sync
        def _(sp):
            xv = x.rearrange("b (i p) d -> b p i d", p=P)
            for b in range(B):
                sp.dma_start(s.x_acc[:, b * BT * D:(b + 1) * BT * D].rearrange("p (i d) -> p i d", d=D),
                             xv[b]).then_inc(x_loaded[b], 16)
                if b == 0:
                    sp.dma_start(wr[:, :, :], Wr.rearrange("(c p) e -> p c e", p=P)).then_inc(small_loaded, 16)
                    sp.dma_start(brc[:, :], br.rearrange("(e a) -> e a", a=1)).then_inc(small_loaded, 16)
                    sp.dma_start(b1r[:, :], b1.rearrange("e (c p) -> (e c) p", p=P)).then_inc(small_loaded, 16)
                    for n, w in enumerate((Wq, Wk, Wv)):
                        sp.dma_start(w3[:, n], w.rearrange("(c p) e -> p c e", p=P)).then_inc(w_loaded, 16)
            for b in range(B):
                sp.wait_ge(xn_ready, b + 1)
                sp.dma_start(xn_rows.rearrange("(b i p) d -> b p i d", b=B, p=P)[b], xn[:, b % 2]
                             ).then_inc(xn_stored[b % 2], 16)
            sp.wait_ge(zero_ready, 1)
            nz = MT * M // P
            sp.dma_start(dispatched.rearrange("(p n) d -> p n d", p=P),
                         zero[:, :].unsqueeze(1).to_broadcast([P, nz, D])).then_inc(zero_filled, 16)
            for u in range(2):
                sp.wait_ge(xn_stored[u], 16 * (B // 2))

            def load_rows(t, u):
                sp.dma_start(xrow[:, u], xn_rows[ds(t * P, P), :]).then_inc(row_loaded[u], 16)

            for u in range(4):
                load_rows(u, u)
            with sp.Fori(1, NT // 4) as g:
                for u in range(4):
                    sp.wait_ge(scattered[u], 16 * K * g)
                    load_rows(4 * g + u, u)
            sp.wait_ge(routed, 1)
            e = sp.value_load(s.tile_expert[0:1, 0:1], min_val=0, max_val=E - 1)
            load_weights(sp, s, W1, W2, e, s.raw, s.raw_loaded)

        @block.gpsimd
        def _(pool):
            pool.memset(zero[:, :], 0.0).then_inc(zero_ready, 1)
            pool.memset(s.ident[:, :], 0.0).then_inc(const_ready, 1)
            pool.memset(ident_b[:, :], 0.0).then_inc(const_ready, 1)
            pool.memset(above[:, :], 0.0).then_inc(const_ready, 1)
            pool.memset(earlier[:, :], 1.0).then_inc(const_ready, 1)
            pool.memset(ones[:, :], 1.0).then_inc(const_ready, 1)
            pool.memset(s.eps[:, :], EPS).then_inc(const_ready, 1)
            pool.iota(tile_no[:, :], [[1, MT + 1]], base=0, channel_multiplier=0,
                      allow_small_or_imprecise_dtypes=True).then_inc(const_ready, 1)
            pool.iota(rank8[:, :], [[-1, E]], base=E, channel_multiplier=0,
                      allow_small_or_imprecise_dtypes=True).then_inc(const_ready, 1)
            pool.wait_ge(const_ready, 8)
            for m in (s.ident, ident_b):
                pool.affine_select(out=m[:, :], in_=m[:, :], compare_op=ALU.not_equal, fill=1.0, base=0,
                                   pattern=[[-1, P]], channel_multiplier=1).then_inc(const_ready, 1)
            pool.affine_select(out=above[:, :], in_=above[:, :], compare_op=ALU.is_ge, fill=MASKED, base=0,
                               pattern=[[-1, P]], channel_multiplier=1).then_inc(const_ready, 1)
            pool.affine_select(out=earlier[:, :], in_=earlier[:, :], compare_op=ALU.is_gt, fill=0.0, base=0,
                               pattern=[[1, P]], channel_multiplier=-1).then_inc(const_ready, 1)

            pool.wait_ge(routed, 1)
            pool.wait_ge(zero_filled, 16)

            def scatter(t, u, turn):
                if turn is not None:
                    hold(pool, scattered[u], 16 * K * turn, passed)
                pool.tensor_copy(slot_now[:, u, :], s.slots[:, ds(K * t, K)]).then_inc(slot_staged, 1)
                hold(pool, slot_staged, t + 1, passed)
                hold(pool, row_loaded[u], 16 if turn is None else 16 * turn + 16, passed)
                for k in range(K):
                    pool.indirect_dma_start(out=dispatched, out_offset=bass.IndirectOffsetOnAxis(
                        ap=slot_now[:, u, k:k + 1], axis=0), in_=xrow[:, u], in_offset=None).then_inc(scattered[u], 16)

            for u in range(4):
                scatter(u, u, None)
            with pool.Fori(1, NT // 4) as g:
                for u in range(4):
                    scatter(4 * g + u, u, g)
            for u in range(4):
                pool.wait_ge(scattered[u], 16 * K * (NT // 4))

        @block.tensor
        def _(pe):
            pe.wait_ge(const_ready, 12)
            pe.wait_ge(small_loaded, 48)
            pe.transpose(ps[:, 7, 0:E * s.HC], b1r[:, :], s.ident[0:E * s.HC, 0:E * s.HC]).then_inc(b1_turned, 1)

            def turn_tokens(b):
                pe.wait_ge(xn_ready, b + 1)
                for q in range(4):
                    c, half = q // 2, q % 2
                    if b > 0:
                        pe.wait_ge(xnT_ready, 4 * b - 3 + q)
                    for i in range(4):
                        mm = pe.transpose(ps[:, q, i * P:(i + 1) * P],
                                          xn[:, b % 2, half * 4 + i, c * P:(c + 1) * P], s.ident[:, :])
                    mm.then_inc(turned, 1)

            def route(b):
                pe.wait_ge(xnT_ready, 4 * b + 4)
                if b > 0:
                    pe.wait_ge(lgT_ready, b)
                for half in range(2):
                    for c in range(DC):
                        at = b * T + half * 512
                        mm = pe.matmul(ps[0:E, 4 + half, :], wr[:, c, :], xnT[:, c, at:at + 512],
                                       start=(c == 0), stop=(c == DC - 1))
                mm.then_inc(lgT_mm, 1)

            def turn_logits(b):
                pe.wait_ge(lgT_ready, b + 1)
                if b > 0:
                    pe.wait_ge(lg_ready, b)
                for i in range(BT):
                    mm = pe.transpose(ps[:, 6, i * E:(i + 1) * E], lgT[:, b % 2, i * P:(i + 1) * P],
                                      s.ident[0:E, 0:E])
                mm.then_inc(lg_turned, 1)

            for n in range(B + 2):
                if n < B:
                    turn_tokens(n)
                if 0 < n <= B:
                    route(n - 1)
                if n > 1:
                    turn_logits(n - 2)

            def three(out, ah, al, bh, bl, start, stop):
                pe.matmul(out, ah, bh, start=start, stop=False, skip_group_check=True)
                pe.matmul(out, ah, bl, start=False, stop=False, skip_group_check=True)
                return pe.matmul(out, al, bh, start=False, stop=stop, skip_group_check=True)

            def project(b, results):
                for n in results:
                    if n >= 4:
                        pe.wait_ge(proj_lo, NPROJ * b + n - 3)
                    bank = ps[:, n % 4, :]
                    if n < 2 * DC * 2:
                        w, m, half = n // 4, n // 2 % 2, n % 2
                        for c in range(DC):
                            mm = three(bank, wh[:, w, c, m * P:(m + 1) * P], wl[:, w, c, m * P:(m + 1) * P],
                                       xh[:, c, half * 512:(half + 1) * 512], xl[:, c, half * 512:(half + 1) * 512],
                                       c == 0, c == DC - 1)
                    else:
                        for j in range(2):
                            i = 2 * (n - 8) + j
                            for c in range(DC):
                                mm = three(bank[:, j * D:(j + 1) * D], xh[:, c, i * P:(i + 1) * P],
                                           xl[:, c, i * P:(i + 1) * P], wh[:, 2, c, :], wl[:, 2, c, :],
                                           c == 0, c == DC - 1)
                    mm.then_inc(proj_mm, 1)

            pe.wait_ge(wl_ready, 1)
            pe.wait_ge(xl_ready, 1)
            project(0, range(NPROJ))
            pe.wait_ge(picked, 1)
            pe.matmul(ps[:, 7, 0:NT * E], earlier[:, :], R[6], start=True, stop=True)
            pe.matmul(ps[:, 6, 0:NT * E], ones[:, :], R[6], start=True, stop=True).then_inc(counted, 1)

            def attend(b, first, last):
                def scores(a):
                    i = ORDER[a]
                    if a < 2:
                        pe.wait_ge(proj_lo, NPROJ * b + 10 + 2 * a)
                    L = (i + 1) * P
                    for h in range((L + 511) // 512):
                        w = min(512, L - 512 * h)
                        bank = ps[:, 2 * (a % 2) + h, 0:w]
                        for c in range(DC):
                            qs, ks = slice(i * P, i * P + P), slice(512 * h, 512 * h + w)
                            mm = three(bank, qkh[:, 0, c, qs], qkl[:, 0, c, qs], qkh[:, 1, c, ks], qkl[:, 1, c, ks],
                                       c == 0, False)
                    mm = pe.matmul(bank[:, w - P:w], ident_b[:, :], above[:, :], start=False, stop=True,
                                   skip_group_check=True)
                    mm.then_inc(score_mm, 1)

                def turn(a):
                    pe.wait_ge(prob_ready, BT * b + a + 1)
                    if a > 0:
                        pe.wait_ge(pT_lo, BT * b + a)
                    for j in range(ORDER[a] + 1):
                        mm = pe.transpose(ps[:, 4 + j // 4, (j % 4) * P:(j % 4 + 1) * P],
                                          prob[:, a % 2, j * P:(j + 1) * P], s.ident[:, :])
                    mm.then_inc(prob_turned, 1)

                def values(a):
                    i = ORDER[a]
                    pe.wait_ge(pT_lo, BT * b + a + 1)
                    pe.wait_ge(attended, BT * b + a + 1)
                    for j in range(i + 1):
                        mm = three(ps[:, 6 + a % 2, 0:D], pTh[:, a % 2, j], pTl[:, a % 2, j], vh[:, j, :], vl[:, j, :],
                                   j == 0, j == i)
                    mm.then_inc(pv_mm, 1)

                scores(0)
                for a in range(BT):
                    if a + 1 < BT:
                        scores(a + 1)
                    turn(a)
                    if 0 < a < BT - 1:
                        values(a - 1)
                if not last:
                    pe.wait_ge(xl_ready, b + 2)
                    project(b + 1, range(8))
                values(BT - 2)
                values(BT - 1)
                if not last:
                    project(b + 1, range(8, NPROJ))

            sequences(pe, attend)

        @block.scalar
        def _(act):
            act.wait_ge(b1_turned, 1)
            act.activation(s.b1T[:, :], ps[:, 7, 0:E * s.HC], ACT.Copy).then_inc(b1_ready, 1)
            act.wait_ge(const_ready, 12)
            act.wait_ge(small_loaded, 48)

            act.wait_ge(w_loaded, 48)
            act.activation(wh[:, :, :, :], w3[:, :, :, :], ACT.Copy).then_inc(wh_ready, 1)

            def deviation(b):
                act.wait_ge(mv_done, b + 1)
                at = slice(b * BT, (b + 1) * BT)
                act.activation(std[:, at], mv[:, at, 1], ACT.Sqrt, bias=s.eps[:, 0:1]).then_inc(std_done, 1)

            deviation(0)
            for n in range(B + 2):
                if n + 1 < B:
                    deviation(n + 1)
                if n < B:
                    for q in range(4):
                        act.wait_ge(turned, 4 * n + q + 1)
                        at = n * T + q % 2 * 512
                        act.activation(xnT[:, q // 2, at:at + 512], ps[:, q, :], ACT.Copy).then_inc(xnT_ready, 1)
                if 0 < n <= B:
                    act.wait_ge(lgT_mm, n)
                    if n > 2:
                        act.wait_ge(lg_turned, n - 2)
                    act.activation(lgT[:, (n - 1) % 2, :], ps[0:E, 4:6, :].rearrange("e h t -> e (h t)"), ACT.Identity,
                                   bias=brc[:, 0:1]).then_inc(lgT_ready, 1)
                if n > 1:
                    act.wait_ge(lg_turned, n - 1)
                    at = (n - 2) * BT * E
                    act.activation(logits[:, at:at + BT * E], ps[:, 6, 0:BT * E], ACT.Copy).then_inc(lg_ready, 1)
                if n == 2:
                    act.activation(xh[:, :, :], xnT[:, :, 0:T], ACT.Copy).then_inc(xh_ready, 1)

            def project_hi(b, results):
                for n in results:
                    act.wait_ge(proj_mm, NPROJ * b + n + 1)
                    if n < 8:
                        act.activation(qkh[:, n // 4, n // 2 % 2, n % 2 * 512:(n % 2 + 1) * 512], ps[:, n % 4, :],
                                       ACT.Copy, scale=D ** -0.5 if n < 4 else 1.0).then_inc(proj_hi, 1)
                    else:
                        act.activation(vh[:, 2 * (n - 8):2 * (n - 8) + 2, :],
                                       ps[:, n % 4, :].rearrange("p (j d) -> p j d", j=2), ACT.Copy
                                       ).then_inc(proj_hi, 1)

            act.wait_ge(centered, 1)
            act.activation(R[1], R[0], ACT.Exp).then_inc(exp_done, 1)
            project_hi(0, range(NPROJ))

            def attend(b, first, last):
                def softmax(a):
                    i = ORDER[a]
                    act.wait_ge(max_done, BT * b + a + 1)
                    L = (i + 1) * P
                    act.activation(prob[:, a % 2, 0:L], ps[:, 2 * (a % 2):2 * (a % 2) + 2, :].rearrange(
                        "p h k -> p (h k)")[:, 0:L], ACT.Exp, bias=neg_max[:, i:i + 1],
                        accum_out=row_sum[:, i:i + 1]).then_inc(prob_ready, 1)

                def turned_hi(a):
                    act.wait_ge(prob_turned, BT * b + a + 1)
                    act.wait_ge(attended, BT * b + a + 1)
                    L = (ORDER[a] + 1) * P
                    act.activation(pTh[:, a % 2, 0:ORDER[a] + 1, :].rearrange("p j q -> p (j q)"),
                                   ps[:, 4:6, :].rearrange("p h k -> p (h k)")[:, 0:L], ACT.Copy).then_inc(pT_hi, 1)

                softmax(0)
                for a in range(BT):
                    if a + 1 < BT:
                        softmax(a + 1)
                    if a == 4 and not last:
                        act.activation(xh[:, :, :], xnT[:, :, ds((b + 1) * T, T)], ACT.Copy).then_inc(xh_ready, 1)
                    turned_hi(a)
                if not last:
                    project_hi(b + 1, range(NPROJ))

            sequences(act, attend)

        @block.vector
        def _(dve):
            V = nc.vector
            dve.sem_inc(attended, 2)
            dve.wait_ge(const_ready, 12)

            def statistics(b):
                dve.wait_ge(x_loaded[b], 16)
                for t in range(b * BT, (b + 1) * BT):
                    op = V.bn_stats(stats[:, t, :], x_tile(t))
                op.then_inc(stats_done, 1)
                dve.wait_ge(stats_done, b + 1)
                for t in range(b * BT, (b + 1) * BT):
                    op = V.bn_aggr(mv[:, t, :], stats[:, t, :])
                op.then_inc(mv_done, 1)

            def normalize(b):
                dve.wait_ge(std_done, b + 1)
                at = slice(b * BT, (b + 1) * BT)
                V.reciprocal(rstd[:, at], std[:, at]).then_inc(rstd_done, 1)
                dve.wait_ge(rstd_done, b + 1)
                if b >= 2:
                    dve.wait_ge(turned, 4 * (b - 1))
                    dve.wait_ge(xn_stored[b % 2], 16)
                for i in range(BT):
                    t = b * BT + i
                    op = V.tensor_scalar(xn[:, b % 2, i, :], x_tile(t), mv[:, t, 0:1], rstd[:, t:t + 1],
                                         ALU.subtract, ALU.mult)
                op.then_inc(xn_ready, 1)

            statistics(0)
            dve.wait_ge(wh_ready, 1)
            V.tensor_tensor(wl[:, :, :, :], w3[:, :, :, :], wh[:, :, :, :].bitcast(F32), ALU.subtract
                            ).then_inc(wl_ready, 1)
            for b in range(B):
                normalize(b)
                if b + 1 < B:
                    statistics(b + 1)
            dve.wait_ge(xh_ready, 1)
            V.tensor_tensor(xl[:, :, :], xnT[:, :, 0:T], xh[:, :, :].bitcast(F32), ALU.subtract).then_inc(xl_ready, 1)

            steps = [0]

            def then(op):
                steps[0] += 1
                op.then_inc(step, 1)
                dve.wait_ge(step, steps[0])

            def per_tile(a):
                return a.unsqueeze(2).to_broadcast([P, NT, E])

            def per_expert(a):
                return a.unsqueeze(1).to_broadcast([P, NT, E])

            def project_lo(b, results):
                for n in results:
                    dve.wait_ge(proj_hi, NPROJ * b + n + 1)
                    if n < 8:
                        at = (slice(None), n // 4, n // 2 % 2, slice(n % 2 * 512, (n % 2 + 1) * 512))
                        V.scalar_tensor_tensor(qkl[at], ps[:, n % 4, :], D ** -0.5 if n < 4 else 1.0,
                                               qkh[at].bitcast(F32), ALU.mult, ALU.subtract).then_inc(proj_lo, 1)
                    else:
                        at = (slice(None), slice(2 * (n - 8), 2 * (n - 8) + 2), slice(None))
                        V.tensor_tensor(vl[at], ps[:, n % 4, :].rearrange("p (j d) -> p j d", j=2),
                                        vh[at].bitcast(F32), ALU.subtract).then_inc(proj_lo, 1)


            lg = logits[:, :].rearrange("p (t e) -> p t e", e=E)
            dve.wait_ge(lg_ready, B)
            dve.wait_ge(turned, 4 * B)
            for u in range(2):
                dve.wait_ge(xn_stored[u], 16 * (B // 2))
            then(V.tensor_reduce(col[:, 0, :], lg, X, ALU.max))
            V.tensor_tensor(R[0], lg, per_tile(col[:, 0, :]), ALU.subtract).then_inc(centered, 1)
            dve.wait_ge(exp_done, 1)
            then(V.tensor_reduce(col[:, 1, :], R[1], X, ALU.add))
            then(V.reciprocal(col[:, 2, :], col[:, 1, :]))
            then(V.tensor_tensor(R[2], R[1], per_tile(col[:, 2, :]), ALU.mult))

            def pick(p, best, one_hot, scratch, key):
                then(V.tensor_reduce(best, p, X, ALU.max))
                then(V.tensor_tensor(scratch, p, per_tile(best), ALU.is_equal))
                then(V.tensor_tensor(scratch, scratch, per_expert(rank8[:, :]), ALU.mult))
                then(V.tensor_reduce(key, scratch, X, ALU.max))
                then(V.tensor_tensor(one_hot, scratch, per_tile(key), ALU.is_equal))

            project_lo(0, range(0, 2))
            pick(R[2], col[:, 3, :], R[3], R[0], col[:, 4, :])
            project_lo(0, range(2, 5))
            then(V.scalar_tensor_tensor(R[1], R[3], -4.0, R[2], ALU.mult, ALU.add))
            pick(R[1], col[:, 5, :], R[4], R[0], col[:, 4, :])
            V.tensor_tensor(R[6], R[3], R[4], ALU.add).then_inc(picked, 1)
            project_lo(0, range(5, 8))
            then(V.tensor_tensor(col[:, 6, :], col[:, 3, :], col[:, 5, :], ALU.add))
            then(V.reciprocal(col[:, 7, :], col[:, 6, :]))
            gv = s.gates[:, :].rearrange("p (t k) -> p t k", k=K)
            then(V.tensor_tensor(gv[:, :, 0], col[:, 3, :], col[:, 7, :], ALU.mult))
            then(V.tensor_tensor(gv[:, :, 1], col[:, 5, :], col[:, 7, :], ALU.mult))
            then(V.memset(col[:, 0, :], 1.0))
            project_lo(0, range(8, NPROJ))
            dve.wait_ge(counted, 1)
            V.tensor_copy(R[8], ps[:, 6, 0:NT * E].rearrange("p (t e) -> p t e", e=E))
            then(V.tensor_copy(R[9], ps[:, 7, 0:NT * E].rearrange("p (t e) -> p t e", e=E)))

            def rank():
                total = R[8]
                for e in range(E):
                    op = V.tensor_tensor_scan(R[5][:, :, e], col[:, 0, :], total[:, :, e], 0.0, ALU.mult, ALU.add)
                then(op)
                then(V.tensor_tensor(R[7], R[5], total, ALU.subtract))

            def place_experts():
                then(V.tensor_scalar(expert_int[:, :], R[5][:, NT - 1, :], float(M - 1), None, ALU.add))
                then(V.tensor_scalar(expert_int[:, :], expert_int[:, :], M.bit_length() - 1, None, ALU.arith_shift_right))
                then(V.tensor_copy(expert_row[:, 0, :], expert_int[:, :]))
                then(V.memset(expert_row[:, 1, :], 1.0))
                then(V.tensor_tensor_scan(expert_row[:, 2, :], expert_row[:, 1, :], expert_row[:, 0, :], 0.0,
                                          ALU.mult, ALU.add))
                then(V.tensor_tensor(expert_row[:, 3, :], expert_row[:, 2, :], expert_row[:, 0, :], ALU.subtract))
                then(V.tensor_scalar(expert_row[:, 4, :], expert_row[:, 3, :], float(M), None, ALU.mult))

            def place_tokens():
                then(V.tensor_tensor(R[7], R[7], per_expert(expert_row[:, 4, :]), ALU.add))
                then(V.tensor_tensor(R[7], R[7], R[9], ALU.add))
                sv = s.slots[:, :].rearrange("p (t k) -> p t k", k=K)
                for k in range(K):
                    then(V.tensor_tensor(R[0], R[7], R[3 + k], ALU.mult))
                    then(V.tensor_reduce(col[:, 1, :], R[0], X, ALU.add))
                    then(V.tensor_copy(sv[:, :, k], col[:, 1, :]))

            def tiles_of_experts():
                then(V.tensor_tensor(cmp[:, :, :], tile_no[:, :].unsqueeze(2).to_broadcast([P, MT + 1, E - 1]),
                                     expert_row[:, 2, 0:E - 1].unsqueeze(1).to_broadcast([P, MT + 1, E - 1]), ALU.is_ge))
                then(V.tensor_reduce(cnt[:, :], cmp[:, :, :], X, ALU.add))
                V.tensor_copy(s.tile_expert[:, :], cnt[:, :]).then_inc(routed, 1)

            def attend(b, first, last):
                def row_max(a):
                    i = ORDER[a]
                    dve.wait_ge(score_mm, BT * b + a + 1)
                    L = (i + 1) * P
                    V.tensor_reduce(neg_max[:, i:i + 1], ps[:, 2 * (a % 2):2 * (a % 2) + 2, :].rearrange(
                        "p h k -> p (h k)")[:, 0:L], X, ALU.max, negate=True).then_inc(max_done, 1)

                def turned_lo(a):
                    dve.wait_ge(pT_hi, BT * b + a + 1)
                    n = ORDER[a] + 1
                    V.tensor_tensor(pTl[:, a % 2, 0:n, :].rearrange("p j q -> p (j q)"),
                                    ps[:, 4:6, :].rearrange("p h k -> p (h k)")[:, 0:n * P],
                                    pTh[:, a % 2, 0:n, :].rearrange("p j q -> p (j q)").bitcast(F32),
                                    ALU.subtract).then_inc(pT_lo, 1)

                def add_attention(a):
                    i = ORDER[a]
                    V.reciprocal(row_inv[:, i:i + 1], row_sum[:, i:i + 1]).then_inc(inv_done, 1)
                    dve.wait_ge(inv_done, BT * b + a + 1)
                    dve.wait_ge(pv_mm, BT * b + a + 1)
                    V.scalar_tensor_tensor(x_tile(b * BT + i), ps[:, 6 + a % 2, 0:D], row_inv[:, i:i + 1],
                                           x_tile(b * BT + i), ALU.mult, ALU.add).then_inc(attended, 1)

                row_max(0)
                for a in range(BT):
                    if a + 1 < BT:
                        row_max(a + 1)
                    if first and a < 4:
                        (rank, place_experts, place_tokens, tiles_of_experts)[a]()
                    if a == 5 and not last:
                        dve.wait_ge(xh_ready, b + 2)
                        V.tensor_tensor(xl[:, :, :], xnT[:, :, ds((b + 1) * T, T)], xh[:, :, :].bitcast(F32),
                                        ALU.subtract).then_inc(xl_ready, 1)
                    turned_lo(a)
                    if 0 < a < BT - 1:
                        add_attention(a - 1)
                if not last:
                    project_lo(b + 1, range(8))
                add_attention(BT - 2)
                add_attention(BT - 1)
                if not last:
                    project_lo(b + 1, range(8, NPROJ))

            sequences(dve, attend)


def experts(nc, s, W1, W2, b2, dispatched, expert_out):
    D, DC, E, H, HC, M, MT = s.D, s.DC, s.E, s.H, s.HC, s.M, s.MT
    MS = M // P
    NQ = HC // 2
    ps = s.ps
    with ExitStack() as ctx:
        def sb(name, shape, dt=F32):
            return ctx.enter_context(nc.sbuf_tensor(name, shape, dt))

        def sem(name):
            return ctx.enter_context(nc.semaphore(name))

        raw = [s.raw, sb("raw_odd", [P, DC * H + HC * D])]
        w1raw = [r[:, 0:DC * H].rearrange("p (c h) -> p c h", c=DC) for r in raw]
        w2raw = [r[:, DC * H:].rearrange("p (k d) -> p k d", k=HC) for r in raw]
        w1h, w1l = sb("w1h", [P, 2, DC, H], F32R), sb("w1l", [P, 2, DC, H], F32R)
        w2h, w2l = sb("w2h", [P, 2, HC, D], F32R), sb("w2l", [P, 2, HC, D], F32R)
        rows = sb("rows", [P, 2, MS, D])
        xTh, xTl = sb("xTh", [P, DC, M], F32R), sb("xTl", [P, DC, M], F32R)
        h32 = sb("h32", [P, HC, M])
        hh, hl = sb("hh", [P, HC, M], F32R), sb("hl", [P, HC, M], F32R)
        y = sb("y", [P, 2, MS, D])
        b2all = sb("b2all", [P, E * D])

        b2_loaded, passed = sem("b2_loaded"), sem("passed")
        rows_loaded = [sem(f"rows_loaded{u}") for u in range(2)]
        w1_loaded = [s.raw_loaded[0], sem("w1_loaded_odd")]
        w2_loaded = [s.raw_loaded[1], sem("w2_loaded_odd")]
        y_stored = [sem(f"y_stored{u}") for u in range(2)]
        w1_hi, w1_lo, w2_hi, w2_lo = sem("w1_hi"), sem("w1_lo"), sem("w2_hi"), sem("w2_lo")
        rows_turned, xT_hi, xT_lo = sem("rows_turned"), sem("xT_hi"), sem("xT_lo")
        up_mm, relu_done, h_hi, h_lo, down_mm, y_done = (sem(n) for n in (
            "up_mm", "relu_done", "h_hi", "h_lo", "down_mm", "y_done"))

        def tiles(eng, body):
            body(0, 0)
            body(0, 1)
            with eng.Fori(1, MT // 2) as g:
                body(g, 0)
                body(g, 1)
            body(MT // 2, 0)

        def is_last(g, u):
            return isinstance(g, int) and 2 * g + u == MT - 1

        def following(g, u):
            return (g, 1) if u == 0 else (g + 1, 0)

        def first(g):
            return isinstance(g, int) and g == 0

        def expert_of(eng, g, u):
            return eng.value_load(s.tile_expert[0:1, ds(2 * g + u, 1)], min_val=0, max_val=E - 1)

        block = ctx.enter_context(nc.Block())

        @block.sync
        def _(sp):
            def load(g, u):
                j = 2 * g + u
                e = expert_of(sp, g, u)
                if not first(g):
                    sp.wait_ge(rows_turned, j - 1)
                sp.dma_start(rows[:, u], dispatched[ds(j * M, M), :].rearrange("(s p) d -> p s d", p=P)
                             ).then_inc(rows_loaded[u], 16)
                if not first(g):
                    sp.wait_ge(w1_lo, NQ * (j - 1))
                    sp.wait_ge(w2_lo, NQ * (j - 1))
                if not (isinstance(g, int) and j == 0):
                    load_weights(sp, s, W1, W2, e, raw[u], (w1_loaded[u], w2_loaded[u]))
                if isinstance(g, int) and j == 1:
                    sp.dma_start(b2all[:, :], b2.rearrange("e d -> (e d)").partition_broadcast(P)
                                 ).then_inc(b2_loaded, 16)

            tiles(sp, load)

        @block.gpsimd
        def _(pool):
            def split(g, u, q):
                pool.tensor_copy(w2h[:, u, 2 * q:2 * q + 2, :], w2raw[u][:, 2 * q:2 * q + 2, :]).then_inc(w2_hi, 1)

            def store(g, u):
                j = 2 * g + u
                hold(pool, y_done, j + 1, passed)
                pool.dma_start(expert_out[ds(j * M, M), :].rearrange("(s p) d -> p s d", p=P), y[:, u]
                               ).then_inc(y_stored[u], 16)

            pool.wait_ge(w2_loaded[0], 16)
            for q in range(NQ):
                split(0, 0, q)

            def body(g, u):
                if not is_last(g, u):
                    ng, nu = following(g, u)
                    hold(pool, w2_loaded[nu], 16 * ng + 16, passed)
                    if not (isinstance(g, int) and 2 * g + u == 0):
                        hold(pool, down_mm, 2 * g + u, passed)
                    for q in range(NQ):
                        split(ng, nu, q)
                store(g, u)

            tiles(pool, body)
            pool.wait_ge(y_stored[0], 16 * (MT // 2 + 1))
            pool.wait_ge(y_stored[1], 16 * (MT // 2))

        @block.tensor
        def _(pe):
            def three(out, ah, al, bh, bl, start, stop):
                pe.matmul(out, ah, bh, start=start, stop=False, skip_group_check=True)
                pe.matmul(out, ah, bl, start=False, stop=False, skip_group_check=True)
                return pe.matmul(out, al, bh, start=False, stop=stop, skip_group_check=True)

            def turn_rows(g, u):
                pe.wait_ge(rows_loaded[u], 16 * g + 16)
                for c in range(DC):
                    for part in range(MS):
                        mm = pe.transpose(ps[:, 6, c * M + part * P:c * M + (part + 1) * P],
                                          rows[:, u, part, c * P:(c + 1) * P], s.ident[:, :])
                mm.then_inc(rows_turned, 1)

            turn_rows(0, 0)

            def body(g, u):
                j = 2 * g + u
                pe.wait_ge(xT_lo, j + 1)
                for q in range(NQ):
                    pe.wait_ge(w1_lo, NQ * j + q + 1)
                    for k in (2 * q, 2 * q + 1):
                        for c in range(DC):
                            ws = slice(k * P, (k + 1) * P)
                            mm = three(ps[:, q, (k % 2) * M:(k % 2 + 1) * M], w1h[:, u, c, ws], w1l[:, u, c, ws],
                                       xTh[:, c, :], xTl[:, c, :], c == 0, c == DC - 1)
                    mm.then_inc(up_mm, 1)
                if not is_last(g, u):
                    turn_rows(*following(g, u))
                if not (isinstance(g, int) and j == 0):
                    pe.wait_ge(y_done, j)
                for k in range(HC):
                    if k % 2 == 0:
                        pe.wait_ge(h_lo, NQ * j + k // 2 + 1)
                        pe.wait_ge(w2_lo, NQ * j + k // 2 + 1)
                    for part in range(MS):
                        bank = 5 if part else 4
                        rs = slice(part * P, (part + 1) * P)
                        mm = three(ps[:, bank, 0:D], hh[:, k, rs], hl[:, k, rs], w2h[:, u, k, :], w2l[:, u, k, :],
                                   k == 0, k == HC - 1)
                mm.then_inc(down_mm, 1)

            tiles(pe, body)

        @block.scalar
        def _(act):
            def split(g, u, q):
                cols = slice(q * H // NQ, (q + 1) * H // NQ)
                act.activation(w1h[:, u, :, cols], w1raw[u][:, :, cols], ACT.Copy).then_inc(w1_hi, 1)

            def turned_hi(g, u):
                act.wait_ge(rows_turned, 2 * g + u + 1)
                act.activation(xTh[:, :, :], ps[:, 6, :].rearrange("p (c m) -> p c m", c=DC), ACT.Copy
                               ).then_inc(xT_hi, 1)

            act.wait_ge(w1_loaded[0], 16)
            for q in range(NQ):
                split(0, 0, q)
            turned_hi(0, 0)

            def body(g, u):
                j = 2 * g + u
                e = expert_of(act, g, u)
                ng, nu = following(g, u)
                for q in range(NQ):
                    act.wait_ge(up_mm, NQ * j + q + 1)
                    for k in (2 * q, 2 * q + 1):
                        op = act.activation(h32[:, k, :], ps[:, q, (k % 2) * M:(k % 2 + 1) * M], ACT.Relu,
                                            bias=s.b1T[:, ds(e * HC + k, 1)])
                    op.then_inc(relu_done, 1)
                    act.wait_ge(relu_done, NQ * j + q + 1)
                    act.activation(hh[:, 2 * q:2 * q + 2, :], h32[:, 2 * q:2 * q + 2, :], ACT.Copy).then_inc(h_hi, 1)
                    if not is_last(g, u) and q > 0:
                        if q == 1:
                            act.wait_ge(w1_loaded[nu], 16 * ng + 16)
                        if q == NQ - 1:
                            turned_hi(ng, nu)
                        split(ng, nu, q - 1)
                if not is_last(g, u):
                    split(ng, nu, NQ - 1)

            tiles(act, body)

        @block.vector
        def _(dve):
            V = nc.vector

            def split1(g, u, q):
                dve.wait_ge(w1_hi, NQ * (2 * g + u) + q + 1)
                cols = slice(q * H // NQ, (q + 1) * H // NQ)
                V.tensor_tensor(w1l[:, u, :, cols], w1raw[u][:, :, cols], w1h[:, u, :, cols].bitcast(F32),
                                ALU.subtract).then_inc(w1_lo, 1)

            def split2(g, u, q):
                dve.wait_ge(w2_hi, NQ * (2 * g + u) + q + 1)
                ks = slice(2 * q, 2 * q + 2)
                V.tensor_tensor(w2l[:, u, ks], w2raw[u][:, ks], w2h[:, u, ks].bitcast(F32), ALU.subtract
                                ).then_inc(w2_lo, 1)

            def turned_lo(g, u):
                dve.wait_ge(xT_hi, 2 * g + u + 1)
                V.tensor_tensor(xTl[:, :, :], ps[:, 6, :].rearrange("p (c m) -> p c m", c=DC),
                                xTh[:, :, :].bitcast(F32), ALU.subtract).then_inc(xT_lo, 1)

            for q in range(NQ):
                split1(0, 0, q)
            turned_lo(0, 0)
            for q in range(NQ):
                split2(0, 0, q)
            dve.wait_ge(b2_loaded, 16)

            def body(g, u):
                j = 2 * g + u
                e = expert_of(dve, g, u)
                ng, nu = following(g, u)
                for q in range(NQ):
                    dve.wait_ge(h_hi, NQ * j + q + 1)
                    at = (slice(None), slice(2 * q, 2 * q + 2), slice(None))
                    V.tensor_tensor(hl[at], h32[at], hh[at].bitcast(F32), ALU.subtract).then_inc(h_lo, 1)
                    if not is_last(g, u) and q > 0:
                        if q == NQ - 1:
                            turned_lo(ng, nu)
                        split1(ng, nu, q - 1)
                        if q > 1:
                            split2(ng, nu, q - 2)
                if not is_last(g, u):
                    split2(ng, nu, NQ - 2)
                    split1(ng, nu, NQ - 1)
                    split2(ng, nu, NQ - 1)
                dve.wait_ge(down_mm, j + 1)
                if not first(g):
                    dve.wait_ge(y_stored[u], 16 * g)
                for part in range(MS):
                    op = V.tensor_tensor(y[:, u, part, :], ps[:, 4 + part, 0:D], b2all[:, ds(e * D, D)], ALU.add)
                op.then_inc(y_done, 1)

            tiles(dve, body)


def combine_and_layer1(nc, s, expert_out, W_qkv, W_out, W_r, W_k, W_v, mu_r, mu_k, rope_cos, rope_sin, out):
    B, BT, D, DC, T, K = s.B, s.BT, s.D, s.DC, s.T, s.K
    HD = rope_cos.shape[1]
    HP = P // HD
    NG = BT // 2
    LOADS = 2 + 3 + 2 * DC + 2
    HB = T // 2
    ps = s.ps
    with ExitStack() as ctx:
        def sb(name, shape, dt=F32):
            return ctx.enter_context(nc.sbuf_tensor(name, shape, dt))

        def sem(name):
            return ctx.enter_context(nc.semaphore(name))

        picked_rows = s.raw[:, 0:BT * K * D].rearrange("p (i k d) -> p i k d", i=BT, k=K)
        slot_now = sb("slot_again", [P, BT, K], U32)
        stats, mv = sb("stats1", [P, BT, 6]), sb("mv1", [P, BT, 2])
        std, rstd, shift = sb("std1", [P, BT]), sb("rstd1", [P, BT]), sb("shift1", [P, BT])
        unused = sb("unused", [P, 1])
        xn = sb("xn1", [P, BT, D])
        xnT = sb("xnT1", [P, DC, T + 1])
        step_T = sb("step_T", [P, DC, T])
        xrT, xkT = sb("xrT", [P, DC, T]), sb("xkT", [P, DC, T])
        qk, rot, straight = sb("qk", [P, 2, 2, 2 * D]), sb("rot", [P, 2, 2, 2 * D]), sb("straight", [P, 2, 2, 2 * D])
        feat = sb("feat", [P, BT, 2 * D])
        v1 = sb("v1", [P, BT, DC, P + 1])
        oT = sb("oT", [P, DC, T])
        qT, act_k = xkT, step_T
        gate = sb("gate", [P, BT, D])
        kv = sb("kv", [P, DC, P + HP])
        att = sb("att", [P, BT, D])
        same_head, head_of = sb("same_head", [P, P]), sb("head_of", [P, HP])
        wout = sb("wout", [P, DC, D])
        wqkv = rot[:, :, :, :].rearrange("p a b d -> p (a b d)")[:, 0:DC * 3 * D].rearrange("p (c e) -> p c e", c=DC)
        wraw = straight[:, :, :, :].rearrange("p a b d -> p (a b d)")[:, 0:3 * DC * D].rearrange(
            "p (n c e) -> p n c e", n=3, c=DC)
        wqkvh, wqkvl = sb("wqkvh", [P, DC, 3 * D], F32R), sb("wqkvl", [P, DC, 3 * D], F32R)
        xh, xl = sb("xh1", [P, DC, T], F32R), sb("xl1", [P, DC, T], F32R)
        wT = sb("wT", [P, 3, DC, D])
        mu = sb("mu", [P, 2, DC])
        cos, sin = sb("cos", [P, BT, HD]), sb("sin", [P, BT, HD])
        den = sb("den", [P, 2, 2, DC, HP])

        loaded, const_ready, weights_turned, weights_ready, passed = (sem(n) for n in (
            "loaded", "const_ready1", "weights_turned", "weights_ready", "passed1"))
        slot_staged, first_added, combined = sem("slot_staged1"), sem("first_added"), sem("combined")
        gathered = [sem(f"gathered{u}") for u in range(BT)]
        stats_done, mv_done, std_done, rstd_done, shift_done, xn_ready = (sem(n) for n in (
            "stats_done1", "mv_done1", "std_done1", "rstd_done1", "shift_done1", "xn_ready1"))
        turned, xnT_ready, step_ready, mixed = sem("turned1"), sem("xnT_ready1"), sem("step_ready"), sem("mixed")
        qkv_mm, qkv_out, rotated, straight_done, summed, clipped, exp_done, feat_done = (sem(n) for n in (
            "qkv_mm", "qkv_out", "rotated", "straight_done", "summed", "clipped", "exp_done1", "feat_done"))
        k_mm, k_out, squared, r_mm, gate_ready = (sem(n) for n in ("k_mm", "k_out", "squared", "r_mm", "gate_ready"))
        qT_mm, qT_ready, kv_mm, kv_ready, v_mm, gated = (sem(n) for n in (
            "qT_mm", "qT_ready", "kv_mm", "kv_ready", "v_mm", "gated"))
        nd_mm, den_clipped, den_inv, att_ready, att_turned, oT_ready = (sem(n) for n in (
            "nd_mm", "den_clipped", "den_inv", "att_ready", "att_turned", "oT_ready"))
        wh_ready, wl_ready, xh_ready, xl_ready = (sem(n) for n in ("wh_ready1", "wl_ready1", "xh_ready1", "xl_ready1"))
        out_mm, out_added, final, stored = (sem(n) for n in ("out_mm", "out_added", "final", "stored"))

        def x_tile(t, n=1):
            return s.x_acc[:, ds(t * D, n * D)]

        def pair_of_tiles(bank):
            return bank.rearrange("p (j d) -> p j d", j=2)

        def sequences(eng, body):
            with eng.Fori(0, B - 1) as b:
                body(b, False)
            body(B - 1, True)

        block = ctx.enter_context(nc.Block())

        @block.sync
        def _(sp):
            def feature_rows(w):
                return w.rearrange("(c p) e -> p c e", p=P)

            sp.dma_start(wqkv[:, :, :], feature_rows(W_qkv)).then_inc(loaded, 16)
            sp.dma_start(wout[:, :, :], feature_rows(W_out)).then_inc(loaded, 16)
            for n, w in enumerate((W_r, W_k, W_v)):
                sp.dma_start(wraw[:, n], feature_rows(w)).then_inc(loaded, 16)
            for n, m in enumerate((mu_r, mu_k)):
                for c in range(DC):
                    sp.dma_start(mu[:, n, c:c + 1], m[c * P:(c + 1) * P].rearrange("(p a) -> p a", a=1)
                                 ).then_inc(loaded, 16)
            sp.dma_start(cos[:, :, :], rope_cos.rearrange("(i p) f -> p i f", p=P)).then_inc(loaded, 16)
            sp.dma_start(sin[:, :, :], rope_sin.rearrange("(i p) f -> p i f", p=P)).then_inc(loaded, 16)
            with sp.Fori(0, B) as b:
                sp.wait_ge(final, NG * b + NG)
                sp.dma_start(out.rearrange("b (i p) d -> b p i d", p=P)[b],
                             x_tile(b * BT, BT).rearrange("p (i d) -> p i d", d=D)).then_inc(stored, 16)
            sp.wait_ge(stored, 16 * B)

        @block.gpsimd
        def _(pool):
            def gather(b):
                for i in range(BT):
                    t = b * BT + i
                    if b > 0 and i % 4 == 0:
                        pool.wait_ge(combined, 2 * (b - 1) + i // 4 + 1)
                    pool.tensor_copy(slot_now[:, i, :], s.slots[:, K * t:K * t + K]).then_inc(slot_staged, 1)
                    pool.wait_ge(slot_staged, t + 1)
                    for k in range(K):
                        pool.indirect_dma_start(out=picked_rows[:, i, k, :], out_offset=None, in_=expert_out,
                                                in_offset=bass.IndirectOffsetOnAxis(ap=slot_now[:, i, k:k + 1], axis=0)
                                                ).then_inc(gathered[i], 16)


            gather(0)
            pool.memset(same_head[:, :], 1.0).then_inc(const_ready, 1)
            pool.memset(xnT[:, :, 0:1], 0.0).then_inc(const_ready, 1)
            pool.memset(v1[:, :, :, P:P + 1], 1.0).then_inc(const_ready, 1)
            heads = same_head[:, :].rearrange("p (h f) -> p h f", f=HD)
            pool.wait_ge(const_ready, 3)
            pool.affine_select(out=heads, in_=heads, compare_op=ALU.is_ge, fill=0.0, base=0,
                               pattern=[[-HD, HP], [0, HD]], channel_multiplier=1).then_inc(const_ready, 1)
            pool.wait_ge(const_ready, 4)
            pool.affine_select(out=heads, in_=heads, compare_op=ALU.is_gt, fill=0.0, base=HD,
                               pattern=[[HD, HP], [0, HD]], channel_multiplier=-1).then_inc(const_ready, 1)
            pool.wait_ge(const_ready, 5)
            pool.tensor_copy(head_of[:, :], heads[:, :, 0]).then_inc(const_ready, 1)

            def rotate(b):
                pool.wait_ge(xnT_ready, 4 * b + 4)
                pool.tensor_tensor(step_T[:, :, :], xnT[:, :, 1:T + 1], xnT[:, :, 0:T], ALU.subtract
                                   ).then_inc(step_ready, 1)
                for n in range(NG):
                    pool.wait_ge(qkv_out, NG * b + n + 1)
                    src = qk[:, n % 2].rearrange("p j (h f) -> p j h f", f=HD)
                    dst = rot[:, n % 2].rearrange("p j (h f) -> p j h f", f=HD)
                    for half in range(2):
                        to = slice(half * HD // 2, (half + 1) * HD // 2)
                        fro = slice((1 - half) * HD // 2, (2 - half) * HD // 2)
                        table = sin[:, 2 * n:2 * n + 2, to].unsqueeze(2).to_broadcast([P, 2, 2 * D // HD, HD // 2])
                        op = pool.tensor_tensor(dst[:, :, :, to], src[:, :, :, fro], table, ALU.mult)
                    op.then_inc(rotated, 1)

            def finish(b):
                for n in range(NG):
                    pool.wait_ge(out_added, NG * b + n + 1 + NG)
                    pool.tensor_tensor(x_tile(b * BT + 2 * n, 2), x_tile(b * BT + 2 * n, 2),
                                       gate[:, 2 * n:2 * n + 2, :].rearrange("p j d -> p (j d)"), ALU.add
                                       ).then_inc(final, 1)

            pool.wait_ge(loaded, 16 * LOADS)
            for b in range(B):
                rotate(b)
                for ahead in ((1, 2) if b == 0 else (b + 2,)):
                    if ahead < B:
                        gather(ahead)
                finish(b)

        @block.tensor
        def _(pe):
            pe.wait_ge(loaded, 16 * LOADS)
            for n in range(3):
                for c in range(DC):
                    for d in range(DC):
                        mm = pe.transpose(ps[:, 4 + n, c * D + d * P:c * D + (d + 1) * P],
                                          wraw[:, n, d, c * P:(c + 1) * P], s.ident[:, :])
            mm.then_inc(weights_turned, 1)
            pe.wait_ge(weights_ready, 1)

            def turn(b, half):
                for c in range(DC):
                    q = 2 * half + c
                    if c == 0:
                        hold(pe, xn_ready, 2 * b + half + 1, passed)
                    for i in range(4):
                        mm = pe.transpose(ps[:, q, i * P:(i + 1) * P], xn[:, half * 4 + i, c * P:(c + 1) * P],
                                          s.ident[:, :])
                    mm.then_inc(turned, 1)

            def product(dst, lhsT, rhs):
                pe.matmul(dst, lhsT(0), rhs(0), start=True, stop=False)
                return pe.matmul(dst, lhsT(1), rhs(1), start=False, stop=True)

            def product_of_parts(dst, ah, al, bh, bl):
                for c in range(DC):
                    pe.matmul(dst, ah(c), bh(c), start=(c == 0), stop=False)
                    pe.matmul(dst, ah(c), bl(c), start=False, stop=False)
                    mm = pe.matmul(dst, al(c), bh(c), start=False, stop=(c == DC - 1))
                return mm

            def tile_of(i):
                return slice(i * P, (i + 1) * P)

            def half_of(h):
                return slice(h * HB, (h + 1) * HB)

            def body(b, last):
                pe.wait_ge(out_added, NG * b + NG)
                for n in range(NG):
                    if n % 2 == 0:
                        pe.wait_ge(xl_ready, 4 * b + 2 + n)
                    if n >= 2:
                        pe.wait_ge(qkv_out, NG * b + n - 1)
                    for j in range(2):
                        i = 2 * n + j

                        ah, al = (lambda c: xh[:, c, tile_of(i)]), (lambda c: xl[:, c, tile_of(i)])
                        product_of_parts(ps[:, (4 + 3 * n + j) % 8, :], ah, al,
                                         lambda c: wqkvh[:, c, 0:2 * D], lambda c: wqkvl[:, c, 0:2 * D])
                        mm = product_of_parts(ps[:, (6 + 3 * n) % 8, j * D:(j + 1) * D], ah, al,
                                              lambda c: wqkvh[:, c, 2 * D:3 * D], lambda c: wqkvl[:, c, 2 * D:3 * D])
                    mm.then_inc(qkv_mm, 1)
                pe.wait_ge(mixed, b + 1)
                pe.wait_ge(qkv_out, NG * b + 3)
                for n in range(4):
                    m, h = n // 2, n % 2
                    product(ps[:, n, :], lambda c: wT[:, 1, c, tile_of(m)], lambda c: xkT[:, c, half_of(h)]
                            ).then_inc(k_mm, 1)
                pe.wait_ge(qkv_out, NG * b + 4)
                for n in range(NG):
                    for j in range(2):
                        mm = product(ps[:, 4 + n, j * D:(j + 1) * D], lambda c: xrT[:, c, tile_of(2 * n + j)],
                                     lambda c: wT[:, 0, c, :])
                    mm.then_inc(r_mm, 1)
                pe.wait_ge(feat_done, NG * b + NG + 2)
                pe.wait_ge(k_out, 4 * b + 4)
                for n in range(4):
                    c, h = n // 2, n % 2
                    for i in range(4):
                        mm = pe.transpose(ps[:, n, tile_of(i)], feat[:, 4 * h + i, tile_of(c)], s.ident[:, :])
                    mm.then_inc(qT_mm, 1)
                pe.wait_ge(gate_ready, NG * b + 2)
                for c in range(DC):
                    for i in range(BT):
                        mm = pe.matmul(ps[:, 4 + c, 0:P + 1], feat[:, i, D + c * P:D + (c + 1) * P], v1[:, i, c, :],
                                       start=(i == 0), stop=(i == BT - 1))
                mm.then_inc(kv_mm, 1)
                pe.wait_ge(squared, 4 * b + 4)
                pe.wait_ge(gate_ready, NG * b + NG)
                for n in range(NG):
                    if n == 2:
                        pe.wait_ge(qT_ready, 4 * b + 2)
                    for j in range(2):
                        mm = product(ps[:, (6 + n) % 8, j * D:(j + 1) * D], lambda c: act_k[:, c, tile_of(2 * n + j)],
                                     lambda c: wT[:, 2, c, :])
                    mm.then_inc(v_mm, 1)
                pe.wait_ge(qT_ready, 4 * b + 4)
                pe.wait_ge(kv_ready, b + 1)
                for i in range(BT):
                    if i in (4, 6):
                        pe.wait_ge(gated, NG * b + i - 2)
                    for c in range(DC):
                        mm = pe.matmul(ps[:, (2 + i) % 8, c * (P + HP):(c + 1) * (P + HP)], qT[:, c, tile_of(i)],
                                       kv[:, c, :], start=True, stop=True)
                    if i % 2:
                        mm.then_inc(nd_mm, 1)
                for h in range(2):
                    pe.wait_ge(att_ready, NG * b + 2 * (h + 1))
                    if h:
                        pe.wait_ge(oT_ready, 4 * b + 2)
                    for c in range(DC):
                        for i in range(4):
                            mm = pe.transpose(ps[:, 2 + c, tile_of(i)], att[:, 4 * h + i, tile_of(c)], s.ident[:, :])
                        mm.then_inc(att_turned, 1)
                    if h and not last:
                        turn(b + 1, 0)
                    pe.wait_ge(oT_ready, 4 * b + 2 * (h + 1))
                    for n in (2 * h, 2 * h + 1):
                        for j in range(2):
                            mm = product(ps[:, 4 + n, j * D:(j + 1) * D], lambda c: oT[:, c, tile_of(2 * n + j)],
                                         lambda c: wout[:, c, :])
                        mm.then_inc(out_mm, 1)
                if not last:
                    turn(b + 1, 1)

            turn(0, 0)
            turn(0, 1)
            sequences(pe, body)

        @block.scalar
        def _(act):
            act.wait_ge(loaded, 16 * LOADS)
            act.activation(wqkvh[:, :, :], wqkv[:, :, :], ACT.Copy).then_inc(wh_ready, 1)
            act.wait_ge(weights_turned, 1)
            act.activation(wT[:, :, :, :].rearrange("p n c d -> p n (c d)"), ps[:, 4:7, :], ACT.Copy
                           ).then_inc(weights_ready, 1)
            act.wait_ge(const_ready, 6)
            act.activation(unused[:, :], s.eps[:, 0:1], ACT.Sqrt)

            def normed(b, halves):
                for h in halves:
                    act.wait_ge(mv_done, 2 * b + h + 1)
                    at = slice(4 * h, 4 * h + 4)
                    act.activation(std[:, at], mv[:, at, 1], ACT.Sqrt, bias=s.eps[:, 0:1]).then_inc(std_done, 1)
                    act.wait_ge(shift_done, 2 * b + h + 1)
                    for i in range(4 * h, 4 * h + 4):
                        op = act.activation(xn[:, i, :], x_tile(b * BT + i), ACT.Identity, bias=shift[:, i:i + 1],
                                            scale=rstd[:, i:i + 1])
                    op.then_inc(xn_ready, 1)

            def turned_out(b, halves):
                for q in range(2 * halves[0], 2 * halves[-1] + 2):
                    act.wait_ge(turned, 4 * b + q + 1)
                    h, c = q // 2, q % 2
                    act.activation(xnT[:, c, 1 + h * HB:1 + (h + 1) * HB], ps[:, q, :], ACT.Copy
                                   ).then_inc(xnT_ready, 1)
                    act.wait_ge(xnT_ready, 4 * b + q + 1)
                    act.activation(xh[:, c, h * HB:(h + 1) * HB], xnT[:, c, 1 + h * HB:1 + (h + 1) * HB], ACT.Copy
                                   ).then_inc(xh_ready, 1)

            for h in range(2):
                normed(0, [h])
                turned_out(0, [h])

            def body(b, last):
                def features(n):
                    act.wait_ge(clipped, NG * b + n + 1)
                    act.activation(qk[:, n % 2], qk[:, n % 2], ACT.Exp).then_inc(exp_done, 1)

                for n in range(NG):
                    act.wait_ge(qkv_mm, NG * b + n + 1)
                    act.wait_ge(feat_done, NG * b + n + 1)
                    for j in range(2):
                        bank = ps[:, (4 + 3 * n + j) % 8, :]
                        act.activation(qk[:, n % 2, j, 0:D], bank[:, 0:D], ACT.Copy, scale=HD ** -0.5)
                        act.activation(qk[:, n % 2, j, D:2 * D], bank[:, D:2 * D], ACT.Copy)
                    act.activation(v1[:, 2 * n:2 * n + 2, :, 0:P],
                                   ps[:, (6 + 3 * n) % 8, :].rearrange("p (j c f) -> p j c f", j=2, c=DC), ACT.Copy
                                   ).then_inc(qkv_out, 1)
                    if n > 0:
                        features(n - 1)
                features(NG - 1)
                for n in range(4):
                    act.wait_ge(k_mm, 4 * b + n + 1)
                    m, h = n // 2, n % 2
                    act.activation(act_k[:, m, h * HB:(h + 1) * HB], ps[:, n, :], ACT.Relu).then_inc(k_out, 1)
                act.wait_ge(rotated, NG * b + NG)
                for n in range(NG):
                    act.wait_ge(r_mm, NG * b + n + 1)
                    act.activation(gate[:, 2 * n:2 * n + 2, :], pair_of_tiles(ps[:, 4 + n, :]), ACT.Sigmoid
                                   ).then_inc(gate_ready, 1)
                for n in range(4):
                    act.wait_ge(qT_mm, 4 * b + n + 1)
                    c, h = n // 2, n % 2
                    act.activation(qT[:, c, h * HB:(h + 1) * HB], ps[:, n, :], ACT.Copy).then_inc(qT_ready, 1)
                if not last:
                    normed(b + 1, [0, 1])
                for m in range(4):
                    h, c = m // 2, m % 2
                    act.wait_ge(att_turned, 4 * b + m + 1)
                    act.activation(oT[:, c, h * HB:(h + 1) * HB], ps[:, 2 + c, :], ACT.Copy).then_inc(oT_ready, 1)
                if not last:
                    act.wait_ge(mixed, b + 1)
                    turned_out(b + 1, [0, 1])

            sequences(act, body)

        @block.vector
        def _(dve):
            V = nc.vector
            dve.sem_inc(feat_done, 2)
            dve.sem_inc(out_added, NG)


            def turned_lo(b, halves):
                for q in range(2 * halves[0], 2 * halves[-1] + 2):
                    dve.wait_ge(xh_ready, 4 * b + q + 1)
                    h, c = q // 2, q % 2
                    V.tensor_tensor(xl[:, c, h * HB:(h + 1) * HB], xnT[:, c, 1 + h * HB:1 + (h + 1) * HB],
                                    xh[:, c, h * HB:(h + 1) * HB].bitcast(F32), ALU.subtract).then_inc(xl_ready, 1)

            def combine(b, halves):
                for h in halves:
                    half = range(4 * h, 4 * h + 4)
                    for k in range(K):
                        for i in half:
                            t = b * BT + i
                            if k == 0:
                                dve.wait_ge(gathered[i], 16 * K * (b + 1))
                            op = V.scalar_tensor_tensor(x_tile(t), picked_rows[:, i, k, :],
                                                        s.gates[:, ds(K * t + k, 1)], x_tile(t), ALU.mult, ALU.add)
                        if k == 0:
                            op.then_inc(first_added, 1)
                            dve.wait_ge(first_added, 2 * b + h + 1)
                    op.then_inc(combined, 1)
                    hold(dve, combined, 2 * b + h + 1, passed)
                    for i in half:
                        op = V.bn_stats(stats[:, i, :], x_tile(b * BT + i))
                    op.then_inc(stats_done, 1)
                    hold(dve, stats_done, 2 * b + h + 1, passed)
                    for i in half:
                        op = V.bn_aggr(mv[:, i, :], stats[:, i, :])
                    op.then_inc(mv_done, 1)
                    at = slice(4 * h, 4 * h + 4)
                    dve.wait_ge(std_done, 2 * b + h + 1)
                    V.reciprocal(rstd[:, at], std[:, at]).then_inc(rstd_done, 1)
                    dve.wait_ge(rstd_done, 2 * b + h + 1)
                    V.scalar_tensor_tensor(shift[:, at], mv[:, at, 0], -1.0, rstd[:, at], ALU.mult, ALU.mult
                                           ).then_inc(shift_done, 1)

            combine(0, [0])
            dve.wait_ge(wh_ready, 1)
            V.tensor_tensor(wqkvl[:, :, :], wqkv[:, :, :], wqkvh[:, :, :].bitcast(F32), ALU.subtract
                            ).then_inc(wl_ready, 1)
            turned_lo(0, [0])
            combine(0, [1])
            turned_lo(0, [1])

            def body(b, last):
                for n in range(NG):
                    if n == 1:
                        dve.wait_ge(step_ready, b + 1)
                        for m, dst in enumerate((xrT, xkT)):
                            for c in range(DC):
                                op = V.scalar_tensor_tensor(dst[:, c, :], step_T[:, c, :], mu[:, m, c:c + 1], xnT[:, c, 0:T],
                                                            ALU.mult, ALU.add)
                        op.then_inc(mixed, 1)
                    dve.wait_ge(qkv_out, NG * b + n + 1)
                    a = straight[:, n % 2]
                    V.tensor_tensor(a.rearrange("p j (h f) -> p j h f", f=HD),
                                    qk[:, n % 2].rearrange("p j (h f) -> p j h f", f=HD),
                                    cos[:, 2 * n:2 * n + 2, :].unsqueeze(2).to_broadcast([P, 2, 2 * D // HD, HD]),
                                    ALU.mult).then_inc(straight_done, 1)
                    dve.wait_ge(straight_done, NG * b + n + 1)
                    dve.wait_ge(rotated, NG * b + n + 1)
                    V.tensor_tensor(a, a, rot[:, n % 2], ALU.add).then_inc(summed, 1)
                    dve.wait_ge(summed, NG * b + n + 1)
                    V.tensor_scalar(qk[:, n % 2], a, 0.0, None, ALU.min).then_inc(clipped, 1)
                    dve.wait_ge(exp_done, NG * b + n + 1)
                    V.scalar_tensor_tensor(feat[:, 2 * n:2 * n + 2, :], a, 0.0, qk[:, n % 2], ALU.max, ALU.add
                                           ).then_inc(feat_done, 1)
                for n in range(4):
                    dve.wait_ge(k_out, 4 * b + n + 1)
                    m, h = n // 2, n % 2
                    at = act_k[:, m, h * HB:(h + 1) * HB]
                    V.tensor_tensor(at, at, at, ALU.mult).then_inc(squared, 1)
                if not last:
                    combine(b + 1, [0, 1])
                dve.wait_ge(kv_mm, b + 1)
                for c in range(DC):
                    V.tensor_tensor(kv[:, c, 0:P], ps[:, 4 + c, 0:P], same_head[:, :], ALU.mult)
                    op = V.tensor_scalar(kv[:, c, P:P + HP], head_of[:, :], ps[:, 4 + c, P:P + 1], None, ALU.mult)
                op.then_inc(kv_ready, 1)
                for n in range(NG):
                    dve.wait_ge(v_mm, NG * b + n + 1)
                    at = gate[:, 2 * n:2 * n + 2, :]
                    V.tensor_tensor(at, pair_of_tiles(ps[:, (6 + n) % 8, :]), at, ALU.mult).then_inc(gated, 1)
                for n in range(NG):
                    dve.wait_ge(nd_mm, NG * b + n + 1)
                    two = slice((2 + 2 * n) % 8, (2 + 2 * n) % 8 + 2)
                    nd = ps[:, two, 0:DC * (P + HP)].rearrange("p j (c f) -> p j c f", c=DC)
                    V.tensor_scalar(den[:, n % 2], nd[:, :, :, P:P + HP], 1e-6, None, ALU.max).then_inc(den_clipped, 1)
                    dve.wait_ge(den_clipped, NG * b + n + 1)
                    V.reciprocal(den[:, n % 2], den[:, n % 2]).then_inc(den_inv, 1)
                    dve.wait_ge(den_inv, NG * b + n + 1)
                    for j in range(2):
                        op = V.tensor_tensor(att[:, 2 * n + j, :].rearrange("p (c h f) -> p c h f", c=DC, f=HD),
                                             nd[:, j, :, 0:P].rearrange("p c (h f) -> p c h f", f=HD),
                                             den[:, n % 2, j].unsqueeze(3).to_broadcast([P, DC, HP, HD]), ALU.mult)
                    op.then_inc(att_ready, 1)
                for n in range(NG):
                    dve.wait_ge(out_mm, NG * b + n + 1)
                    V.tensor_tensor(x_tile(b * BT + 2 * n, 2), x_tile(b * BT + 2 * n, 2), ps[:, 4 + n, :], ALU.add
                                    ).then_inc(out_added, 1)
                if not last:
                    turned_lo(b + 1, [0, 1])

            dve.wait_ge(loaded, 16 * LOADS)
            dve.wait_ge(const_ready, 6)
            sequences(dve, body)


def build(nc, t, out):
    s = Shapes(t["L0_attn_x"], t["L0_ffn_W1"])
    xn_rows = nc.dram_tensor("xn_rows", [s.N, s.D], F32, kind="Internal").ap()
    dispatched = nc.dram_tensor("dispatched", [s.MT * s.M, s.D], F32, kind="Internal").ap()
    expert_out = nc.dram_tensor("expert_out", [s.MT * s.M, s.D], F32, kind="Internal").ap()
    with ExitStack() as ctx:
        s.ctx = ctx
        constants(nc, s)
        norm_route_attend(nc, s, t["L0_attn_x"], t["L0_attn_Wq"], t["L0_attn_Wk"], t["L0_attn_Wv"],
                          t["L0_ffn_Wr"], t["L0_ffn_br"], t["L0_ffn_b1"], t["L0_ffn_W1"], t["L0_ffn_W2"],
                          xn_rows, dispatched)
        experts(nc, s, t["L0_ffn_W1"], t["L0_ffn_W2"], t["L0_ffn_b2"], dispatched, expert_out)
        combine_and_layer1(nc, s, expert_out, t["L1_attn_W_qkv"], t["L1_attn_W_out"], t["L1_ffn_W_r"],
                           t["L1_ffn_W_k"], t["L1_ffn_W_v"], t["L1_ffn_mu_r"], t["L1_ffn_mu_k"],
                           t["rope_cos"], t["rope_sin"], out)


_INS = ["L0_attn_x", "L0_attn_Wq", "L0_attn_Wk", "L0_attn_Wv", "L0_ffn_Wr", "L0_ffn_br", "L0_ffn_W1", "L0_ffn_b1",
        "L0_ffn_W2", "L0_ffn_b2", "L1_attn_W_qkv", "L1_attn_W_out", "L1_ffn_W_r", "L1_ffn_W_k", "L1_ffn_W_v",
        "L1_ffn_mu_r", "L1_ffn_mu_k"]
_HEADS, _ROPE_BASE = 16, 500000.0


def _rope_tables(T, D):
    import numpy as _np

    hd = D // _HEADS
    inv = (_np.float32(1.0) / _np.float32(_ROPE_BASE) ** (_np.arange(0, hd, 2, dtype=_np.float32) / _np.float32(hd)))
    freqs = (_np.arange(T, dtype=_np.float32)[:, None] * inv.astype(_np.float32)[None, :]).astype(_np.float32)
    cos, sin = _np.cos(freqs), _np.sin(freqs)
    return (_np.concatenate([cos, cos], axis=1).astype(_np.float32),
            _np.concatenate([-sin, sin], axis=1).astype(_np.float32))


def kernel(**inputs):
    import numpy as _np
    import concourse.bacc as _bacc
    from concourse.bass_utils import run_bass_kernel_spmd as _run

    nc = _bacc.Bacc("TRN2", target_bir_lowering=False, num_devices=1)
    _, T, D = inputs["L0_attn_x"].shape
    cos, sin = _rope_tables(T, D)
    arrays, args = {}, {}
    for name, a in [(n, inputs[n]) for n in _INS] + [("rope_cos", cos), ("rope_sin", sin)]:
        a = _np.ascontiguousarray(a)
        arrays[f"in_{name}"] = a
        args[name] = nc.dram_tensor(f"in_{name}", a.shape, mybir.dt.from_np(a.dtype), kind="ExternalInput").ap()
    out = nc.dram_tensor("out", inputs["L0_attn_x"].shape, F32, kind="ExternalOutput").ap()
    build(nc, args, out)
    r = _run(nc, [arrays], core_ids=[0])
    return r.results[0]["out"]
```

```python
from contextlib import ExitStack

import concourse.bass as bass
from concourse import mybir

F32 = mybir.dt.float32
F32R = mybir.dt.float32r
BF16 = mybir.dt.bfloat16
I32 = mybir.dt.int32
U32 = mybir.dt.uint32
ALU = mybir.AluOpType
ACT = mybir.ActivationFunctionType
X = mybir.AxisListType.X
ds = bass.ds

P = 128
EPS = 1e-5
MASKED = -1e30


def hold(eng, semaphore, value, passed):
    eng.wait_ge(semaphore, value)
    eng.sem_inc(passed, 1)


class Shapes:

    def __init__(self, x, W1):
        self.B, self.T, self.D = x.shape
        self.E, _, self.H = W1.shape
        self.N = self.B * self.T
        self.DC = self.D // P
        self.HC = self.H // P
        self.BT = self.T // P
        self.NT = self.N // P
        self.K = 2
        self.M = 256
        self.MT = (self.K * self.N + self.E * (self.M - 1)) // self.M
        assert self.DC == 2 and self.B == 4 and self.MT % 2 == 1


def constants(nc, s):
    ctx = s.ctx

    def sb(name, shape, dt=F32):
        return ctx.enter_context(nc.sbuf_tensor(name, shape, dt))

    s.x_acc = sb("x_acc", [P, s.NT * s.D])
    s.ident = sb("ident", [P, P])
    s.slots = sb("slots", [P, s.NT * s.K], U32)
    s.gates = sb("gates", [P, s.NT * s.K])
    s.tile_expert = sb("tile_expert", [P, s.MT + 1], I32)
    s.b1T = sb("b1T", [P, s.E * s.HC])
    s.eps = sb("eps", [P, 1])
    s.raw = sb("raw", [P, (s.DC * s.H + s.HC * s.D)])
    s.rows = sb("rows", [P, 2, s.M // P, s.D])
    s.shared = sb("shared", [P, 2, 8 * s.D])
    s.wqkv = s.shared[:, 0, 0:s.DC * 3 * s.D].rearrange("p (c e) -> p c e", c=s.DC)
    s.wraw = s.shared[:, 1, 0:3 * s.DC * s.D].rearrange("p (n c e) -> p n c e", n=3, c=s.DC)
    s.picked_rows = s.raw[:, 0:s.BT * s.K * s.D].rearrange("p (i k d) -> p i k d", i=s.BT, k=s.K)
    s.slot_now = sb("slot_again", [P, s.BT, s.K], U32)
    s.rows_loaded = [ctx.enter_context(nc.semaphore(f"rows_loaded{u}")) for u in range(2)]
    s.later_loaded = ctx.enter_context(nc.semaphore("later_loaded"))
    s.slot_staged = ctx.enter_context(nc.semaphore("slot_staged1"))
    s.gathered = [ctx.enter_context(nc.semaphore(f"gathered{u}")) for u in range(s.BT)]
    s.raw_loaded = [ctx.enter_context(nc.semaphore(f"raw_loaded{n}")) for n in range(2)]
    s.ps = ctx.enter_context(nc.psum_tensor("ps", [P, 8, 512], F32))


def load_rows_of_tile(sp, s, dispatched, j, u):
    sp.dma_start(s.rows[:, u], dispatched[ds(j * s.M, s.M), :].rearrange("(s p) d -> p s d", p=P)
                 ).then_inc(s.rows_loaded[u], 16)


def gather(pool, s, expert_out, b, i):
    t = b * s.BT + i
    pool.tensor_copy(s.slot_now[:, i, :], s.slots[:, s.K * t:s.K * t + s.K]).then_inc(s.slot_staged, 1)
    pool.wait_ge(s.slot_staged, t + 1)
    for k in range(s.K):
        pool.indirect_dma_start(out=s.picked_rows[:, i, k, :], out_offset=None, in_=expert_out,
                                in_offset=bass.IndirectOffsetOnAxis(ap=s.slot_now[:, i, k:k + 1], axis=0)
                                ).then_inc(s.gathered[i], 16)


def load_weights(sp, s, W1, W2, e, raw, loaded):
    n = s.DC * s.H
    sp.dma_start(raw[:, 0:n].rearrange("p (c h) -> p c h", c=s.DC),
                 W1.rearrange("e (c p) h -> e p c h", p=P)[e]).then_inc(loaded[0], 16)
    sp.dma_start(raw[:, n:].rearrange("p (k d) -> p k d", k=s.HC),
                 W2.rearrange("e (k p) d -> e p k d", p=P)[e]).then_inc(loaded[1], 16)


def norm_route_attend(nc, s, x, Wq, Wk, Wv, Wr, br, b1, W1, W2, xn_rows, dispatched):
    B, BT, NT, D, DC, E, K, T, M, MT = s.B, s.BT, s.NT, s.D, s.DC, s.E, s.K, s.T, s.M, s.MT
    ps = s.ps
    with ExitStack() as ctx:
        def sb(name, shape, dt=F32):
            return ctx.enter_context(nc.sbuf_tensor(name, shape, dt))

        def sem(name):
            return ctx.enter_context(nc.semaphore(name))

        xnT = sb("xnT", [P, DC, s.N])
        xn = s.raw[:, :].rearrange("p (u i d) -> p u i d", u=2, i=BT)
        xh, xl = sb("xh", [P, DC, T], F32R), sb("xl", [P, DC, T], F32R)
        qkh, qkl = sb("qkh", [P, 2, DC, T], F32R), sb("qkl", [P, 2, DC, T], F32R)
        vh, vl = sb("vh", [P, BT, D], F32R), sb("vl", [P, BT, D], F32R)
        wh, wl = sb("wh", [P, 3, DC, D], F32R), sb("wl", [P, 3, DC, D], F32R)
        prob = s.shared[:, 1, :].rearrange("p (u k) -> p u k", u=2)
        pTh, pTl = sb("pTh", [P, 2, BT, P], F32R), sb("pTl", [P, 2, BT, P], F32R)
        row_sum, row_inv, neg_max = sb("row_sum", [P, BT]), sb("row_inv", [P, BT]), sb("neg_max", [P, BT])
        ident_b, above = sb("ident_b", [P, P], BF16), sb("above", [P, P], BF16)
        w3 = s.shared[:, 0, 0:3 * DC * D].rearrange("p (n c e) -> p n c e", n=3, c=DC)
        earlier, ones = sb("earlier", [P, P]), sb("ones", [P, P])
        wr, brc = sb("wr", [P, DC, E]), sb("brc", [E, 1])
        lgT = sb("lgT", [E, 2, T])
        stats, mv = sb("stats", [P, NT, 6]), sb("mv", [P, NT, 2])
        std, rstd = sb("std", [P, NT]), sb("rstd", [P, NT])
        unused = sb("unused_root", [P, 1])
        b1r = sb("b1r", [E * s.HC, P])
        rest = s.shared[:, 0, 3 * DC * D:]
        logits, zero = rest[:, 0:NT * E], rest[:, NT * E:NT * E + D]
        R = [s.raw[:, n * NT * E:(n + 1) * NT * E].rearrange("p (t e) -> p t e", e=E) for n in range(10)]
        col = sb("col", [P, 8, NT])
        expert_row = sb("expert_row", [P, 6, E])
        expert_int = sb("expert_int", [P, E], I32)
        rank8, tile_no = sb("rank8", [P, E]), sb("tile_no", [P, MT + 1])
        cmp = s.raw[:, 10 * NT * E:10 * NT * E + (MT + 1) * (E - 1)].rearrange("p (j e) -> p j e", e=E - 1)
        cnt = sb("cnt", [P, MT + 1])
        xrow, slot_now = s.rows[:, :, :, :].rearrange("p u s d -> p (u s) d"), sb("slot_now", [P, 4, K], U32)

        UNITS = [(0, range(0, BT // 2)), (0, range(BT // 2, BT))] + [
            (b, range(b * BT, (b + 1) * BT)) for b in range(1, B)]
        x_loaded = [sem(f"x_loaded{n}") for n in range(len(UNITS))]
        w_loaded, small_loaded = sem("w_loaded"), sem("small_loaded")
        const_ready, zero_ready, zero_filled = sem("const_ready"), sem("zero_ready"), sem("zero_filled")
        wh_ready, wl_ready = sem("wh_ready"), sem("wl_ready")
        b1_turned, b1_ready = sem("b1_turned"), sem("b1_ready")
        stats_done, mv_done, std_done, rstd_done, xn_ready = (sem(n) for n in (
            "stats_done", "mv_done", "std_done", "rstd_done", "xn_ready"))
        xn_stored = [sem(f"xn_stored{u}") for u in range(2)]
        turned, xnT_ready, lgT_mm, lgT_ready, lg_turned, lg_ready = (sem(n) for n in (
            "turned", "xnT_ready", "lgT_mm", "lgT_ready", "lg_turned", "lg_ready"))
        step, passed = sem("step"), sem("passed")
        centered, exp_done, picked, counted, routed = (sem(n) for n in (
            "centered", "exp_done", "picked", "counted", "routed"))
        row_loaded = [sem(f"row_loaded{u}") for u in range(4)]
        slot_staged = sem("slot_staged")
        scattered = [sem(f"scattered{u}") for u in range(4)]
        xh_ready, xl_ready, proj_mm, proj_hi, proj_lo = (sem(n) for n in (
            "xh_ready", "xl_ready", "proj_mm", "proj_hi", "proj_lo"))
        score_mm, max_done, prob_ready, prob_turned, pT_hi, pT_lo, pv_mm, inv_done, attended = (sem(n) for n in (
            "score_mm", "max_done", "prob_ready", "prob_turned", "pT_hi", "pT_lo", "pv_mm", "inv_done", "attended"))

        def x_tile(t):
            return s.x_acc[:, ds(t * D, D)]

        def sequences(eng, body):
            body(0, True, False)
            with eng.Fori(1, B - 1) as b:
                body(b, False, False)
            body(B - 1, False, True)

        ORDER = (7, 6, 5, 4, 3, 2, 1, 0)
        NPROJ = 2 * DC * (T // 512) + BT // 2

        def bank_of(n):
            return 7 if n == NPROJ - 1 else (1, 3, 2, 0)[n % 4]

        block = ctx.enter_context(nc.Block())

        @block.sync
        def _(sp):
            xv = x.rearrange("b (i p) d -> b p i d", p=P)
            for n, (b, tiles) in enumerate(UNITS):
                sp.dma_start(s.x_acc[:, tiles[0] * D:(tiles[-1] + 1) * D].rearrange("p (i d) -> p i d", d=D),
                             xv[b][:, tiles[0] - b * BT:tiles[-1] + 1 - b * BT]).then_inc(x_loaded[n], 16)
                if n == 1:
                    sp.dma_start(wr[:, :, :], Wr.rearrange("(c p) e -> p c e", p=P)).then_inc(small_loaded, 16)
                    sp.dma_start(brc[:, :], br.rearrange("(e a) -> e a", a=1)).then_inc(small_loaded, 16)
                    sp.dma_start(b1r[:, :], b1.rearrange("e (c p) -> (e c) p", p=P)).then_inc(small_loaded, 16)
                if n == 2:
                    for m, w in enumerate((Wq, Wk, Wv)):
                        sp.dma_start(w3[:, m], w.rearrange("(c p) e -> p c e", p=P)).then_inc(w_loaded, 16)
            for b in range(B):
                sp.wait_ge(xn_ready, b + 2)
                sp.dma_start(xn_rows.rearrange("(b i p) d -> b p i d", b=B, p=P)[b], xn[:, b % 2]
                             ).then_inc(xn_stored[b % 2], 16)
            sp.wait_ge(zero_ready, 1)
            nz = MT * M // P
            sp.dma_start(dispatched.rearrange("(p n) d -> p n d", p=P),
                         zero[:, :].unsqueeze(1).to_broadcast([P, nz, D])).then_inc(zero_filled, 16)
            for u in range(2):
                sp.wait_ge(xn_stored[u], 16 * (B // 2))

            def load_rows(t, u):
                sp.dma_start(xrow[:, u], xn_rows[ds(t * P, P), :]).then_inc(row_loaded[u], 16)

            for u in range(4):
                load_rows(u, u)
            with sp.Fori(1, NT // 4) as g:
                for u in range(4):
                    sp.wait_ge(scattered[u], 16 * K * g)
                    load_rows(4 * g + u, u)
            sp.wait_ge(routed, 1)
            e = sp.value_load(s.tile_expert[0:1, 0:1], min_val=0, max_val=E - 1)
            load_weights(sp, s, W1, W2, e, s.raw, s.raw_loaded)
            for u in range(4):
                sp.wait_ge(scattered[u], 16 * K * (NT // 4))
            load_rows_of_tile(sp, s, dispatched, 0, 0)

        @block.gpsimd
        def _(pool):
            pool.memset(zero[:, :], 0.0).then_inc(zero_ready, 1)
            pool.memset(s.ident[:, :], 0.0).then_inc(const_ready, 1)
            pool.memset(ident_b[:, :], 0.0).then_inc(const_ready, 1)
            pool.memset(above[:, :], 0.0).then_inc(const_ready, 1)
            pool.memset(earlier[:, :], 1.0).then_inc(const_ready, 1)
            pool.memset(ones[:, :], 1.0).then_inc(const_ready, 1)
            pool.memset(s.eps[:, :], EPS).then_inc(const_ready, 1)
            pool.iota(tile_no[:, :], [[1, MT + 1]], base=0, channel_multiplier=0,
                      allow_small_or_imprecise_dtypes=True).then_inc(const_ready, 1)
            pool.iota(rank8[:, :], [[-1, E]], base=E, channel_multiplier=0,
                      allow_small_or_imprecise_dtypes=True).then_inc(const_ready, 1)
            pool.wait_ge(const_ready, 8)
            for m in (s.ident, ident_b):
                pool.affine_select(out=m[:, :], in_=m[:, :], compare_op=ALU.not_equal, fill=1.0, base=0,
                                   pattern=[[-1, P]], channel_multiplier=1).then_inc(const_ready, 1)
            pool.affine_select(out=above[:, :], in_=above[:, :], compare_op=ALU.is_ge, fill=MASKED, base=0,
                               pattern=[[-1, P]], channel_multiplier=1).then_inc(const_ready, 1)
            pool.affine_select(out=earlier[:, :], in_=earlier[:, :], compare_op=ALU.is_gt, fill=0.0, base=0,
                               pattern=[[1, P]], channel_multiplier=-1).then_inc(const_ready, 1)

            pool.wait_ge(wh_ready, 1)
            pool.tensor_tensor(wl[:, :, :, :], w3[:, :, :, :], wh[:, :, :, :].bitcast(F32), ALU.subtract
                               ).then_inc(wl_ready, 1)

            pool.wait_ge(routed, 1)
            pool.wait_ge(zero_filled, 16)

            def scatter(t, u, turn):
                if turn is not None:
                    hold(pool, scattered[u], 16 * K * turn, passed)
                pool.tensor_copy(slot_now[:, u, :], s.slots[:, ds(K * t, K)]).then_inc(slot_staged, 1)
                hold(pool, slot_staged, t + 1, passed)
                hold(pool, row_loaded[u], 16 if turn is None else 16 * turn + 16, passed)
                for k in range(K):
                    pool.indirect_dma_start(out=dispatched, out_offset=bass.IndirectOffsetOnAxis(
                        ap=slot_now[:, u, k:k + 1], axis=0), in_=xrow[:, u], in_offset=None).then_inc(scattered[u], 16)

            for u in range(4):
                scatter(u, u, None)
            with pool.Fori(1, NT // 4) as g:
                for u in range(4):
                    scatter(4 * g + u, u, g)
            for u in range(4):
                pool.wait_ge(scattered[u], 16 * K * (NT // 4))

        @block.tensor
        def _(pe):
            pe.wait_ge(const_ready, 12)
            pe.wait_ge(small_loaded, 48)
            pe.transpose(ps[:, 7, 0:E * s.HC], b1r[:, :], s.ident[0:E * s.HC, 0:E * s.HC]).then_inc(b1_turned, 1)

            def turn_tokens(b):
                for q in range(4):
                    half, c = q // 2, q % 2
                    if c == 0:
                        pe.wait_ge(xn_ready, b + 1 + (half if b == 0 else 1))
                    if b > 0:
                        pe.wait_ge(xnT_ready, 4 * b - 3 + q)
                    for i in range(4):
                        mm = pe.transpose(ps[:, q, i * P:(i + 1) * P],
                                          xn[:, b % 2, half * 4 + i, c * P:(c + 1) * P], s.ident[:, :])
                    mm.then_inc(turned, 1)

            def route(b):
                pe.wait_ge(xnT_ready, 4 * b + 4)
                if b > 0:
                    pe.wait_ge(lgT_ready, b)
                for half in range(2):
                    for c in range(DC):
                        at = b * T + half * 512
                        mm = pe.matmul(ps[0:E, 4 + half, :], wr[:, c, :], xnT[:, c, at:at + 512],
                                       start=(c == 0), stop=(c == DC - 1))
                mm.then_inc(lgT_mm, 1)

            def turn_logits(b):
                pe.wait_ge(lgT_ready, b + 1)
                if b > 0:
                    pe.wait_ge(lg_ready, b)
                for i in range(BT):
                    mm = pe.transpose(ps[:, 6, i * E:(i + 1) * E], lgT[:, b % 2, i * P:(i + 1) * P],
                                      s.ident[0:E, 0:E])
                mm.then_inc(lg_turned, 1)

            turn_tokens(0)
            route(0)
            turn_tokens(1)
            for b in range(2, B + 2):
                if b < B:
                    turn_tokens(b)
                if b <= B:
                    route(b - 1)
                turn_logits(b - 2)

            def three(out, ah, al, bh, bl, start, stop):
                pe.matmul(out, ah, bh, start=start, stop=False, skip_group_check=True)
                pe.matmul(out, ah, bl, start=False, stop=False, skip_group_check=True)
                return pe.matmul(out, al, bh, start=False, stop=stop, skip_group_check=True)

            def project(b, results):
                for n in results:
                    if n >= 4:
                        pe.wait_ge(proj_lo, NPROJ * b + n - 3)
                    bank = ps[:, bank_of(n), :]
                    if n < 2 * DC * 2:
                        w, m, half = n // 4, n // 2 % 2, n % 2
                        for c in range(DC):
                            mm = three(bank, wh[:, w, c, m * P:(m + 1) * P], wl[:, w, c, m * P:(m + 1) * P],
                                       xh[:, c, half * 512:(half + 1) * 512], xl[:, c, half * 512:(half + 1) * 512],
                                       c == 0, c == DC - 1)
                    else:
                        for j in range(2):
                            i = 2 * (n - 8) + j
                            for c in range(DC):
                                mm = three(bank[:, j * D:(j + 1) * D], xh[:, c, i * P:(i + 1) * P],
                                           xl[:, c, i * P:(i + 1) * P], wh[:, 2, c, :], wl[:, 2, c, :],
                                           c == 0, c == DC - 1)
                    mm.then_inc(proj_mm, 1)

            pe.wait_ge(wl_ready, 1)
            pe.wait_ge(xl_ready, 1)
            project(0, range(NPROJ - 1))
            pe.wait_ge(picked, 1)
            pe.matmul(ps[:, 7, 0:NT * E], earlier[:, :], R[6], start=True, stop=True)
            pe.matmul(ps[:, 6, 0:NT * E], ones[:, :], R[6], start=True, stop=True).then_inc(counted, 1)

            def attend(b, first, last):
                def scores(a):
                    i = ORDER[a]
                    if a < 2:
                        pe.wait_ge(proj_lo, NPROJ * b + 9 + 2 * a)
                    L = (i + 1) * P
                    for h in range((L + 511) // 512):
                        w = min(512, L - 512 * h)
                        bank = ps[:, 2 * (a % 2) + h, 0:w]
                        for c in range(DC):
                            qs, ks = slice(i * P, i * P + P), slice(512 * h, 512 * h + w)
                            mm = three(bank, qkh[:, 0, c, qs], qkl[:, 0, c, qs], qkh[:, 1, c, ks], qkl[:, 1, c, ks],
                                       c == 0, False)
                    mm = pe.matmul(bank[:, w - P:w], ident_b[:, :], above[:, :], start=False, stop=True,
                                   skip_group_check=True)
                    mm.then_inc(score_mm, 1)

                def turn(a):
                    pe.wait_ge(prob_ready, BT * b + a + 1)
                    if a > 0:
                        pe.wait_ge(pT_lo, BT * b + a)
                    for j in range(ORDER[a] + 1):
                        mm = pe.transpose(ps[:, 4 + j // 4, (j % 4) * P:(j % 4 + 1) * P],
                                          prob[:, a % 2, j * P:(j + 1) * P], s.ident[:, :])
                    mm.then_inc(prob_turned, 1)

                def values(a):
                    i = ORDER[a]
                    pe.wait_ge(pT_lo, BT * b + a + 1)
                    if a == 0:
                        pe.wait_ge(proj_lo, NPROJ * (b + 1))
                    pe.wait_ge(attended, BT * b + a + 1)
                    for j in range(i + 1):
                        mm = three(ps[:, 6 + a % 2, 0:D], pTh[:, a % 2, j], pTl[:, a % 2, j], vh[:, j, :], vl[:, j, :],
                                   j == 0, j == i)
                    mm.then_inc(pv_mm, 1)

                scores(0)
                for a in range(BT):
                    if a + 1 < BT:
                        scores(a + 1)
                    if a == BT - 2 and not last:
                        pe.wait_ge(xl_ready, b + 2)
                        project(b + 1, [0])
                    if a == BT - 1 and not last:
                        project(b + 1, [1])
                    turn(a)
                    if a == 0:
                        pe.wait_ge(attended, BT * b + 2)
                        project(b, [NPROJ - 1])
                    if 0 < a < BT - 1:
                        values(a - 1)
                if not last:
                    project(b + 1, range(2, 8))
                values(BT - 2)
                values(BT - 1)
                if not last:
                    project(b + 1, range(8, NPROJ - 1))

            sequences(pe, attend)

        @block.scalar
        def _(act):
            act.wait_ge(const_ready, 12)
            act.activation(unused[:, :], s.eps[:, 0:1], ACT.Sqrt)

            def deviation(n):
                act.wait_ge(mv_done, n + 1)
                at = slice(UNITS[n][1][0], UNITS[n][1][-1] + 1)
                act.activation(std[:, at], mv[:, at, 1], ACT.Sqrt, bias=s.eps[:, 0:1]).then_inc(std_done, 1)

            def turned_out(b):
                for q in range(4):
                    act.wait_ge(turned, 4 * b + q + 1)
                    at = b * T + q // 2 * 512
                    act.activation(xnT[:, q % 2, at:at + 512], ps[:, q, :], ACT.Copy).then_inc(xnT_ready, 1)

            def add_bias(b):
                act.wait_ge(lgT_mm, b + 1)
                if b > 1:
                    act.wait_ge(lg_turned, b - 1)
                act.activation(lgT[:, b % 2, :], ps[0:E, 4:6, :].rearrange("e h t -> e (h t)"), ACT.Identity,
                               bias=brc[:, 0:1]).then_inc(lgT_ready, 1)

            def logits_out(b):
                act.wait_ge(lg_turned, b + 1)
                act.activation(logits[:, b * BT * E:(b + 1) * BT * E], ps[:, 6, 0:BT * E], ACT.Copy
                               ).then_inc(lg_ready, 1)

            deviation(0)
            deviation(1)
            act.wait_ge(b1_turned, 1)
            act.activation(s.b1T[:, :], ps[:, 7, 0:E * s.HC], ACT.Copy).then_inc(b1_ready, 1)
            act.wait_ge(small_loaded, 48)
            turned_out(0)
            deviation(2)
            add_bias(0)
            act.wait_ge(w_loaded, 48)
            act.activation(wh[:, :, :, :], w3[:, :, :, :], ACT.Copy).then_inc(wh_ready, 1)
            deviation(3)
            turned_out(1)
            act.activation(xh[:, :, :], xnT[:, :, 0:T], ACT.Copy).then_inc(xh_ready, 1)
            for b in range(2, B + 2):
                if b + 2 < len(UNITS):
                    deviation(b + 2)
                if b < B:
                    turned_out(b)
                if b <= B:
                    add_bias(b - 1)
                logits_out(b - 2)

            def project_hi(b, results):
                for n in results:
                    act.wait_ge(proj_mm, NPROJ * b + n + 1)
                    if n < 8:
                        act.activation(qkh[:, n // 4, n // 2 % 2, n % 2 * 512:(n % 2 + 1) * 512], ps[:, bank_of(n), :],
                                       ACT.Copy, scale=D ** -0.5 if n < 4 else 1.0).then_inc(proj_hi, 1)
                    else:
                        act.activation(vh[:, 2 * (n - 8):2 * (n - 8) + 2, :],
                                       ps[:, bank_of(n), :].rearrange("p (j d) -> p j d", j=2), ACT.Copy
                                       ).then_inc(proj_hi, 1)

            act.wait_ge(centered, 1)
            act.activation(R[1], R[0], ACT.Exp).then_inc(exp_done, 1)
            project_hi(0, range(NPROJ - 1))

            def attend(b, first, last):
                def softmax(a):
                    i = ORDER[a]
                    act.wait_ge(max_done, BT * b + a + 1)
                    L = (i + 1) * P
                    act.activation(prob[:, a % 2, 0:L], ps[:, 2 * (a % 2):2 * (a % 2) + 2, :].rearrange(
                        "p h k -> p (h k)")[:, 0:L], ACT.Exp, bias=neg_max[:, i:i + 1],
                        accum_out=row_sum[:, i:i + 1]).then_inc(prob_ready, 1)

                def turned_hi(a):
                    act.wait_ge(prob_turned, BT * b + a + 1)
                    act.wait_ge(attended, BT * b + a + 1)
                    L = (ORDER[a] + 1) * P
                    act.activation(pTh[:, a % 2, 0:ORDER[a] + 1, :].rearrange("p j q -> p (j q)"),
                                   ps[:, 4:6, :].rearrange("p h k -> p (h k)")[:, 0:L], ACT.Copy).then_inc(pT_hi, 1)

                softmax(0)
                for a in range(BT):
                    if a + 1 < BT:
                        softmax(a + 1)
                    turned_hi(a)
                    if a == 0:
                        project_hi(b, [NPROJ - 1])
                    if a == 1 and not last:
                        act.activation(xh[:, :, :], xnT[:, :, ds((b + 1) * T, T)], ACT.Copy).then_inc(xh_ready, 1)
                if not last:
                    project_hi(b + 1, range(NPROJ - 1))

            sequences(act, attend)

        @block.vector
        def _(dve):
            V = nc.vector
            dve.sem_inc(attended, 2)
            dve.wait_ge(const_ready, 12)

            def statistics(n):
                dve.wait_ge(x_loaded[n], 16)
                for t in UNITS[n][1]:
                    op = V.bn_stats(stats[:, t, :], x_tile(t))
                op.then_inc(stats_done, 1)
                dve.wait_ge(stats_done, n + 1)
                for t in UNITS[n][1]:
                    op = V.bn_aggr(mv[:, t, :], stats[:, t, :])
                op.then_inc(mv_done, 1)

            def normalize(n):
                b, tiles = UNITS[n]
                dve.wait_ge(std_done, n + 1)
                at = slice(tiles[0], tiles[-1] + 1)
                V.reciprocal(rstd[:, at], std[:, at]).then_inc(rstd_done, 1)
                dve.wait_ge(rstd_done, n + 1)
                if b >= 2:
                    dve.wait_ge(turned, 4 * (b - 1))
                    dve.wait_ge(xn_stored[b % 2], 16)
                for t in tiles:
                    op = V.tensor_scalar(xn[:, b % 2, t % BT, :], x_tile(t), mv[:, t, 0:1], rstd[:, t:t + 1],
                                         ALU.subtract, ALU.mult)
                op.then_inc(xn_ready, 1)

            statistics(0)
            statistics(1)
            normalize(0)
            normalize(1)
            statistics(2)
            for n in range(2, len(UNITS)):
                if n + 1 < len(UNITS):
                    statistics(n + 1)
                if n == len(UNITS) - 1:
                    dve.wait_ge(xh_ready, 1)
                    V.tensor_tensor(xl[:, :, :], xnT[:, :, 0:T], xh[:, :, :].bitcast(F32), ALU.subtract
                                    ).then_inc(xl_ready, 1)
                normalize(n)

            steps = [0]

            def then(op):
                steps[0] += 1
                op.then_inc(step, 1)
                dve.wait_ge(step, steps[0])

            def per_tile(a):
                return a.unsqueeze(2).to_broadcast([P, NT, E])

            def per_expert(a):
                return a.unsqueeze(1).to_broadcast([P, NT, E])

            def project_lo(b, results):
                for n in results:
                    dve.wait_ge(proj_hi, NPROJ * b + n + 1)
                    if n < 8:
                        at = (slice(None), n // 4, n // 2 % 2, slice(n % 2 * 512, (n % 2 + 1) * 512))
                        V.scalar_tensor_tensor(qkl[at], ps[:, bank_of(n), :], D ** -0.5 if n < 4 else 1.0,
                                               qkh[at].bitcast(F32), ALU.mult, ALU.subtract).then_inc(proj_lo, 1)
                    else:
                        at = (slice(None), slice(2 * (n - 8), 2 * (n - 8) + 2), slice(None))
                        V.tensor_tensor(vl[at], ps[:, bank_of(n), :].rearrange("p (j d) -> p j d", j=2),
                                        vh[at].bitcast(F32), ALU.subtract).then_inc(proj_lo, 1)


            lg = logits[:, :].rearrange("p (t e) -> p t e", e=E)
            dve.wait_ge(lg_ready, B)
            dve.wait_ge(turned, 4 * B)
            for u in range(2):
                dve.wait_ge(xn_stored[u], 16 * (B // 2))
            then(V.tensor_reduce(col[:, 0, :], lg, X, ALU.max))
            V.tensor_tensor(R[0], lg, per_tile(col[:, 0, :]), ALU.subtract).then_inc(centered, 1)
            dve.wait_ge(exp_done, 1)
            then(V.tensor_reduce(col[:, 1, :], R[1], X, ALU.add))
            then(V.reciprocal(col[:, 2, :], col[:, 1, :]))
            then(V.tensor_tensor(R[2], R[1], per_tile(col[:, 2, :]), ALU.mult))

            def pick(p, best, one_hot, scratch, key):
                then(V.tensor_reduce(best, p, X, ALU.max))
                then(V.tensor_tensor(scratch, p, per_tile(best), ALU.is_equal))
                then(V.tensor_tensor(scratch, scratch, per_expert(rank8[:, :]), ALU.mult))
                then(V.tensor_reduce(key, scratch, X, ALU.max))
                then(V.tensor_tensor(one_hot, scratch, per_tile(key), ALU.is_equal))

            project_lo(0, range(0, 2))
            pick(R[2], col[:, 3, :], R[3], R[0], col[:, 4, :])
            project_lo(0, range(2, 5))
            then(V.scalar_tensor_tensor(R[1], R[3], -4.0, R[2], ALU.mult, ALU.add))
            pick(R[1], col[:, 5, :], R[4], R[0], col[:, 4, :])
            V.tensor_tensor(R[6], R[3], R[4], ALU.add).then_inc(picked, 1)
            project_lo(0, range(5, 8))
            then(V.tensor_tensor(col[:, 6, :], col[:, 3, :], col[:, 5, :], ALU.add))
            then(V.reciprocal(col[:, 7, :], col[:, 6, :]))
            gv = s.gates[:, :].rearrange("p (t k) -> p t k", k=K)
            then(V.tensor_tensor(gv[:, :, 0], col[:, 3, :], col[:, 7, :], ALU.mult))
            then(V.tensor_tensor(gv[:, :, 1], col[:, 5, :], col[:, 7, :], ALU.mult))
            then(V.memset(col[:, 0, :], 1.0))
            project_lo(0, range(8, NPROJ - 1))
            dve.wait_ge(counted, 1)
            V.tensor_copy(R[8], ps[:, 6, 0:NT * E].rearrange("p (t e) -> p t e", e=E))
            then(V.tensor_copy(R[9], ps[:, 7, 0:NT * E].rearrange("p (t e) -> p t e", e=E)))

            def rank():
                total = R[8]
                for e in range(E):
                    op = V.tensor_tensor_scan(R[5][:, :, e], col[:, 0, :], total[:, :, e], 0.0, ALU.mult, ALU.add)
                then(op)
                then(V.tensor_tensor(R[7], R[5], total, ALU.subtract))

            def place_experts():
                then(V.tensor_scalar(expert_int[:, :], R[5][:, NT - 1, :], float(M - 1), None, ALU.add))
                then(V.tensor_scalar(expert_int[:, :], expert_int[:, :], M.bit_length() - 1, None, ALU.arith_shift_right))
                then(V.tensor_copy(expert_row[:, 0, :], expert_int[:, :]))
                then(V.memset(expert_row[:, 1, :], 1.0))
                then(V.tensor_tensor_scan(expert_row[:, 2, :], expert_row[:, 1, :], expert_row[:, 0, :], 0.0,
                                          ALU.mult, ALU.add))
                then(V.tensor_tensor(expert_row[:, 3, :], expert_row[:, 2, :], expert_row[:, 0, :], ALU.subtract))
                then(V.tensor_scalar(expert_row[:, 4, :], expert_row[:, 3, :], float(M), None, ALU.mult))

            def place_tokens(k):
                if k == 0:
                    then(V.tensor_tensor(R[7], R[7], per_expert(expert_row[:, 4, :]), ALU.add))
                    then(V.tensor_tensor(R[7], R[7], R[9], ALU.add))
                sv = s.slots[:, :].rearrange("p (t k) -> p t k", k=K)
                then(V.tensor_tensor(R[0], R[7], R[3 + k], ALU.mult))
                then(V.tensor_reduce(col[:, 1, :], R[0], X, ALU.add))
                then(V.tensor_copy(sv[:, :, k], col[:, 1, :]))

            def tiles_of_experts():
                then(V.tensor_tensor(cmp[:, :, :], tile_no[:, :].unsqueeze(2).to_broadcast([P, MT + 1, E - 1]),
                                     expert_row[:, 2, 0:E - 1].unsqueeze(1).to_broadcast([P, MT + 1, E - 1]), ALU.is_ge))
                then(V.tensor_reduce(cnt[:, :], cmp[:, :, :], X, ALU.add))
                V.tensor_copy(s.tile_expert[:, :], cnt[:, :]).then_inc(routed, 1)

            def attend(b, first, last):
                def row_max(a):
                    i = ORDER[a]
                    dve.wait_ge(score_mm, BT * b + a + 1)
                    L = (i + 1) * P
                    V.tensor_reduce(neg_max[:, i:i + 1], ps[:, 2 * (a % 2):2 * (a % 2) + 2, :].rearrange(
                        "p h k -> p (h k)")[:, 0:L], X, ALU.max, negate=True).then_inc(max_done, 1)

                def turned_lo(a):
                    dve.wait_ge(pT_hi, BT * b + a + 1)
                    n = ORDER[a] + 1
                    V.tensor_tensor(pTl[:, a % 2, 0:n, :].rearrange("p j q -> p (j q)"),
                                    ps[:, 4:6, :].rearrange("p h k -> p (h k)")[:, 0:n * P],
                                    pTh[:, a % 2, 0:n, :].rearrange("p j q -> p (j q)").bitcast(F32),
                                    ALU.subtract).then_inc(pT_lo, 1)

                def add_attention(a):
                    i = ORDER[a]
                    V.reciprocal(row_inv[:, i:i + 1], row_sum[:, i:i + 1]).then_inc(inv_done, 1)
                    dve.wait_ge(inv_done, BT * b + a + 1)
                    dve.wait_ge(pv_mm, BT * b + a + 1)
                    V.scalar_tensor_tensor(x_tile(b * BT + i), ps[:, 6 + a % 2, 0:D], row_inv[:, i:i + 1],
                                           x_tile(b * BT + i), ALU.mult, ALU.add).then_inc(attended, 1)

                row_max(0)
                for a in range(BT):
                    if a + 1 < BT:
                        row_max(a + 1)
                    if first and a == 0:
                        rank()
                    if first and a == 1:
                        place_experts()
                    if first and a in (2, 3):
                        place_tokens(a - 2)
                    if first and a == 4:
                        tiles_of_experts()
                    if a in (2, 3) and not last:
                        c = a - 2
                        dve.wait_ge(xh_ready, b + 2)
                        op = V.tensor_tensor(xl[:, c, :], xnT[:, c, ds((b + 1) * T, T)], xh[:, c, :].bitcast(F32),
                                             ALU.subtract)
                        if c:
                            op.then_inc(xl_ready, 1)
                    turned_lo(a)
                    if a == 0:
                        project_lo(b, [NPROJ - 1])
                    if 0 < a < BT - 1:
                        add_attention(a - 1)
                if not last:
                    project_lo(b + 1, range(8))
                add_attention(BT - 2)
                add_attention(BT - 1)
                if not last:
                    project_lo(b + 1, range(8, NPROJ - 1))

            sequences(dve, attend)


def experts(nc, s, W1, W2, b2, W_qkv, W_r, W_k, W_v, dispatched, expert_out):
    D, DC, E, H, HC, M, MT = s.D, s.DC, s.E, s.H, s.HC, s.M, s.MT
    MS = M // P
    NQ = HC // 2
    ps = s.ps
    with ExitStack() as ctx:
        def sb(name, shape, dt=F32):
            return ctx.enter_context(nc.sbuf_tensor(name, shape, dt))

        def sem(name):
            return ctx.enter_context(nc.semaphore(name))

        raw = [s.raw, sb("raw_odd", [P, DC * H + HC * D])]
        w1raw = [r[:, 0:DC * H].rearrange("p (c h) -> p c h", c=DC) for r in raw]
        w2raw = [r[:, DC * H:].rearrange("p (k d) -> p k d", k=HC) for r in raw]
        w1h, w1l = sb("w1h", [P, 2, DC, H], F32R), sb("w1l", [P, 2, DC, H], F32R)
        w2h, w2l = sb("w2h", [P, 2, HC, D], F32R), sb("w2l", [P, 2, HC, D], F32R)
        rows = s.rows
        xTh, xTl = sb("xTh", [P, DC, M], F32R), sb("xTl", [P, DC, M], F32R)
        h32 = sb("h32", [P, HC, M])
        hh, hl = sb("hh", [P, HC, M], F32R), sb("hl", [P, HC, M], F32R)
        y = sb("y", [P, 2, MS, D])
        b2all = sb("b2all", [P, E * D])

        b2_loaded, passed = sem("b2_loaded"), sem("passed")
        rows_loaded = s.rows_loaded
        w1_loaded = [s.raw_loaded[0], sem("w1_loaded_odd")]
        w2_loaded = [s.raw_loaded[1], sem("w2_loaded_odd")]
        y_stored = [sem(f"y_stored{u}") for u in range(2)]
        last_stored = sem("last_stored")
        w1_hi, w1_lo, w2_hi, w2_lo = sem("w1_hi"), sem("w1_lo"), sem("w2_hi"), sem("w2_lo")
        rows_turned, xT_hi, xT_lo = sem("rows_turned"), sem("xT_hi"), sem("xT_lo")
        up_mm, relu_done, h_hi, h_lo, down_mm, y_done = (sem(n) for n in (
            "up_mm", "relu_done", "h_hi", "h_lo", "down_mm", "y_done"))

        def tiles(eng, body):
            body(0, 0)
            body(0, 1)
            with eng.Fori(1, MT // 2) as g:
                body(g, 0)
                body(g, 1)
            body(MT // 2, 0)

        def is_last(g, u):
            return isinstance(g, int) and 2 * g + u == MT - 1

        def following(g, u):
            return (g, 1) if u == 0 else (g + 1, 0)

        def first(g):
            return isinstance(g, int) and g == 0

        def expert_of(eng, g, u):
            return eng.value_load(s.tile_expert[0:1, ds(2 * g + u, 1)], min_val=0, max_val=E - 1)

        block = ctx.enter_context(nc.Block())

        @block.sync
        def _(sp):
            def load(g, u):
                j = 2 * g + u
                e = expert_of(sp, g, u)
                if not first(g):
                    sp.wait_ge(rows_turned, j - 1)
                if not (isinstance(g, int) and j == 0):
                    load_rows_of_tile(sp, s, dispatched, j, u)
                if not first(g):
                    sp.wait_ge(w1_lo, NQ * (j - 1))
                    sp.wait_ge(w2_lo, NQ * (j - 1))
                if not (isinstance(g, int) and j == 0):
                    load_weights(sp, s, W1, W2, e, raw[u], (w1_loaded[u], w2_loaded[u]))
                if isinstance(g, int) and j == 1:
                    sp.dma_start(b2all[:, :], b2.rearrange("e d -> (e d)").partition_broadcast(P)
                                 ).then_inc(b2_loaded, 16)
                    sp.dma_start(s.wqkv, W_qkv.rearrange("(c p) e -> p c e", p=P)).then_inc(s.later_loaded, 16)
                    for n, w in enumerate((W_r, W_k, W_v)):
                        sp.dma_start(s.wraw[:, n], w.rearrange("(c p) e -> p c e", p=P)
                                     ).then_inc(s.later_loaded, 16)

            tiles(sp, load)
            j = MT - 1
            sp.wait_ge(y_done, MT)
            sp.dma_start(expert_out[j * M:MT * M, :].rearrange("(s p) d -> p s d", p=P), y[:, 0]
                         ).then_inc(last_stored, 16)
            sp.wait_ge(last_stored, 16)

        @block.gpsimd
        def _(pool):
            def split(g, u, q):
                pool.tensor_copy(w2h[:, u, 2 * q:2 * q + 2, :], w2raw[u][:, 2 * q:2 * q + 2, :]).then_inc(w2_hi, 1)

            def store(g, u):
                j = 2 * g + u
                hold(pool, y_done, j + 1, passed)
                pool.dma_start(expert_out[ds(j * M, M), :].rearrange("(s p) d -> p s d", p=P), y[:, u]
                               ).then_inc(y_stored[u], 16)

            pool.wait_ge(w2_loaded[0], 16)
            for q in range(NQ):
                split(0, 0, q)

            def body(g, u):
                if not is_last(g, u):
                    ng, nu = following(g, u)
                    hold(pool, w2_loaded[nu], 16 * ng + 16, passed)
                    if not (isinstance(g, int) and 2 * g + u == 0):
                        hold(pool, down_mm, 2 * g + u, passed)
                    for q in range(NQ):
                        split(ng, nu, q)
                if not is_last(g, u):
                    store(g, u)

            tiles(pool, body)
            for u in range(2):
                pool.wait_ge(y_stored[u], 16 * (MT // 2))

        @block.tensor
        def _(pe):
            def three(out, ah, al, bh, bl, start, stop):
                pe.matmul(out, ah, bh, start=start, stop=False, skip_group_check=True)
                pe.matmul(out, ah, bl, start=False, stop=False, skip_group_check=True)
                return pe.matmul(out, al, bh, start=False, stop=stop, skip_group_check=True)

            def turn_rows(g, u):
                pe.wait_ge(rows_loaded[u], 16 * g + 16)
                for c in range(DC):
                    for part in range(MS):
                        mm = pe.transpose(ps[:, 6, c * M + part * P:c * M + (part + 1) * P],
                                          rows[:, u, part, c * P:(c + 1) * P], s.ident[:, :])
                mm.then_inc(rows_turned, 1)

            turn_rows(0, 0)

            def body(g, u):
                j = 2 * g + u
                pe.wait_ge(xT_lo, j + 1)
                for q in range(NQ):
                    pe.wait_ge(w1_lo, NQ * j + q + 1)
                    for k in (2 * q, 2 * q + 1):
                        for c in range(DC):
                            ws = slice(k * P, (k + 1) * P)
                            mm = three(ps[:, q, (k % 2) * M:(k % 2 + 1) * M], w1h[:, u, c, ws], w1l[:, u, c, ws],
                                       xTh[:, c, :], xTl[:, c, :], c == 0, c == DC - 1)
                    mm.then_inc(up_mm, 1)
                if not is_last(g, u):
                    turn_rows(*following(g, u))
                if not (isinstance(g, int) and j == 0):
                    pe.wait_ge(y_done, j)
                for k in range(HC):
                    if k % 2 == 0:
                        pe.wait_ge(h_lo, NQ * j + k // 2 + 1)
                        pe.wait_ge(w2_lo, NQ * j + k // 2 + 1)
                    for part in range(MS):
                        bank = 5 if part else 4
                        rs = slice(part * P, (part + 1) * P)
                        mm = three(ps[:, bank, 0:D], hh[:, k, rs], hl[:, k, rs], w2h[:, u, k, :], w2l[:, u, k, :],
                                   k == 0, k == HC - 1)
                mm.then_inc(down_mm, 1)

            tiles(pe, body)

        @block.scalar
        def _(act):
            def split(g, u, q):
                cols = slice(q * H // NQ, (q + 1) * H // NQ)
                act.activation(w1h[:, u, :, cols], w1raw[u][:, :, cols], ACT.Copy).then_inc(w1_hi, 1)

            def turned_hi(g, u):
                act.wait_ge(rows_turned, 2 * g + u + 1)
                act.activation(xTh[:, :, :], ps[:, 6, :].rearrange("p (c m) -> p c m", c=DC), ACT.Copy
                               ).then_inc(xT_hi, 1)

            act.wait_ge(w1_loaded[0], 16)
            split(0, 0, 0)
            turned_hi(0, 0)
            for q in range(1, NQ):
                split(0, 0, q)

            def body(g, u):
                j = 2 * g + u
                e = expert_of(act, g, u)
                ng, nu = following(g, u)
                for q in range(NQ):
                    act.wait_ge(up_mm, NQ * j + q + 1)
                    for k in (2 * q, 2 * q + 1):
                        op = act.activation(h32[:, k, :], ps[:, q, (k % 2) * M:(k % 2 + 1) * M], ACT.Relu,
                                            bias=s.b1T[:, ds(e * HC + k, 1)])
                    op.then_inc(relu_done, 1)
                    act.wait_ge(relu_done, NQ * j + q + 1)
                    act.activation(hh[:, 2 * q:2 * q + 2, :], h32[:, 2 * q:2 * q + 2, :], ACT.Copy).then_inc(h_hi, 1)
                    if not is_last(g, u) and q > 0:
                        if q == 1:
                            act.wait_ge(w1_loaded[nu], 16 * ng + 16)
                        if q == NQ - 1:
                            turned_hi(ng, nu)
                        split(ng, nu, q - 1)
                if not is_last(g, u):
                    split(ng, nu, NQ - 1)

            tiles(act, body)

        @block.vector
        def _(dve):
            V = nc.vector

            def split1(g, u, q):
                dve.wait_ge(w1_hi, NQ * (2 * g + u) + q + 1)
                cols = slice(q * H // NQ, (q + 1) * H // NQ)
                V.tensor_tensor(w1l[:, u, :, cols], w1raw[u][:, :, cols], w1h[:, u, :, cols].bitcast(F32),
                                ALU.subtract).then_inc(w1_lo, 1)

            def split2(g, u, q):
                dve.wait_ge(w2_hi, NQ * (2 * g + u) + q + 1)
                ks = slice(2 * q, 2 * q + 2)
                V.tensor_tensor(w2l[:, u, ks], w2raw[u][:, ks], w2h[:, u, ks].bitcast(F32), ALU.subtract
                                ).then_inc(w2_lo, 1)

            def turned_lo(g, u):
                dve.wait_ge(xT_hi, 2 * g + u + 1)
                V.tensor_tensor(xTl[:, :, :], ps[:, 6, :].rearrange("p (c m) -> p c m", c=DC),
                                xTh[:, :, :].bitcast(F32), ALU.subtract).then_inc(xT_lo, 1)

            split1(0, 0, 0)
            turned_lo(0, 0)
            for q in range(1, NQ):
                split1(0, 0, q)
            for q in range(NQ):
                split2(0, 0, q)

            def body(g, u):
                j = 2 * g + u
                e = expert_of(dve, g, u)
                ng, nu = following(g, u)
                for q in range(NQ):
                    dve.wait_ge(h_hi, NQ * j + q + 1)
                    at = (slice(None), slice(2 * q, 2 * q + 2), slice(None))
                    V.tensor_tensor(hl[at], h32[at], hh[at].bitcast(F32), ALU.subtract).then_inc(h_lo, 1)
                    if not is_last(g, u) and q > 0:
                        if q == NQ - 1:
                            turned_lo(ng, nu)
                        split1(ng, nu, q - 1)
                        if q > 1:
                            split2(ng, nu, q - 2)
                if not is_last(g, u):
                    split2(ng, nu, NQ - 2)
                    split1(ng, nu, NQ - 1)
                    split2(ng, nu, NQ - 1)
                dve.wait_ge(down_mm, j + 1)
                if first(g):
                    dve.wait_ge(b2_loaded, 16)
                else:
                    dve.wait_ge(y_stored[u], 16 * g)
                for part in range(MS):
                    op = V.tensor_tensor(y[:, u, part, :], ps[:, 4 + part, 0:D], b2all[:, ds(e * D, D)], ALU.add)
                op.then_inc(y_done, 1)

            tiles(dve, body)


def combine_and_layer1(nc, s, expert_out, W_out, mu_r, mu_k, rope_cos, rope_sin, out):
    B, BT, D, DC, T, K = s.B, s.BT, s.D, s.DC, s.T, s.K
    HD = rope_cos.shape[1]
    HP = P // HD
    NG = BT // 2
    LOADS = 1 + 2 * DC + 2
    HB = T // 2
    ps = s.ps
    with ExitStack() as ctx:
        def sb(name, shape, dt=F32):
            return ctx.enter_context(nc.sbuf_tensor(name, shape, dt))

        def sem(name):
            return ctx.enter_context(nc.semaphore(name))

        stats, mv = sb("stats1", [P, BT, 6]), sb("mv1", [P, BT, 2])
        std, rstd, shift = sb("std1", [P, BT]), sb("rstd1", [P, BT]), sb("shift1", [P, BT])
        unused = sb("unused", [P, 1])
        xn = sb("xn1", [P, BT, D])
        xnT = sb("xnT1", [P, DC, T + 1])
        step_T = sb("step_T", [P, DC, T])
        xrT, xkT = sb("xrT", [P, DC, T]), sb("xkT", [P, DC, T])
        qk = sb("qk", [P, 2, 2, 2 * D])
        rot, straight = (s.shared[:, n, :].rearrange("p (u j d) -> p u j d", u=2, j=2) for n in range(2))
        feat = sb("feat", [P, BT, 2 * D])
        v1 = sb("v1", [P, BT, DC, P + 1])
        oT = sb("oT", [P, DC, T])
        qT, act_k = xkT, step_T
        gate = sb("gate", [P, BT, D])
        kv = sb("kv", [P, DC, P + HP])
        att = sb("att", [P, BT, D])
        same_head, head_of = sb("same_head", [P, P]), sb("head_of", [P, HP])
        wout = sb("wout", [P, DC, D])
        wqkvh, wqkvl = sb("wqkvh", [P, DC, 3 * D], F32R), sb("wqkvl", [P, DC, 3 * D], F32R)
        xh, xl = sb("xh1", [P, DC, T], F32R), sb("xl1", [P, DC, T], F32R)
        wT = sb("wT", [P, 3, DC, D])
        mu = sb("mu", [P, 2, DC])
        cos, sin = sb("cos", [P, BT, HD]), sb("sin", [P, BT, HD])
        den = sb("den", [P, 2, 2, DC, HP])

        loaded, const_ready, weights_turned, weights_ready, passed = (sem(n) for n in (
            "loaded", "const_ready1", "weights_turned", "weights_ready", "passed1"))
        first_added, combined = sem("first_added"), sem("combined")
        stats_done, mv_done, std_done, rstd_done, shift_done, xn_ready = (sem(n) for n in (
            "stats_done1", "mv_done1", "std_done1", "rstd_done1", "shift_done1", "xn_ready1"))
        turned, xnT_ready, step_ready = sem("turned1"), sem("xnT_ready1"), sem("step_ready")
        k_mixed, r_mixed = sem("k_mixed"), sem("r_mixed")
        qkv_mm, qkv_out, rotated, straight_done, summed, clipped, exp_done, feat_done = (sem(n) for n in (
            "qkv_mm", "qkv_out", "rotated", "straight_done", "summed", "clipped", "exp_done1", "feat_done"))
        k_mm, k_out, squared, r_mm, gate_ready = (sem(n) for n in ("k_mm", "k_out", "squared", "r_mm", "gate_ready"))
        qT_mm, qT_ready, kv_mm, kv_ready, v_mm, gated = (sem(n) for n in (
            "qT_mm", "qT_ready", "kv_mm", "kv_ready", "v_mm", "gated"))
        nd_mm, den_clipped, den_inv, att_ready, att_turned, oT_ready = (sem(n) for n in (
            "nd_mm", "den_clipped", "den_inv", "att_ready", "att_turned", "oT_ready"))
        wh_ready, wl_ready, xh_ready, xl_ready = (sem(n) for n in ("wh_ready1", "wl_ready1", "xh_ready1", "xl_ready1"))
        out_mm, out_added, final, stored = (sem(n) for n in ("out_mm", "out_added", "final", "stored"))

        def x_tile(t, n=1):
            return s.x_acc[:, ds(t * D, n * D)]

        def pair_of_tiles(bank):
            return bank.rearrange("p (j d) -> p j d", j=2)

        def sequences(eng, body):
            body(0, True, False)
            with eng.Fori(1, B - 1) as b:
                body(b, False, False)
            body(B - 1, False, True)

        def units(b):
            if isinstance(b, int) and b == 0:
                return [(2 * u, 2, u + 1) for u in range(4)]
            return [(4 * h, 4, 2 * b + h + 3) for h in range(2)]

        def turns(b, u):
            i, size, count = units(b)[u]
            first_bank = (0, 2, 2, 5)[u] if size == 2 else 2 * u
            return [(c, first_bank + c, slice(i % 4 * P, (i % 4 + size) * P), slice(i * P, (i + size) * P),
                     2 * (count - 1) + c + 1) for c in range(DC)]

        def all_turned(b):
            return 2 * units(b)[-1][2]

        block = ctx.enter_context(nc.Block())

        @block.sync
        def _(sp):
            sp.dma_start(wout[:, :, :], W_out.rearrange("(c p) e -> p c e", p=P)).then_inc(loaded, 16)
            for n, m in enumerate((mu_r, mu_k)):
                for c in range(DC):
                    sp.dma_start(mu[:, n, c:c + 1], m[c * P:(c + 1) * P].rearrange("(p a) -> p a", a=1)
                                 ).then_inc(loaded, 16)
            sp.dma_start(cos[:, :, :], rope_cos.rearrange("(i p) f -> p i f", p=P)).then_inc(loaded, 16)
            sp.dma_start(sin[:, :, :], rope_sin.rearrange("(i p) f -> p i f", p=P)).then_inc(loaded, 16)
            with sp.Fori(0, B) as b:
                sp.wait_ge(final, NG * b + NG)
                sp.dma_start(out.rearrange("b (i p) d -> b p i d", p=P)[b],
                             x_tile(b * BT, BT).rearrange("p (i d) -> p i d", d=D)).then_inc(stored, 16)
            sp.wait_ge(stored, 16 * B)

        @block.gpsimd
        def _(pool):
            def gather_sequence(b):
                for start, size, count in units(b - 1):
                    pool.wait_ge(combined, count)
                    for i in range(start, start + size):
                        gather(pool, s, expert_out, b, i)

            pool.memset(same_head[:, :], 1.0).then_inc(const_ready, 1)
            pool.memset(xnT[:, :, 0:1], 0.0).then_inc(const_ready, 1)
            pool.memset(v1[:, :, :, P:P + 1], 1.0).then_inc(const_ready, 1)
            for i in range(BT // 2):
                gather(pool, s, expert_out, 0, i)
            heads = same_head[:, :].rearrange("p (h f) -> p h f", f=HD)
            pool.wait_ge(const_ready, 3)
            pool.affine_select(out=heads, in_=heads, compare_op=ALU.is_ge, fill=0.0, base=0,
                               pattern=[[-HD, HP], [0, HD]], channel_multiplier=1).then_inc(const_ready, 1)
            pool.wait_ge(const_ready, 4)
            pool.affine_select(out=heads, in_=heads, compare_op=ALU.is_gt, fill=0.0, base=HD,
                               pattern=[[HD, HP], [0, HD]], channel_multiplier=-1).then_inc(const_ready, 1)
            pool.wait_ge(const_ready, 5)
            pool.tensor_copy(head_of[:, :], heads[:, :, 0]).then_inc(const_ready, 1)
            for i in range(BT // 2, BT):
                gather(pool, s, expert_out, 0, i)

            def rotate(b):
                for n in range(NG):
                    if n == (2 if b == 0 else 0):
                        pool.wait_ge(xnT_ready, all_turned(b))
                        pool.tensor_tensor(step_T[:, :, :], xnT[:, :, 1:T + 1], xnT[:, :, 0:T], ALU.subtract
                                           ).then_inc(step_ready, 1)
                    pool.wait_ge(qkv_out, NG * b + n + 1)
                    src = qk[:, n % 2].rearrange("p j (h f) -> p j h f", f=HD)
                    dst = rot[:, n % 2].rearrange("p j (h f) -> p j h f", f=HD)
                    for half in range(2):
                        to = slice(half * HD // 2, (half + 1) * HD // 2)
                        fro = slice((1 - half) * HD // 2, (2 - half) * HD // 2)
                        table = sin[:, 2 * n:2 * n + 2, to].unsqueeze(2).to_broadcast([P, 2, 2 * D // HD, HD // 2])
                        op = pool.tensor_tensor(dst[:, :, :, to], src[:, :, :, fro], table, ALU.mult)
                    op.then_inc(rotated, 1)

            def finish(b):
                for n in range(NG):
                    pool.wait_ge(out_added, NG * b + n + 1 + NG)
                    pool.tensor_tensor(x_tile(b * BT + 2 * n, 2), x_tile(b * BT + 2 * n, 2),
                                       gate[:, 2 * n:2 * n + 2, :].rearrange("p j d -> p (j d)"), ALU.add
                                       ).then_inc(final, 1)

            pool.wait_ge(loaded, 16 * LOADS)
            for b in range(B):
                rotate(b)
                for ahead in ((1, 2) if b == 0 else (b + 2,)):
                    if ahead < B:
                        gather_sequence(ahead)
                finish(b)

        @block.tensor
        def _(pe):
            pe.wait_ge(s.later_loaded, 16 * 4)
            for n in range(3):
                for c in range(DC):
                    for d in range(DC):
                        mm = pe.transpose(ps[:, 4 + n, c * D + d * P:c * D + (d + 1) * P],
                                          s.wraw[:, n, d, c * P:(c + 1) * P], s.ident[:, :])
            mm.then_inc(weights_turned, 1)
            pe.wait_ge(weights_ready, 1)

            def turn(b, u):
                i, size, count = units(b)[u]
                hold(pe, xn_ready, count, passed)
                for c, bank, cols, _, _ in turns(b, u):
                    for k in range(size):
                        mm = pe.transpose(ps[:, bank, cols.start + k * P:cols.start + (k + 1) * P],
                                          xn[:, i + k, c * P:(c + 1) * P], s.ident[:, :])
                    mm.then_inc(turned, 1)

            def product(dst, lhsT, rhs):
                pe.matmul(dst, lhsT(0), rhs(0), start=True, stop=False)
                return pe.matmul(dst, lhsT(1), rhs(1), start=False, stop=True)

            def product_of_parts(dst, ah, al, bh, bl):
                for c in range(DC):
                    pe.matmul(dst, ah(c), bh(c), start=(c == 0), stop=False)
                    pe.matmul(dst, ah(c), bl(c), start=False, stop=False)
                    mm = pe.matmul(dst, al(c), bh(c), start=False, stop=(c == DC - 1))
                return mm

            def tile_of(i):
                return slice(i * P, (i + 1) * P)

            def half_of(h):
                return slice(h * HB, (h + 1) * HB)

            def body(b, first, last):
                pe.wait_ge(out_added, NG * b + NG - 1)
                for n in range(NG):
                    if first:
                        pe.wait_ge(xl_ready, 2 * (n + 1))
                    elif n % 2 == 0:
                        pe.wait_ge(xl_ready, 2 * units(b)[n // 2][2])
                    if n == 1:
                        pe.wait_ge(out_added, NG * b + NG)
                    if n >= 2:
                        pe.wait_ge(qkv_out, NG * b + n - 1)
                    for j in range(2):
                        i = 2 * n + j
                        if first and i in (1, 3, 5):
                            turn(0, (i + 1) // 2)
                        ah, al = (lambda c: xh[:, c, tile_of(i)]), (lambda c: xl[:, c, tile_of(i)])
                        product_of_parts(ps[:, (4 + 3 * n + j) % 8, :], ah, al,
                                         lambda c: wqkvh[:, c, 0:2 * D], lambda c: wqkvl[:, c, 0:2 * D])
                        mm = product_of_parts(ps[:, (6 + 3 * n) % 8, j * D:(j + 1) * D], ah, al,
                                              lambda c: wqkvh[:, c, 2 * D:3 * D], lambda c: wqkvl[:, c, 2 * D:3 * D])
                    mm.then_inc(qkv_mm, 1)
                pe.wait_ge(k_mixed, b + 1)
                pe.wait_ge(qkv_out, NG * b + 2)
                for n in range(4):
                    m, h = n // 2, n % 2
                    if n == 2:
                        pe.wait_ge(qkv_out, NG * b + 3)
                    product(ps[:, n, :], lambda c: wT[:, 1, c, tile_of(m)], lambda c: xkT[:, c, half_of(h)]
                            ).then_inc(k_mm, 1)
                pe.wait_ge(r_mixed, b + 1)
                pe.wait_ge(qkv_out, NG * b + 4)
                for n in range(NG):
                    for j in range(2):
                        mm = product(ps[:, 4 + n, j * D:(j + 1) * D], lambda c: xrT[:, c, tile_of(2 * n + j)],
                                     lambda c: wT[:, 0, c, :])
                    mm.then_inc(r_mm, 1)
                for n in range(4):
                    h, c = n // 2, n % 2
                    if c == 0:
                        pe.wait_ge(feat_done, NG * b + 2 * (h + 1))
                        pe.wait_ge(k_out, 4 * b + 2 * (h + 1))
                    for i in range(4):
                        mm = pe.transpose(ps[:, n, tile_of(i)], feat[:, 4 * h + i, tile_of(c)], s.ident[:, :])
                    mm.then_inc(qT_mm, 1)
                pe.wait_ge(gate_ready, NG * b + 2)
                for c in range(DC):
                    for i in range(BT):
                        mm = pe.matmul(ps[:, 4 + c, 0:P + 1], feat[:, i, D + c * P:D + (c + 1) * P], v1[:, i, c, :],
                                       start=(i == 0), stop=(i == BT - 1))
                mm.then_inc(kv_mm, 1)
                def mix_values(pairs):
                    for n in pairs:
                        if n == 2:
                            pe.wait_ge(qT_ready, 4 * b + 2)
                        for j in range(2):
                            mm = product(ps[:, (6 + n) % 8, j * D:(j + 1) * D],
                                         lambda c: act_k[:, c, tile_of(2 * n + j)], lambda c: wT[:, 2, c, :])
                        mm.then_inc(v_mm, 1)

                def quotients(pairs):
                    for n in pairs:
                        if n >= 2:
                            pe.wait_ge(gated, NG * b + 2 * (n - 1))
                        for i in (2 * n, 2 * n + 1):
                            for c in range(DC):
                                mm = pe.matmul(ps[:, (2 + i) % 8, c * (P + HP):(c + 1) * (P + HP)],
                                               qT[:, c, tile_of(i)], kv[:, c, :], start=True, stop=True)
                        mm.then_inc(nd_mm, 1)

                def turn_attention(h):
                    pe.wait_ge(att_ready, NG * b + 2 * (h + 1))
                    if h:
                        pe.wait_ge(oT_ready, 4 * b + 2)
                    for c in range(DC):
                        for i in range(4):
                            mm = pe.transpose(ps[:, 2 + c, tile_of(i)], att[:, 4 * h + i, tile_of(c)], s.ident[:, :])
                        mm.then_inc(att_turned, 1)

                def project_out(h):
                    pe.wait_ge(oT_ready, 4 * b + 2 * (h + 1))
                    for n in (2 * h, 2 * h + 1):
                        for j in range(2):
                            mm = product(ps[:, 4 + n, j * D:(j + 1) * D], lambda c: oT[:, c, tile_of(2 * n + j)],
                                         lambda c: wout[:, c, :])
                        mm.then_inc(out_mm, 1)

                pe.wait_ge(squared, 4 * b + 4)
                pe.wait_ge(gate_ready, NG * b + NG)
                mix_values(range(3))
                pe.wait_ge(qT_ready, 4 * b + 4)
                pe.wait_ge(kv_ready, b + 1)
                quotients([0, 1])
                mix_values([3])
                quotients([2])
                turn_attention(0)
                quotients([3])
                project_out(0)
                turn_attention(1)
                if not last:
                    turn(b + 1, 0)
                project_out(1)
                if not last:
                    turn(b + 1, 1)

            turn(0, 0)
            pe.wait_ge(loaded, 16 * LOADS)
            sequences(pe, body)

        @block.scalar
        def _(act):
            act.wait_ge(s.later_loaded, 16 * 4)
            act.activation(wqkvh[:, :, :], s.wqkv, ACT.Copy).then_inc(wh_ready, 1)
            act.wait_ge(weights_turned, 1)
            act.activation(wT[:, :, :, :].rearrange("p n c d -> p n (c d)"), ps[:, 4:7, :], ACT.Copy
                           ).then_inc(weights_ready, 1)
            act.activation(unused[:, :], s.eps[:, 0:1], ACT.Sqrt)

            def normed(b, u):
                i, size, count = units(b)[u]
                act.wait_ge(mv_done, count)
                at = slice(i, i + size)
                act.activation(std[:, at], mv[:, at, 1], ACT.Sqrt, bias=s.eps[:, 0:1]).then_inc(std_done, 1)
                act.wait_ge(shift_done, count)
                for k in range(i, i + size):
                    op = act.activation(xn[:, k, :], x_tile(b * BT + k), ACT.Identity, bias=shift[:, k:k + 1],
                                        scale=rstd[:, k:k + 1])
                op.then_inc(xn_ready, 1)

            def turned_out(b, u):
                for c, bank, cols, tokens, count in turns(b, u):
                    act.wait_ge(turned, count)
                    at = slice(1 + tokens.start, 1 + tokens.stop)
                    act.activation(xnT[:, c, at], ps[:, bank, cols], ACT.Copy).then_inc(xnT_ready, 1)
                    act.wait_ge(xnT_ready, count)
                    act.activation(xh[:, c, tokens], xnT[:, c, at], ACT.Copy).then_inc(xh_ready, 1)

            act.wait_ge(const_ready, 3)
            for u in range(2):
                normed(0, u)
                turned_out(0, u)
            normed(0, 2)

            def body(b, first, last):
                def features(n):
                    two = feat[:, 2 * n:2 * n + 2, :]
                    act.wait_ge(summed, NG * b + n + 1 + 2)
                    act.activation(two, straight[:, n % 2], ACT.Relu, scale=-1.0).then_inc(clipped, 1)
                    act.wait_ge(clipped, NG * b + n + 1)
                    act.activation(two, two, ACT.Exp, scale=-1.0).then_inc(exp_done, 1)

                for n in range(NG):
                    act.wait_ge(qkv_mm, NG * b + n + 1)
                    act.wait_ge(summed, NG * b + n + 1)
                    for j in range(2):
                        bank = ps[:, (4 + 3 * n + j) % 8, :]
                        act.activation(qk[:, n % 2, j, 0:D], bank[:, 0:D], ACT.Copy, scale=HD ** -0.5)
                        act.activation(qk[:, n % 2, j, D:2 * D], bank[:, D:2 * D], ACT.Copy)
                    act.activation(v1[:, 2 * n:2 * n + 2, :, 0:P],
                                   ps[:, (6 + 3 * n) % 8, :].rearrange("p (j c f) -> p j c f", j=2, c=DC), ACT.Copy
                                   ).then_inc(qkv_out, 1)
                    if first and n == 0:
                        turned_out(0, 2)
                        normed(0, 3)
                    if first and n == 1:
                        turned_out(0, 3)
                    if n > 0:
                        features(n - 1)
                def relu(n):
                    act.wait_ge(k_mm, 4 * b + n + 1)
                    m, h = n // 2, n % 2
                    at = act_k[:, m, h * HB:(h + 1) * HB]
                    act.activation(at, ps[:, n, :], ACT.Relu).then_inc(k_out, 1)

                def square(n):
                    act.wait_ge(k_out, 4 * b + n + 1)
                    m, h = n // 2, n % 2
                    at = act_k[:, m, h * HB:(h + 1) * HB]
                    act.activation(at, at, ACT.Square).then_inc(squared, 1)

                act.wait_ge(r_mixed, b + 1)
                relu(0)
                features(NG - 1)
                for n in range(1, 4):
                    relu(n)
                for n in range(4):
                    square(n)
                act.wait_ge(rotated, NG * b + NG)
                for n in range(NG):
                    act.wait_ge(r_mm, NG * b + n + 1)
                    act.activation(gate[:, 2 * n:2 * n + 2, :], pair_of_tiles(ps[:, 4 + n, :]), ACT.Sigmoid
                                   ).then_inc(gate_ready, 1)
                for n in range(4):
                    act.wait_ge(qT_mm, 4 * b + n + 1)
                    h, c = n // 2, n % 2
                    act.activation(qT[:, c, h * HB:(h + 1) * HB], ps[:, n, :], ACT.Copy).then_inc(qT_ready, 1)
                if not last:
                    normed(b + 1, 0)
                    normed(b + 1, 1)
                for m in range(4):
                    h, c = m // 2, m % 2
                    act.wait_ge(att_turned, 4 * b + m + 1)
                    act.activation(oT[:, c, h * HB:(h + 1) * HB], ps[:, 2 + c, :], ACT.Copy).then_inc(oT_ready, 1)
                if not last:
                    act.wait_ge(r_mixed, b + 1)
                    turned_out(b + 1, 0)
                    turned_out(b + 1, 1)

            sequences(act, body)

        @block.vector
        def _(dve):
            V = nc.vector
            dve.sem_inc(summed, 2)
            dve.sem_inc(out_added, NG)

            def turned_lo(b, u):
                for c, _, _, tokens, count in turns(b, u):
                    dve.wait_ge(xh_ready, count)
                    V.tensor_tensor(xl[:, c, tokens], xnT[:, c, 1 + tokens.start:1 + tokens.stop],
                                    xh[:, c, tokens].bitcast(F32), ALU.subtract).then_inc(xl_ready, 1)

            def combine(b, u):
                start, size, count = units(b)[u]
                for k in range(K):
                    for i in range(start, start + size):
                        t = b * BT + i
                        if k == 0:
                            dve.wait_ge(s.gathered[i], 16 * K * (b + 1))
                        op = V.scalar_tensor_tensor(x_tile(t), s.picked_rows[:, i, k, :],
                                                    s.gates[:, ds(K * t + k, 1)], x_tile(t), ALU.mult, ALU.add)
                    if k == 0:
                        op.then_inc(first_added, 1)
                        dve.wait_ge(first_added, count)
                op.then_inc(combined, 1)
                hold(dve, combined, count, passed)
                for i in range(start, start + size):
                    op = V.bn_stats(stats[:, i, :], x_tile(b * BT + i))
                op.then_inc(stats_done, 1)
                hold(dve, stats_done, count, passed)
                for i in range(start, start + size):
                    op = V.bn_aggr(mv[:, i, :], stats[:, i, :])
                op.then_inc(mv_done, 1)

            def scales(b, u):
                i, size, count = units(b)[u]
                at = slice(i, i + size)
                dve.wait_ge(std_done, count)
                V.reciprocal(rstd[:, at], std[:, at]).then_inc(rstd_done, 1)
                dve.wait_ge(rstd_done, count)
                V.scalar_tensor_tensor(shift[:, at], mv[:, at, 0], -1.0, rstd[:, at], ALU.mult, ALU.mult
                                       ).then_inc(shift_done, 1)

            dve.wait_ge(wh_ready, 1)
            V.tensor_tensor(wqkvl[:, :, :], s.wqkv, wqkvh[:, :, :].bitcast(F32), ALU.subtract).then_inc(wl_ready, 1)
            combine(0, 0)
            scales(0, 0)
            turned_lo(0, 0)
            combine(0, 1)
            scales(0, 1)
            combine(0, 2)
            turned_lo(0, 1)
            scales(0, 2)
            combine(0, 3)
            turned_lo(0, 2)
            scales(0, 3)

            def body(b, first, last):
                def mix(dst, m, done):
                    for c in range(DC):
                        op = V.scalar_tensor_tensor(dst[:, c, :], step_T[:, c, :], mu[:, m, c:c + 1], xnT[:, c, 0:T],
                                                    ALU.mult, ALU.add)
                    op.then_inc(done, 1)

                def turn_by_position(n):
                    dve.wait_ge(qkv_out, NG * b + n + 1)
                    if n >= 2:
                        dve.wait_ge(feat_done, NG * b + n - 1)
                    a = straight[:, n % 2]
                    V.tensor_tensor(a.rearrange("p j (h f) -> p j h f", f=HD),
                                    qk[:, n % 2].rearrange("p j (h f) -> p j h f", f=HD),
                                    cos[:, 2 * n:2 * n + 2, :].unsqueeze(2).to_broadcast([P, 2, 2 * D // HD, HD]),
                                    ALU.mult).then_inc(straight_done, 1)
                    dve.wait_ge(straight_done, NG * b + n + 1)
                    dve.wait_ge(rotated, NG * b + n + 1)
                    V.tensor_tensor(a, a, rot[:, n % 2], ALU.add).then_inc(summed, 1)

                def feature(n):
                    dve.wait_ge(exp_done, NG * b + n + 1)
                    two = feat[:, 2 * n:2 * n + 2, :]
                    V.scalar_tensor_tensor(two, straight[:, n % 2], 0.0, two, ALU.max, ALU.add).then_inc(feat_done, 1)

                if not first:
                    dve.wait_ge(step_ready, b + 1)
                    mix(xkT, 1, k_mixed)
                turn_by_position(0)
                if first:
                    turned_lo(0, 3)
                else:
                    mix(xrT, 0, r_mixed)
                for n in range(1, NG):
                    turn_by_position(n)
                    feature(n - 1)
                    if first and n == 1:
                        dve.wait_ge(step_ready, b + 1)
                        mix(xkT, 1, k_mixed)
                        mix(xrT, 0, r_mixed)
                feature(NG - 1)

                def apply_gate(n):
                    dve.wait_ge(v_mm, NG * b + n + 1)
                    at = gate[:, 2 * n:2 * n + 2, :]
                    V.tensor_tensor(at, pair_of_tiles(ps[:, (6 + n) % 8, :]), at, ALU.mult).then_inc(gated, 1)

                def divide(n):
                    dve.wait_ge(nd_mm, NG * b + n + 1)
                    two = slice((2 + 2 * n) % 8, (2 + 2 * n) % 8 + 2)
                    nd = ps[:, two, 0:DC * (P + HP)].rearrange("p j (c f) -> p j c f", c=DC)
                    V.tensor_scalar(den[:, n % 2], nd[:, :, :, P:P + HP], 1e-6, None, ALU.max).then_inc(den_clipped, 1)
                    dve.wait_ge(den_clipped, NG * b + n + 1)
                    V.reciprocal(den[:, n % 2], den[:, n % 2]).then_inc(den_inv, 1)
                    dve.wait_ge(den_inv, NG * b + n + 1)
                    for j in range(2):
                        op = V.tensor_tensor(att[:, 2 * n + j, :].rearrange("p (c h f) -> p c h f", c=DC, f=HD),
                                             nd[:, j, :, 0:P].rearrange("p c (h f) -> p c h f", f=HD),
                                             den[:, n % 2, j].unsqueeze(3).to_broadcast([P, DC, HP, HD]), ALU.mult)
                    op.then_inc(att_ready, 1)

                if not last:
                    combine(b + 1, 0)
                    combine(b + 1, 1)
                dve.wait_ge(kv_mm, b + 1)
                for c in range(DC):
                    V.tensor_tensor(kv[:, c, 0:P], ps[:, 4 + c, 0:P], same_head[:, :], ALU.mult)
                    op = V.tensor_scalar(kv[:, c, P:P + HP], head_of[:, :], ps[:, 4 + c, P:P + 1], None, ALU.mult)
                op.then_inc(kv_ready, 1)
                if not last:
                    scales(b + 1, 0)
                apply_gate(0)
                apply_gate(1)
                if not last:
                    scales(b + 1, 1)
                divide(0)
                divide(1)
                apply_gate(2)
                apply_gate(3)
                divide(2)
                divide(3)
                for n in range(NG):
                    if n == NG - 1 and not last:
                        turned_lo(b + 1, 0)
                    dve.wait_ge(out_mm, NG * b + n + 1)
                    V.tensor_tensor(x_tile(b * BT + 2 * n, 2), x_tile(b * BT + 2 * n, 2), ps[:, 4 + n, :], ALU.add
                                    ).then_inc(out_added, 1)
                if not last:
                    turned_lo(b + 1, 1)

            dve.wait_ge(loaded, 16 * LOADS)
            dve.wait_ge(const_ready, 6)
            sequences(dve, body)


def build(nc, t, out):
    s = Shapes(t["L0_attn_x"], t["L0_ffn_W1"])
    xn_rows = nc.dram_tensor("xn_rows", [s.N, s.D], F32, kind="Internal").ap()
    dispatched = nc.dram_tensor("dispatched", [s.MT * s.M, s.D], F32, kind="Internal").ap()
    expert_out = nc.dram_tensor("expert_out", [s.MT * s.M, s.D], F32, kind="Internal").ap()
    with ExitStack() as ctx:
        s.ctx = ctx
        constants(nc, s)
        norm_route_attend(nc, s, t["L0_attn_x"], t["L0_attn_Wq"], t["L0_attn_Wk"], t["L0_attn_Wv"],
                          t["L0_ffn_Wr"], t["L0_ffn_br"], t["L0_ffn_b1"], t["L0_ffn_W1"], t["L0_ffn_W2"],
                          xn_rows, dispatched)
        experts(nc, s, t["L0_ffn_W1"], t["L0_ffn_W2"], t["L0_ffn_b2"], t["L1_attn_W_qkv"], t["L1_ffn_W_r"],
                t["L1_ffn_W_k"], t["L1_ffn_W_v"], dispatched, expert_out)
        combine_and_layer1(nc, s, expert_out, t["L1_attn_W_out"], t["L1_ffn_mu_r"], t["L1_ffn_mu_k"],
                           t["rope_cos"], t["rope_sin"], out)


_INS = ["L0_attn_x", "L0_attn_Wq", "L0_attn_Wk", "L0_attn_Wv", "L0_ffn_Wr", "L0_ffn_br", "L0_ffn_W1", "L0_ffn_b1",
        "L0_ffn_W2", "L0_ffn_b2", "L1_attn_W_qkv", "L1_attn_W_out", "L1_ffn_W_r", "L1_ffn_W_k", "L1_ffn_W_v",
        "L1_ffn_mu_r", "L1_ffn_mu_k"]
_HEADS, _ROPE_BASE = 16, 500000.0


def _rope_tables(T, D):
    import numpy as _np

    hd = D // _HEADS
    inv = (_np.float32(1.0) / _np.float32(_ROPE_BASE) ** (_np.arange(0, hd, 2, dtype=_np.float32) / _np.float32(hd)))
    freqs = (_np.arange(T, dtype=_np.float32)[:, None] * inv.astype(_np.float32)[None, :]).astype(_np.float32)
    cos, sin = _np.cos(freqs), _np.sin(freqs)
    return (_np.concatenate([cos, cos], axis=1).astype(_np.float32),
            _np.concatenate([-sin, sin], axis=1).astype(_np.float32))


def kernel(**inputs):
    import numpy as _np
    import concourse.bacc as _bacc
    from concourse.bass_utils import run_bass_kernel_spmd as _run

    nc = _bacc.Bacc("TRN2", target_bir_lowering=False, num_devices=1)
    _, T, D = inputs["L0_attn_x"].shape
    cos, sin = _rope_tables(T, D)
    arrays, args = {}, {}
    for name, a in [(n, inputs[n]) for n in _INS] + [("rope_cos", cos), ("rope_sin", sin)]:
        a = _np.ascontiguousarray(a)
        arrays[f"in_{name}"] = a
        args[name] = nc.dram_tensor(f"in_{name}", a.shape, mybir.dt.from_np(a.dtype), kind="ExternalInput").ap()
    out = nc.dram_tensor("out", inputs["L0_attn_x"].shape, F32, kind="ExternalOutput").ap()
    build(nc, args, out)
    r = _run(nc, [arrays], core_ids=[0])
    return r.results[0]["out"]
```
